# Optimizing a Trainium2 kernel written in Bass

```python
import numpy as np
import jax
import jax.numpy as jnp

def _softmax(x, axis=-1):
    return jax.nn.softmax(x, axis=axis)

def _gelu(x):
    return jax.nn.gelu(x, approximate=True)

def _silu(x):
    return jax.nn.silu(x)

def _sigmoid(x):
    return jax.nn.sigmoid(x)

def _layernorm(x, axis=-1, eps=1e-05):
    m = jnp.mean(x, axis=axis, keepdims=True)
    v = jnp.var(x, axis=axis, keepdims=True)
    return (x - m) / jnp.sqrt(v + eps)

def _scatter_add(tgt, idx, src, axis=0):
    return tgt.at[idx].add(src)

def _segment_sum(src, seg, n):
    return jax.ops.segment_sum(src, seg, n)
kernel_name = 'mk_hybrid_d1_jaxref_r4_d22c1f'

def setup_inputs(seed: int=0):
    np.random.seed(seed)
    _w = jnp.asarray

    def _L0_attn_a_setup():
        import jax, jax.numpy as jnp
        import numpy as np
        B, S, D = (4, 512, 256)
        H = 16
        HD = D // H
        key = jax.random.key(seed)
        ks = jax.random.split(key, 6)
        scale = 0.02
        return {'x': jax.random.normal(ks[0], (B, S, D), dtype=jnp.float32), 'W_q': jax.random.normal(ks[1], (D, D), dtype=jnp.float32) * scale, 'W_k': jax.random.normal(ks[2], (D, D), dtype=jnp.float32) * scale, 'W_v': jax.random.normal(ks[3], (D, D), dtype=jnp.float32) * scale, 'W_o': jax.random.normal(ks[4], (D, D), dtype=jnp.float32) * scale, 'b_o': jax.random.normal(ks[5], (D,), dtype=jnp.float32) * scale}
    _L0_attn_a_in = _L0_attn_a_setup()

    def _L0_attn_b_setup():
        import jax, jax.numpy as jnp
        import numpy as np
        from jax import lax
        B, S, H = (8, 1024, 256)
        key = jax.random.key(seed)
        ks = jax.random.split(key, 9)
        x = jax.random.normal(ks[0], (B, S, H), dtype=jnp.float32)
        time_decay = jax.random.normal(ks[1], (H,), dtype=jnp.float32) * 0.01
        time_mix_k = jnp.ones((H,), dtype=jnp.float32) * 0.5
        time_mix_v = jnp.ones((H,), dtype=jnp.float32) * 0.5
        time_mix_r = jnp.ones((H,), dtype=jnp.float32) * 0.5
        sc = 1.0 / np.sqrt(H)
        Wk = jax.random.uniform(ks[2], (H, H), jnp.float32, -sc, sc)
        Wv = jax.random.uniform(ks[3], (H, H), jnp.float32, -sc, sc)
        Wr = jax.random.uniform(ks[4], (H, H), jnp.float32, -sc, sc)
        Wo = jax.random.uniform(ks[5], (H, H), jnp.float32, -sc, sc)
        return {'x': x, 'time_decay': time_decay, 'time_mix_k': time_mix_k, 'time_mix_v': time_mix_v, 'time_mix_r': time_mix_r, 'Wk': Wk, 'Wv': Wv, 'Wr': Wr, 'Wo': Wo}
    _L0_attn_b_in = _L0_attn_b_setup()

    def _L0_ffn_setup():
        import jax, jax.numpy as jnp
        import numpy as np
        D_MODEL = 256
        EXPANSION = 4
        D_HIDDEN = D_MODEL * EXPANSION
        NUM_STAGES = int(np.log2(D_HIDDEN))

        def butterfly(y, weights, dim):
            lead = y.shape[:-1]
            for stage in range(weights.shape[0]):
                s = 2 ** stage
                nb = dim // (2 * s)
                yr = y.reshape(*lead, nb, 2, s)
                a = yr[..., 0, :]
                b = yr[..., 1, :]
                w = weights[stage].reshape(nb, s, 2, 2)
                na = w[..., 0, 0] * a + w[..., 0, 1] * b
                nb2 = w[..., 1, 0] * a + w[..., 1, 1] * b
                y = jnp.stack([na, nb2], axis=-2).reshape(*lead, dim)
            return y
        key = jax.random.key(seed)
        ks = jax.random.split(key, 6)
        B, S = (4, 512)
        x = jax.random.normal(ks[0], (B, S, D_MODEL), jnp.float32)
        W_exp = jax.random.normal(ks[1], (D_MODEL, D_HIDDEN), jnp.float32) * 0.02
        b_exp = jnp.zeros((D_HIDDEN,), jnp.float32)
        up_weights = jax.random.normal(ks[2], (NUM_STAGES, D_HIDDEN // 2, 2, 2), jnp.float32) * 0.02
        up_bias = jnp.zeros((D_HIDDEN,), jnp.float32)
        down_weights = jax.random.normal(ks[3], (NUM_STAGES, D_HIDDEN // 2, 2, 2), jnp.float32) * 0.02
        W_con = jax.random.normal(ks[4], (D_HIDDEN, D_MODEL), jnp.float32) * 0.02
        b_con = jnp.zeros((D_MODEL,), jnp.float32)
        down_bias = jnp.zeros((D_MODEL,), jnp.float32)
        return dict(x=x, W_exp=W_exp, b_exp=b_exp, up_weights=up_weights, up_bias=up_bias, down_weights=down_weights, W_con=W_con, b_con=b_con, down_bias=down_bias)
    _L0_ffn_in = _L0_ffn_setup()
    _d = {'L0_attn_a_x': _L0_attn_a_in['x'], 'L0_attn_a_W_q': _L0_attn_a_in['W_q'], 'L0_attn_a_W_k': _L0_attn_a_in['W_k'], 'L0_attn_a_W_v': _L0_attn_a_in['W_v'], 'L0_attn_a_W_o': _L0_attn_a_in['W_o'], 'L0_attn_a_b_o': _L0_attn_a_in['b_o'], 'L0_attn_b_time_decay': _L0_attn_b_in['time_decay'], 'L0_attn_b_time_mix_k': _L0_attn_b_in['time_mix_k'], 'L0_attn_b_time_mix_v': _L0_attn_b_in['time_mix_v'], 'L0_attn_b_time_mix_r': _L0_attn_b_in['time_mix_r'], 'L0_attn_b_Wk': _L0_attn_b_in['Wk'], 'L0_attn_b_Wv': _L0_attn_b_in['Wv'], 'L0_attn_b_Wr': _L0_attn_b_in['Wr'], 'L0_attn_b_Wo': _L0_attn_b_in['Wo'], 'L0_ffn_W_exp': _L0_ffn_in['W_exp'], 'L0_ffn_b_exp': _L0_ffn_in['b_exp'], 'L0_ffn_up_weights': _L0_ffn_in['up_weights'], 'L0_ffn_up_bias': _L0_ffn_in['up_bias'], 'L0_ffn_down_weights': _L0_ffn_in['down_weights'], 'L0_ffn_W_con': _L0_ffn_in['W_con'], 'L0_ffn_b_con': _L0_ffn_in['b_con'], 'L0_ffn_down_bias': _L0_ffn_in['down_bias']}
    _x0 = _d['L0_attn_a_x']
    _d['L0_attn_a_x'] = jax.random.normal(jax.random.fold_in(jax.random.key(seed), 1), (4, 2048, 256), dtype=_x0.dtype)
    del _x0
    return _d

def reference(L0_attn_a_x, L0_attn_a_W_q, L0_attn_a_W_k, L0_attn_a_W_v, L0_attn_a_W_o, L0_attn_a_b_o, L0_attn_b_time_decay, L0_attn_b_time_mix_k, L0_attn_b_time_mix_v, L0_attn_b_time_mix_r, L0_attn_b_Wk, L0_attn_b_Wv, L0_attn_b_Wr, L0_attn_b_Wo, L0_ffn_W_exp, L0_ffn_b_exp, L0_ffn_up_weights, L0_ffn_up_bias, L0_ffn_down_weights, L0_ffn_W_con, L0_ffn_b_con, L0_ffn_down_bias):

    def _L0_attn_a_ref(x, W_q, W_k, W_v, W_o, b_o):
        import jax, jax.numpy as jnp
        import numpy as np
        B, S, D = (4, 512, 256)
        H = 16
        HD = D // H
        b, s, d = x.shape
        q = (x @ W_q).reshape(b, s, H, HD).transpose(0, 2, 1, 3)
        k = (x @ W_k).reshape(b, s, H, HD).transpose(0, 2, 1, 3)
        v = (x @ W_v).reshape(b, s, H, HD).transpose(0, 2, 1, 3)
        scores = jnp.einsum('bhqd,bhkd->bhqk', q, k)
        causal = jnp.triu(jnp.ones((s, s), dtype=bool), k=1)
        scores = jnp.where(causal, -jnp.inf, scores)
        attn = jax.nn.softmax(scores / jnp.sqrt(jnp.float32(HD)), axis=-1)
        ctx = jnp.einsum('bhqk,bhkd->bhqd', attn, v)
        ctx = ctx.transpose(0, 2, 1, 3).reshape(b, s, d)
        return ctx @ W_o + b_o

    def _L0_attn_b_ref(x, time_decay, time_mix_k, time_mix_v, time_mix_r, Wk, Wv, Wr, Wo):
        import jax, jax.numpy as jnp
        import numpy as np
        from jax import lax
        B, S, H = (8, 1024, 256)
        d = jnp.exp(-jnp.exp(time_decay))
        b, s, h = x.shape

        def step(state, xt):
            new_state = xt + state * d
            return (new_state, state)
        init = jnp.zeros((b, h), dtype=x.dtype)
        _, prev = lax.scan(step, init, jnp.swapaxes(x, 0, 1))
        prev = jnp.swapaxes(prev, 0, 1)
        k_in = x * time_mix_k + prev * (1.0 - time_mix_k)
        v_in = x * time_mix_v + prev * (1.0 - time_mix_v)
        r_in = x * time_mix_r + prev * (1.0 - time_mix_r)
        _k = jnp.einsum('bsh,oh->bso', k_in, Wk)
        v = jnp.einsum('bsh,oh->bso', v_in, Wv)
        r = jax.nn.sigmoid(jnp.einsum('bsh,oh->bso', r_in, Wr))
        out = r * jnp.einsum('bsh,oh->bso', v, Wo)
        return out

    def _L0_ffn_ref(x, W_exp, b_exp, up_weights, up_bias, down_weights, W_con, b_con, down_bias):
        import jax, jax.numpy as jnp
        import numpy as np
        D_MODEL = 256
        EXPANSION = 4
        D_HIDDEN = D_MODEL * EXPANSION
        NUM_STAGES = int(np.log2(D_HIDDEN))

        def butterfly(y, weights, dim):
            lead = y.shape[:-1]
            for stage in range(weights.shape[0]):
                s = 2 ** stage
                nb = dim // (2 * s)
                yr = y.reshape(*lead, nb, 2, s)
                a = yr[..., 0, :]
                b = yr[..., 1, :]
                w = weights[stage].reshape(nb, s, 2, 2)
                na = w[..., 0, 0] * a + w[..., 0, 1] * b
                nb2 = w[..., 1, 0] * a + w[..., 1, 1] * b
                y = jnp.stack([na, nb2], axis=-2).reshape(*lead, dim)
            return y
        h = jnp.einsum('bsd,dh->bsh', x, W_exp) + b_exp
        h = butterfly(h, up_weights, D_HIDDEN)
        h = jax.nn.gelu(h + up_bias, approximate=False)
        h = butterfly(h, down_weights, D_HIDDEN)
        y = jnp.einsum('bsh,hd->bsd', h, W_con) + b_con
        return y + down_bias
    x = L0_attn_a_x
    x = x + _L0_attn_a_ref(_layernorm(x, axis=-1), L0_attn_a_W_q, L0_attn_a_W_k, L0_attn_a_W_v, L0_attn_a_W_o, L0_attn_a_b_o)
    x = x + _L0_ffn_ref(_layernorm(x, axis=-1), L0_ffn_W_exp, L0_ffn_b_exp, L0_ffn_up_weights, L0_ffn_up_bias, L0_ffn_down_weights, L0_ffn_W_con, L0_ffn_b_con, L0_ffn_down_bias)
    x = x + _L0_attn_b_ref(_layernorm(x, axis=-1), L0_attn_b_time_decay, L0_attn_b_time_mix_k, L0_attn_b_time_mix_v, L0_attn_b_time_mix_r, L0_attn_b_Wk, L0_attn_b_Wv, L0_attn_b_Wr, L0_attn_b_Wo)
    x = x + _L0_ffn_ref(_layernorm(x, axis=-1), L0_ffn_W_exp, L0_ffn_b_exp, L0_ffn_up_weights, L0_ffn_up_bias, L0_ffn_down_weights, L0_ffn_W_con, L0_ffn_b_con, L0_ffn_down_bias)
    return x

_drawn_inputs = setup_inputs


def setup_inputs(seed=0):
    import zlib

    import numpy as np

    out = dict(_drawn_inputs(seed))
    spreads = {'L0_attn_b_time_mix_k': (0.5, 0.2),
     'L0_attn_b_time_mix_v': (0.5, 0.6),
     'L0_attn_b_time_mix_r': (0.5, 0.6),
     'L0_ffn_b_exp': (0.0, 0.1),
     'L0_ffn_up_bias': (0.0, 0.1),
     'L0_ffn_b_con': (0.0, 0.1),
     'L0_ffn_down_bias': (0.0, 0.1)}
    factors = {'L0_attn_a_W_q': 8.0,
     'L0_attn_a_W_k': 8.0,
     'L0_attn_a_W_v': 8.0,
     'L0_attn_a_W_o': 8.0,
     'L0_attn_a_b_o': 13.055,
     'L0_attn_b_time_decay': 200.0,
     'L0_attn_b_Wr': 6.018}
    for name, (base, spread) in spreads.items():
        noise = np.random.default_rng([zlib.crc32(name.encode()), seed]).standard_normal(out[name].shape)
        drawn = base * np.exp(spread * noise) if base else spread * noise
        out[name] = jnp.asarray(drawn.astype(out[name].dtype))
    for name, factor in factors.items():
        out[name] = (out[name] * factor).astype(out[name].dtype)
    return out
```

```python
from contextlib import ExitStack

import concourse.bass as bass
from concourse import mybir

F32 = mybir.dt.float32
BF16 = mybir.dt.bfloat16
ALU = mybir.AluOpType
ACT = mybir.ActivationFunctionType
AX = mybir.AxisListType

P = 128
BATCH, SEQ, D = 4, 2048, 256
HEADS, HD = 16, 16
HID = 1024
STAGES = 10
CT = D // P
HT = HID // P
BLK = 512
TT = BLK // P
BPS = SEQ // BLK
NBLK = BATCH * BPS
EPS = 1e-5

GH = 4
HG = HEADS // GH
UNITS = BATCH * HG
KB = SEQ // P
GROUPS = SEQ // BLK
SCALE = float(HD) ** -0.5
NEG = -1e30
Q_PART = [0, 0, 1, 1, 0, 2]
K_PART = [0, 1, 0, 1, 2, 0]
PROD = HD * len(Q_PART)
ROWS = PROD + 3


class Steps:

    LEAD = 38
    PBUF = 8

    def __init__(self):
        self.tiles = []
        self.plan = {}
        self.round_of_tile = []
        self.first = {}
        rounds = 0
        masked = 0
        self.masked_before = []
        for g in range(GROUPS):
            self.first[g] = len(self.tiles)
            for r in range(2 * g + 1):
                kind = "full" if r < 2 * g else "diag"
                for h in range(GH):
                    self.tiles.append((kind, g, h, 2 * r))
                    self.round_of_tile.append(rounds + 1)
                    self.masked_before.append(masked)
                    masked += kind == "diag"
                last = len(self.tiles) - 1
                late = 2 + (kind == "diag")
                for half in range(2):
                    self.add("pv", last + late + half, (g, kind, 2 * r, half, last - GH + 1, rounds, masked))
                rounds += 1
            self.tiles.append(("corner", g, 0, 4 * g + 2))
            self.masked_before.append(masked)
            masked += 1
            self.round_of_tile.append(rounds + 1)
            c = len(self.tiles) - 1
            self.add("pv", c + 3, (g, "corner", 4 * g + 2, 0, c, rounds, masked))
            rounds += 1
            self.add("o_copy", c + 4, (g, rounds))
            self.add("ctx_turn", c + 6, (g,))
            self.add("ctx_norm", c + 7, (g,))
            self.add("ctx_store", c + 8, (g,))
        self.n = len(self.tiles)
        self.rounds = rounds
        self.masked = masked
        self.banks = []
        for g in range(GROUPS):
            for h in range(GH):
                for qb in range(TT):
                    for j in range(g):
                        self.banks.append((g, [(h, qb, j * BLK, BLK, False)]))
            for h in range(GH):
                self.banks.append((g, [(h, 3, g * BLK, 4 * P, True)]))
            for h in range(GH):
                self.banks.append((g, [(h, 2, g * BLK, 3 * P, True), (h, 0, g * BLK, P, True)]))
            for h in range(0, GH, 2):
                self.banks.append((g, [(h, 1, g * BLK, 2 * P, True), (h + 1, 1, g * BLK, 2 * P, True)]))
            assert len(self.banks) % 2 == 0
            s = len(self.banks) // 2 - 1 - self.LEAD
            self.add("shift_max", s, (g, len(self.banks)))
            self.add("shift_turn", s + 3, (g,))
            self.add("shift_copy", s + 4, (g,))
            self.add("shift_send", s + 5, (g,))
            assert s + 6 < self.first[g]
        assert len(self.banks) == 2 * self.n and self.n % 4 == 0
        self.add("load", 3 - self.n, ())
        self.add("values", 3 - self.n, ())

    def add(self, kind, step, what):
        self.plan.setdefault(kind, []).append((step, what))

    def due(self, kind, step, u, before=True, after=True):
        for rel in (-1, 0, 1):
            if (rel < 0 and not before) or (rel > 0 and not after):
                continue
            for s, what in self.plan[kind]:
                if s == step - rel * self.n:
                    yield (u + rel, rel) + what

    def banks_due(self, step, u, after=True):
        j = step + self.LEAD
        if j < self.n:
            yield from ((u, 0, 2 * j), (u, 0, 2 * j + 1))
        elif after:
            yield from ((u + 1, 1, 2 * (j - self.n)), (u + 1, 1, 2 * (j - self.n) + 1))


ST = Steps()


def wait(eng, sem, value):
    if isinstance(value, int) and value <= 0:
        return
    eng.wait_ge(sem, value)


def apart(eng):
    eng.nop(nofuse=True)


class Shared:
    pass


def consts_phase(nc, k, w):
    with ExitStack() as ctx:
        sb = lambda n, s, d=F32: ctx.enter_context(nc.sbuf_tensor(n, s, d))
        sem = lambda n: ctx.enter_context(nc.semaphore(n))
        weights_row = sb("butterfly_row", [1, 2, 4 * HID // 2])
        weights = sb("butterfly_weights", [P, 2, 4 * HID // 2])
        up = [sb(f"up_work{i}", [P, CT, HID]) for i in range(2)]
        up_row = [sb(f"up_bias_work{i}", [1, HID]) for i in range(2)]
        down = [sb(f"down_work{i}", [P, CT, HID]) for i in range(2)]
        product = sb("butterfly_product", [P, 3, 4, HID // 2])
        con = sb("w_con_rows", [P, HT, D])
        up_bias = sb("up_bias_row", [1, HID])
        square = sb("square_weights", [P, 3, CT, D])
        wo_t = sb("wo_turned", [P, CT, D])
        rows = sb("bias_rows", [1, 3, D])
        turned = ctx.enter_context(nc.psum_tensor("turned", [P, 4, 512], F32))
        turned2 = ctx.enter_context(nc.psum_tensor("turned2", [P, 4, 512], F32))
        loaded = sem("c_loaded")
        small_loaded = sem("c_small_loaded")
        stage_loaded = [sem(f"c_stage_loaded{i}") for i in range(2)]
        spread = sem("c_spread")
        ident_step = sem("c_ident_step")
        made = sem("c_made")
        pool_step = sem("c_pool_step")
        up_done = sem("c_up_done")
        dve_step = sem("c_dve_step")
        down_stage = sem("c_down_stage")
        con_turned = sem("c_con_turned")
        small_turned = sem("c_small_turned")
        small_copied = sem("c_small_copied")
        composed = sem("c_composed")
        down_turned = sem("c_down_turned")
        bias_turned = sem("c_bias_turned")
        block = ctx.enter_context(nc.Block())
        N_STAGE = 2 * STAGES
        order = list(range(STAGES)) + list(reversed(range(STAGES)))

        @block.sync
        def _(sp):
            sp.dma_start(con[:], w.W_con.rearrange("(t p) n -> p t n", p=P)).then_inc(loaded, 16)
            for i, m in enumerate((w.Wr, w.Wo, w.Wv)):
                sp.dma_start(square[:, i], m.rearrange("(t p) n -> p t n", p=P)).then_inc(loaded, 16)
            sp.dma_start(up[0][:], w.W_exp.rearrange("(t p) n -> p t n", p=P)).then_inc(loaded, 16)
            sp.dma_start(up_row[0][:], w.b_exp.rearrange("(o n) -> o n", o=1)).then_inc(loaded, 16)
            sp.dma_start(up_bias[:], w.up_bias.rearrange("(o n) -> o n", o=1)).then_inc(loaded, 16)
            for i, m in enumerate((w.b_o, w.b_con, w.down_bias)):
                sp.dma_start(rows[:, i], m.rearrange("(o n) -> o n", o=1)).then_inc(loaded, 16)
            sp.dma_start(k.w_o[:], w.W_o.rearrange("(t p) n -> p t n", p=P)).then_inc(small_loaded, 16)
            for i, m in enumerate((w.time_decay, w.time_mix_v, w.time_mix_r)):
                sp.dma_start(k.channel[:, i, :], m.rearrange("(t p) -> p t", p=P),
                             allow_slow_non_contiguous=True).then_inc(small_loaded, 16)
            for n, s in enumerate(order):
                source = w.up_weights if n < STAGES else w.down_weights
                if n >= 2:
                    sp.wait_ge(spread, n - 1)
                sp.dma_start(weights_row[:, n % 2], source[s].rearrange("(o k) r c -> o (k r c)", o=1))\
                    .then_inc(stage_loaded[n % 2], 16)
            sp.wait_ge(small_loaded, 4 * 16)

        def halves(m, s):
            v = m.rearrange("p (b two s) -> p b two s", two=2, s=2 ** s)
            return v[:, :, 0, :], v[:, :, 1, :]

        def weight(n, s, r, c, parts):
            v = weights[0:parts, n % 2, :].rearrange("p (b s rc) -> p b s rc", s=2 ** s, rc=4)
            return v[:, :, :, 2 * r + c]

        def product_view(parts, i, j, s):
            return product[0:parts, i, j, :].rearrange("p (b s) -> p b s", s=2 ** s)

        @block.gpsimd
        def _(pool):
            pool.memset(k.ident[:], 0.0).then_inc(ident_step, 1)
            pool.memset(k.causal[:], 0.0).then_inc(ident_step, 1)
            pool.wait_ge(ident_step, 2)
            pool.affine_select(out=k.ident[:], in_=k.ident[:], compare_op=ALU.not_equal, fill=1.0, base=0,
                               pattern=[[-1, P]], channel_multiplier=1).then_inc(ident_step, 1)
            pool.affine_select(out=k.causal[:], in_=k.causal[:], compare_op=ALU.is_ge, fill=NEG, base=0,
                               pattern=[[-1, P]], channel_multiplier=1).then_inc(ident_step, 1)
            pool.wait_ge(ident_step, 4)
            pool.tensor_copy(k.ident_b[:], k.ident[:]).then_inc(made, 1)
            pool.memset(k.minus_half[:], -0.5).then_inc(made, 1)
            pool.wait_ge(loaded, 10 * 16)
            pool.tensor_tensor(rows[:, 1], rows[:, 1], rows[:, 2], ALU.add).then_inc(pool_step, 1)
            pool.wait_ge(pool_step, 1)
            pool.partition_broadcast(k.row_bias[:, 0, :], rows[:, 0]).then_inc(made, 1)
            pool.partition_broadcast(k.row_bias[:, 1, :], rows[:, 1]).then_inc(made, 1)
            step = 1
            for n, s in enumerate(order):
                pool.wait_ge(stage_loaded[n % 2], 16 * (n // 2 + 1))
                if n >= STAGES + 2:
                    pool.wait_ge(down_stage, n - STAGES - 1)
                pool.partition_broadcast(weights[:, n % 2, :], weights_row[:, n % 2]).then_inc(spread, 1)
                if n >= STAGES:
                    continue
                pool.wait_ge(spread, n + 1)
                src, dst = up[n % 2], up[(n + 1) % 2]
                lanes = [(P, src[:, c, :], dst[:, c, :]) for c in range(CT)]
                lanes.append((1, up_row[n % 2][:], up_row[(n + 1) % 2][:]))
                for i, (parts, a_b, _) in enumerate(lanes):
                    for j, (r, c) in enumerate(((0, 0), (0, 1), (1, 0), (1, 1))):
                        pool.tensor_tensor(product_view(parts, i, j, s), halves(a_b, s)[c],
                                           weight(n, s, r, c, parts), ALU.mult).then_inc(pool_step, 1)
                        step += 1
                pool.wait_ge(pool_step, step)
                for i, (parts, _, out) in enumerate(lanes):
                    for r in range(2):
                        pool.tensor_tensor(halves(out, s)[r], product_view(parts, i, 2 * r, s),
                                           product_view(parts, i, 2 * r + 1, s), ALU.add).then_inc(pool_step, 1)
                        step += 1
                pool.wait_ge(pool_step, step)
                if n == STAGES - 1:
                    pool.tensor_tensor(up_row[0][:], up_row[0][:], up_bias[:], ALU.add).then_inc(up_done, 1)
                    pool.tensor_copy(k.up_matrix[:], up[0][:]).then_inc(made, 1)
            pool.wait_ge(made, 5)

        @block.vector
        def _(dve):
            for c in range(CT):
                dve.wait_ge(con_turned, c + 1)
                if c:
                    dve.wait_ge(dve_step, c)
                dve.tensor_copy(down[0][:, c, :], turned[:, 2 * c:2 * c + 2, :].rearrange("p a n -> p (a n)"))\
                    .then_inc(dve_step, 1)
            dve.wait_ge(small_turned, 1)
            dve.tensor_copy(k.w_r[:], turned2[:, 0, :].rearrange("p (a n) -> p a n", a=CT)).then_inc(small_copied, 1)
            dve.tensor_copy(wo_t[:], turned2[:, 1, :].rearrange("p (a n) -> p a n", a=CT)).then_inc(small_copied, 1)
            dve.wait_ge(composed, 1)
            dve.tensor_copy(k.w_vo[:], turned2[:, 2, :].rearrange("p (a n) -> p a n", a=CT)).then_inc(small_copied, 1)
            step = CT
            for m in range(STAGES):
                n = STAGES + m
                s = order[n]
                dve.wait_ge(spread, n + 1)
                dve.wait_ge(up_done, 1)
                src, dst = down[m % 2], down[(m + 1) % 2]
                dve.wait_ge(dve_step, step)
                for i in range(CT):
                    for j, (r, c) in enumerate(((0, 0), (0, 1), (1, 0), (1, 1))):
                        dve.tensor_tensor(product_view(P, i, j, s), halves(src[:, i, :], s)[c],
                                          weight(n, s, c, r, P), ALU.mult).then_inc(dve_step, 1)
                        step += 1
                dve.wait_ge(dve_step, step)
                for i in range(CT):
                    for r in range(2):
                        ins = dve.tensor_tensor(halves(dst[:, i, :], s)[r], product_view(P, i, 2 * r, s),
                                                product_view(P, i, 2 * r + 1, s), ALU.add)
                        if (i, r) == (CT - 1, 1):
                            ins.then_inc(down_stage, 1)
                        else:
                            ins.then_inc(dve_step, 1)
                            step += 1
                dve.wait_ge(down_stage, m + 1)
            dve.wait_ge(dve_step, step)
            dve.wait_ge(bias_turned, 1)
            dve.tensor_copy(k.hidden_bias[:], turned2[:, 3, 0:HT]).then_inc(small_copied, 1)
            for half in range(2):
                dve.wait_ge(down_turned, half + 1)
                dve.tensor_copy(k.down_matrix[:, 4 * half:4 * half + 4, :],
                                turned[:, 2 * half:2 * half + 2, :].rearrange("p a (t n) -> p (a t) n", n=D))\
                    .then_inc(dve_step, 1)
            dve.wait_ge(dve_step, step + 2)

        @block.scalar
        def _(act):
            act.wait_ge(small_loaded, 4 * 16)
            act.activation(k.channel[:, 3, :], k.channel[:, 0, :], ACT.Exp).then_inc(k.setup_done, 1)
            act.wait_ge(k.setup_done, 1)
            act.activation(k.channel[:, 4, :], k.channel[:, 3, :], ACT.Exp, scale=-1.0).then_inc(k.setup_done, 1)
            act.wait_ge(k.setup_done, 2)

        @block.tensor
        def _(pe):
            pe.wait_ge(ident_step, 4)
            pe.wait_ge(loaded, 10 * 16)
            for c in range(CT):
                for t in range(HT):
                    ins = pe.transpose(turned[:, 2 * c + t // 4, (t % 4) * P:(t % 4 + 1) * P],
                                       con[:, t, c * P:(c + 1) * P], k.ident[:])
                ins.then_inc(con_turned, 1)
            for i in range(2):
                for a in range(CT):
                    for b in range(CT):
                        ins = pe.transpose(turned2[:, i, b * D + a * P:b * D + (a + 1) * P],
                                           square[:, i, a, b * P:(b + 1) * P], k.ident[:])
            ins.then_inc(small_turned, 1)
            pe.wait_ge(small_copied, 2)
            for h in range(CT):
                for m in range(CT):
                    ins = pe.matmul(turned2[:, 2, h * D:(h + 1) * D], square[:, 2, m, h * P:(h + 1) * P],
                                    wo_t[:, m, :], start=(m == 0), stop=(m == CT - 1))
            ins.then_inc(composed, 1)
            pe.wait_ge(up_done, 1)
            for t in range(HT):
                ins = pe.matmul(turned2[:, 3, t:t + 1], up_row[0][:, t * P:(t + 1) * P], k.ident[0:1, 0:1],
                                start=True, stop=True)
            ins.then_inc(bias_turned, 1)
            pe.wait_ge(down_stage, STAGES)
            pe.wait_ge(dve_step, CT + STAGES * (4 * CT + 2 * CT - 1))
            for t in range(HT):
                for c in range(CT):
                    ins = pe.transpose(turned[:, t // 2, (t % 2) * D + c * P:(t % 2) * D + (c + 1) * P],
                                       down[0][:, c, t * P:(t + 1) * P], k.ident[:])
                if t % 4 == 3:
                    ins.then_inc(down_turned, 1)


def project_phase(nc, k, w):
    with ExitStack() as ctx:
        sb = lambda n, s, d=F32: ctx.enter_context(nc.sbuf_tensor(n, s, d))
        sem = lambda n: ctx.enter_context(nc.semaphore(n))
        w_qk = sb("w_qk", [P, CT, 2 * D])
        w_v = sb("w_v", [P, CT, D])
        w_loaded = sem("a_w_loaded")
        x_in = sb("a_x", [P, 2, TT, D])
        stats = sb("a_stats", [P, 2, TT, 6])
        mean_var = sb("a_mean_var", [P, 2, TT, 2])
        var_eps = sb("a_var_eps", [P, 2, TT])
        rstd = sb("a_rstd", [P, 2, TT])
        xn = sb("a_xn", [P, 2, TT, D])
        xt = sb("a_xt", [P, 2, CT, BLK])
        part = sb("a_parts", [P, 2, 3, 2 * CT, BLK], BF16)
        rest = sb("a_rest", [P, 2, 2 * CT, BLK])
        p_turn = ctx.enter_context(nc.psum_tensor("a_turn", [P, CT, BLK], F32))
        p_qk = ctx.enter_context(nc.psum_tensor("a_qk", [P, 2 * CT, BLK], F32))
        p_v = ctx.enter_context(nc.psum_tensor("a_v", [P, TT, D], F32))
        x_loaded = [sem(f"a_x_loaded{i}") for i in range(2)]
        stat_step = sem("a_stat_step")
        stats_done = sem("a_stats_done")
        eps_added = sem("a_eps_added")
        rstd_done = sem("a_rstd_done")
        xn_done = sem("a_xn_done")
        turned = sem("a_turned")
        xt_done = sem("a_xt_done")
        qk_done = sem("a_qk_done")
        v_done = sem("a_v_done")
        part1 = sem("a_part1")
        rest_done = sem("a_rest_done")
        part2 = sem("a_part2")
        part3 = sem("a_part3")
        v_copied = sem("a_v_copied")
        stored = [sem(f"a_stored{i}") for i in range(2)]
        block = ctx.enter_context(nc.Block())
        x_tiles = w.x.rearrange("b (n j p) c -> (b n) p j c", n=BPS, p=P)

        def sequences(eng, body):
            for j in range(BPS):
                body(0, j)
            with eng.Fori(1, BATCH - 1) as b:
                for j in range(BPS):
                    body(b, j)
            for j in range(BPS):
                body(BATCH - 1, j)

        def is_last(b, j):
            return isinstance(b, int) and (b, j) == (BATCH - 1, BPS - 1)

        @block.sync
        def _(sp):
            for i, m in enumerate((w.W_q, w.W_k)):
                sp.dma_start(w_qk[:, :, i * D:(i + 1) * D], m.rearrange("(t p) n -> p t n", p=P))\
                    .then_inc(w_loaded, 16)
            sp.dma_start(w_v[:], w.W_v.rearrange("(t p) n -> p t n", p=P)).then_inc(w_loaded, 16)

            def store(b, j):
                t = b * BPS + j
                z = j % 2
                wait(sp, part1, 4 * t + 4)
                apart(sp)
                wait(sp, part2, 4 * t + 4)
                apart(sp)
                wait(sp, part3, 4 * t + 4)
                apart(sp)
                for i in range(3):
                    for m in range(2 * CT):
                        dst = k.q_parts if m < CT else k.k_parts
                        for hh in range(2):
                            sp.dma_start(
                                dst[b * HG + (m % CT) * 2 + hh, i, :, j * BLK:(j + 1) * BLK],
                                part[64 * hh:64 * hh + 64, z, i, m, :]).then_inc(stored[z], 16)

            def load(b, j):
                t = b * BPS + j
                wait(sp, xn_done, TT * (t - 1))
                apart(sp)
                sp.dma_start(x_in[:, j % 2], x_tiles[t]).then_inc(x_loaded[j % 2], 16)

            def body(b, j):
                load(b, j)
                if not (isinstance(b, int) and (b, j) == (0, 0)):
                    if j:
                        store(b, j - 1)
                    else:
                        store(b - 1, BPS - 1)
            sequences(sp, body)
            store(BATCH - 1, BPS - 1)
            for z in range(2):
                sp.wait_ge(stored[z], 16 * 24 * NBLK // 2)

        @block.gpsimd
        def _(pool):
            def body(b, j):
                t = b * BPS + j
                z = j % 2
                wait(pool, stats_done, TT * (t + 1))
                apart(pool)
                pool.tensor_scalar(var_eps[:, z], mean_var[:, z, :, 1], EPS, None, ALU.add).then_inc(eps_added, 1)
                wait(pool, eps_added, t + 1)
                pool.tensor_tensor(rstd[:, z], var_eps[:, z], k.minus_half[:], ALU.pow).then_inc(rstd_done, 1)
                if not (isinstance(b, int) and (b, j) == (0, 0)):
                    split(b, j - 1) if j else split(b - 1, BPS - 1)

            def split(b, j):
                t = b * BPS + j
                z = j % 2
                for m in range(2 * CT):
                    wait(pool, part2, 4 * t + m + 1)
                    pool.tensor_tensor(part[:, z, 2, m], rest[:, z, m], part[:, z, 1, m], ALU.subtract)\
                        .then_inc(part3, 1)
            sequences(pool, body)
            split(BATCH - 1, BPS - 1)

        @block.vector
        def _(dve):
            def norm(b, j):
                t = b * BPS + j
                z = j % 2
                wait(dve, x_loaded[z], 16 * (b * (BPS // 2) + j // 2 + 1))
                for a in range(TT):
                    dve.bn_stats(stats[:, z, a], x_in[:, z, a]).then_inc(stat_step, 1)
                wait(dve, stat_step, TT * (t + 1))
                wait(dve, rstd_done, t - 1)
                apart(dve)
                for a in range(TT):
                    dve.bn_aggr(mean_var[:, z, a], stats[:, z, a]).then_inc(stats_done, 1)
                wait(dve, stats_done, TT * (t + 1))
                wait(dve, rstd_done, t + 1)
                wait(dve, turned, t - 1)
                for a in range(TT):
                    dve.tensor_scalar(xn[:, z, a], x_in[:, z, a], mean_var[:, z, a, 0:1], rstd[:, z, a:a + 1],
                                      ALU.subtract, ALU.mult).then_inc(xn_done, 1)

            def split(b, j):
                t = b * BPS + j
                z = j % 2
                for m in range(2 * CT):
                    wait(dve, part1, 4 * t + m + 1)
                    wait(dve, part3, 4 * (t - 2) + m + 1) if not (isinstance(t, int) and t < 2) else None
                    dve.tensor_tensor(rest[:, z, m], p_qk[:, m], part[:, z, 0, m], ALU.subtract)\
                        .then_inc(rest_done, 1)
                for m in range(2 * CT):
                    wait(dve, rest_done, 4 * t + m + 1)
                    if m == 0 and not (isinstance(t, int) and t < 2):
                        wait(dve, stored[z], 16 * 24 * (b * (BPS // 2) + j // 2))
                    dve.tensor_copy(part[:, z, 1, m], rest[:, z, m]).then_inc(part2, 1)
            norm(0, 0)

            def body(b, j):
                if not is_last(b, j):
                    norm(b, j + 1) if j + 1 < BPS else norm(b + 1, 0)
                split(b, j)
            sequences(dve, body)

        @block.scalar
        def _(act):
            def turn(b, j):
                t = b * BPS + j
                z = j % 2
                wait(act, turned, t + 1)
                wait(act, v_done, t - 1)
                for c in range(CT):
                    act.activation(xt[:, z, c], p_turn[:, c], ACT.Copy).then_inc(xt_done, 1)

            def body(b, j):
                t = b * BPS + j
                z = j % 2
                if not is_last(b, j):
                    turn(b, j + 1) if j + 1 < BPS else turn(b + 1, 0)
                for m in range(2 * CT):
                    wait(act, qk_done, 4 * t + m + 1)
                    if m == 0 and not (isinstance(t, int) and t < 2):
                        wait(act, stored[z], 16 * 24 * (b * (BPS // 2) + j // 2))
                    act.activation(part[:, z, 0, m], p_qk[:, m], ACT.Copy).then_inc(part1, 1)
                wait(act, v_done, t + 1)
                for g in range(HG):
                    act.activation(
                        k.v_all[:, b * HG + g, TT * j:TT * j + TT, :] if isinstance(b, int) else
                        k.v_all[:, bass.ds(b * HG + g, 1), TT * j:TT * j + TT, :].rearrange("p u t d -> p (u t) d"),
                        p_v[:, :, g * GH * HD:(g + 1) * GH * HD], ACT.Copy).then_inc(v_copied, 1)
            turn(0, 0)
            sequences(act, body)

        @block.tensor
        def _(pe):
            def turn(b, j):
                t = b * BPS + j
                z = j % 2
                wait(pe, xn_done, TT * (t + 1))
                wait(pe, xt_done, CT * t)
                for c in range(CT):
                    for a in range(TT):
                        ins = pe.transpose(p_turn[:, c, a * P:(a + 1) * P], xn[:, z, a, c * P:(c + 1) * P],
                                           k.ident[:])
                ins.then_inc(turned, 1)

            def body(b, j):
                t = b * BPS + j
                z = j % 2
                if not is_last(b, j):
                    turn(b, j + 1) if j + 1 < BPS else turn(b + 1, 0)
                wait(pe, xt_done, CT * (t + 1))
                for m in range(2 * CT):
                    wait(pe, rest_done, 4 * (t - 1) + m + 1) if not (isinstance(t, int) and t < 1) else None
                    for c in range(CT):
                        ins = pe.matmul(p_qk[:, m], w_qk[:, c, m * P:(m + 1) * P], xt[:, z, c],
                                        start=(c == 0), stop=(c == CT - 1))
                    ins.then_inc(qk_done, 1)
                wait(pe, v_copied, HG * t)
                for a in range(TT):
                    for c in range(CT):
                        ins = pe.matmul(p_v[:, a], xt[:, z, c, a * P:(a + 1) * P], w_v[:, c],
                                        start=(c == 0), stop=(c == CT - 1))
                ins.then_inc(v_done, 1)
            turn(0, 0)
            pe.wait_ge(w_loaded, 3 * 16)
            sequences(pe, body)


def attention_phase(nc, k):
    with ExitStack() as ctx:
        sb = lambda n, s, d=F32: ctx.enter_context(nc.sbuf_tensor(n, s, d))
        ps = lambda n, s, d=F32: ctx.enter_context(nc.psum_tensor(n, s, d))
        sem = lambda n: ctx.enter_context(nc.semaphore(n))
        q_op = [sb(f"q_op{z}", [ROWS, GH, SEQ], BF16) for z in range(2)]
        k_op = [sb(f"k_op{z}", [ROWS, GH, SEQ], BF16) for z in range(2)]
        v_op = [sb(f"v_op{z}", [P, KB, GH, 2 * HD]) for z in range(2)]
        prob = sb("prob", [P, ST.PBUF, 2, BLK])
        part_max = sb("part_max", [P, GH, TT, GROUPS])
        neg_max = sb("neg_max", [P, GH, TT])
        neg_rest = sb("neg_rest", [P, GH, TT])
        shift_cols = sb("shift_cols", [P, P], BF16)
        shift = shift_cols[:, 0:3 * GH * TT].rearrange("p (h a n) -> p h a n", h=GH, a=3)
        shift_row = sb("shift_row", [3 * GH * TT, P], BF16)
        o_t = sb("o_t", [P, BLK])
        inv_sum = sb("inv_sum", [P, TT, GH])
        ctx_out = sb("ctx_out", [P, TT, GH, HD])
        p_s = [ps(f"p_score{i}", [P, 2, BLK]) for i in range(2)]
        p_m = ps("p_max", [P, 2, BLK])
        p_o = ps("p_out", [P, BLK])
        p_x = ps("p_turn", [P, BLK])
        loaded = [sem(f"b_loaded{z}") for z in range(2)]
        ones_made = sem("b_ones_made")
        values_ready = sem("b_values_ready")
        score_ready = sem("b_score_ready")
        prob_ready = sem("b_prob_ready")
        prob_masked = sem("b_prob_masked")
        round_done = sem("b_round_done")
        bank_ready = sem("b_bank_ready")
        bank_read = sem("b_bank_read")
        max_ready = sem("b_max_ready")
        split_step = sem("b_split_step")
        shift_ready = sem("b_shift_ready")
        shift_turned = sem("b_shift_turned")
        shift_copied = sem("b_shift_copied")
        shift_sent = [sem(f"b_shift_sent{i}") for i in range(2)]
        o_copied = sem("b_o_copied")
        ctx_turned = sem("b_ctx_turned")
        inv_ready = sem("b_inv_ready")
        ctx_ready = sem("b_ctx_ready")
        ctx_stored = sem("b_ctx_stored")
        block = ctx.enter_context(nc.Block())
        N, G = ST.n, GROUPS

        def units(eng, step):
            for s in range(-ST.LEAD, 0):
                step(0, 0, s, False, False)
            for z in range(2):
                for s in range(N):
                    step(z, z, s, z > 0, True)
            with eng.Fori(1, UNITS // 2 - 1) as i:
                for z in range(2):
                    for s in range(N):
                        step(2 * i + z, z, s, True, True)
            for z in range(2):
                for s in range(N):
                    step(UNITS - 2 + z, z, s, True, z == 0)
            for s in range(N, N + 14):
                step(UNITS - 1, 1, s, False, False)

        @block.sync
        def _(sp):
            def load(u, z):
                wait(sp, score_ready, N * (u - 1))
                apart(sp)
                wait(sp, bank_ready, 2 * N * (u - 1))
                apart(sp)
                for i in range(len(Q_PART)):
                    for dst, src, p in ((q_op, k.q_parts, Q_PART[i]), (k_op, k.k_parts, K_PART[i])):
                        sp.dma_start(dst[z][i * HD:(i + 1) * HD, :, :],
                                     src[u, p].rearrange("(h r) s -> r h s", r=HD)).then_inc(loaded[z], 16)

            load(0, 0)

            def step(u, z, s, before, after):
                for v, rel in ST.due("load", s, u, False, after):
                    load(v, (z + rel) % 2)
                for v, rel, g in ST.due("shift_send", s, u, before, after):
                    y = (z + rel) % 2
                    wait(sp, shift_copied, G * v + g + 1)
                    apart(sp)
                    for h in range(GH):
                        sp.dma_start(q_op[y][PROD:ROWS, h, g * BLK:(g + 1) * BLK],
                                     shift_row[h * 3 * TT:(h + 1) * 3 * TT, :]).then_inc(shift_sent[g % 2], 16)
                for v, rel, g in ST.due("ctx_store", s, u, before, after):
                    wait(sp, ctx_ready, G * v + g + 1)
                    apart(sp)
                    sp.dma_start(k.ctx[v, g * BLK:(g + 1) * BLK, :].rearrange("(a p) c -> p a c", p=P),
                                 ctx_out[:].rearrange("p a h d -> p a (h d)")).then_inc(ctx_stored, 16)
            units(sp, step)
            sp.wait_ge(ctx_stored, 16 * G * UNITS)

        @block.gpsimd
        def _(pool):
            pool.memset(shift_cols[:], 0.0).then_inc(ones_made, 1)
            made = 1
            for z in range(2):
                for part in (k_op[z][PROD:ROWS], v_op[z][:, :, :, HD:2 * HD]):
                    pool.wait_ge(ones_made, made)
                    pool.memset(part, 1.0).then_inc(ones_made, 1)
                    made += 1

            def values(v, z):
                wait(pool, round_done, ST.rounds * (v - 1))
                apart(pool)
                src = k.v_all[:, v] if isinstance(v, int) else \
                    k.v_all[:, bass.ds(v, 1)].rearrange("p u t d -> p (u t) d")
                pool.tensor_copy(v_op[z][:, :, :, 0:HD], src.rearrange("p t (h d) -> p t h d", h=GH))\
                    .then_inc(values_ready, 1)
            pool.wait_ge(ones_made, 5)
            values(0, 0)

            def mask(i, at, n, stride):
                part = prob[:, i % ST.PBUF, :, :].rearrange("p b n -> p (b n)")
                if n > 1:
                    part = part[:, at:at + n * stride].rearrange("p (n w) -> p n w", n=n)[:, :, 0:P]
                    pattern = [[0, n], [1, P]]
                else:
                    part = part[:, at:at + P]
                    pattern = [[1, P]]
                return pool.affine_select(out=part, in_=part, compare_op=ALU.is_ge, fill=0.0, base=0,
                                          pattern=pattern, channel_multiplier=-1)

            def step(u, z, s, before, after):
                for v, rel in ST.due("values", s, u, False, after):
                    values(v, (z + rel) % 2)
                if 0 <= s < N and ST.tiles[s][0] != "full":
                    kind = ST.tiles[s][0]
                    i = s + N * z
                    wait(pool, prob_ready, N * u + s + 1)
                    apart(pool)
                    if kind == "diag":
                        mask(i, 0, 2, BLK)
                        mask(i, BLK + 3 * P, 1, 0).then_inc(prob_masked, 1)
                    else:
                        mask(i, 0, GH, 2 * P).then_inc(prob_masked, 1)
                for v, rel, g, _ in ST.due("shift_max", s, u, before, after):
                    c = (G * v + g) * 4
                    wait(pool, max_ready, G * v + g + 1)
                    wait(pool, shift_turned, G * v + g)
                    apart(pool)
                    pool.tensor_copy(shift[:, :, 0, :], neg_max[:]).then_inc(split_step, 1)
                    wait(pool, split_step, c + 1)
                    pool.tensor_tensor(neg_rest[:], neg_max[:], shift[:, :, 0, :], ALU.subtract).then_inc(split_step, 1)
                    wait(pool, split_step, c + 2)
                    apart(pool)
                    pool.tensor_copy(shift[:, :, 1, :], neg_rest[:]).then_inc(split_step, 1)
                    wait(pool, split_step, c + 3)
                    pool.tensor_tensor(shift[:, :, 2, :], neg_rest[:], shift[:, :, 1, :], ALU.subtract)\
                        .then_inc(split_step, 1)
            units(pool, step)

        @block.vector
        def _(dve):
            def step(u, z, s, before, after):
                for v, rel, j in ST.banks_due(s, u, after):
                    g, pieces = ST.banks[j]
                    wait(dve, bank_ready, 2 * N * v + j + 1)
                    if len(pieces) == 1:
                        h, qb, key, n, _ = pieces[0]
                        dve.tensor_reduce(part_max[:, h, qb, key // BLK:key // BLK + 1], p_m[:, j % 2, 0:n],
                                          AX.X, ALU.max).then_inc(bank_read, 1)
                    elif pieces[0][3] == pieces[1][3]:
                        h = pieces[0][0]
                        dve.tensor_reduce(part_max[:, h:h + 2, 1, g:g + 1],
                                          p_m[:, j % 2, :].rearrange("p (h n) -> p h n", h=2),
                                          AX.X, ALU.max).then_inc(bank_read, 1)
                    else:
                        at = 0
                        for h, qb, key, n, _ in pieces:
                            ins = dve.tensor_reduce(part_max[:, h, qb, g:g + 1], p_m[:, j % 2, at:at + n],
                                                    AX.X, ALU.max)
                            at += n
                        ins.then_inc(bank_read, 1)
                for v, rel, g, nb in ST.due("shift_max", s, u, before, after):
                    wait(dve, bank_read, 2 * N * v + nb)
                    wait(dve, split_step, 4 * (G * v + g))
                    dve.tensor_reduce(neg_max[:], part_max[:, :, :, 0:g + 1],
                                      AX.X, ALU.max, negate=True).then_inc(max_ready, 1)
                    wait(dve, max_ready, G * v + g + 1)
                for v, rel, g in ST.due("ctx_norm", s, u, before, after):
                    turned = p_x[:].rearrange("p (a h e) -> p a h e", a=TT, h=GH)
                    wait(dve, ctx_turned, G * v + g + 1)
                    dve.reciprocal(inv_sum[:], turned[:, :, :, HD]).then_inc(inv_ready, 1)
                    wait(dve, inv_ready, G * v + g + 1)
                    wait(dve, ctx_stored, 16 * (G * v + g))
                    dve.tensor_tensor(ctx_out[:], turned[:, :, :, 0:HD],
                                      inv_sum[:].unsqueeze(3).broadcast_to([P, TT, GH, HD]), ALU.mult)\
                        .then_inc(ctx_ready, 1)
            units(dve, step)

        @block.scalar
        def _(act):
            def step(u, z, s, before, after):
                if 0 <= s < N:
                    i = s + N * z
                    wait(act, score_ready, N * u + s + 1)
                    if not (isinstance(u, int) and u == 0 and s < ST.PBUF):
                        if s >= ST.PBUF:
                            wait(act, round_done, ST.rounds * u + ST.round_of_tile[s - ST.PBUF])
                        else:
                            wait(act, round_done, ST.rounds * (u - 1) + ST.round_of_tile[s - ST.PBUF + N])
                    act.activation(prob[:, i % ST.PBUF, :, :], p_s[s % 2][:], ACT.Exp, scale=SCALE)\
                        .then_inc(prob_ready, 1)
                for v, rel, g in ST.due("shift_copy", s, u, before, after):
                    wait(act, shift_turned, G * v + g + 1)
                    if not (isinstance(v, int) and (v, g) == (0, 0)):
                        n = G * v + g
                        y = (g - 1) % 2
                        sent_before = (G // 2) * v + (g + 1) // 2 if y == 0 else (G // 2) * v + g // 2
                        wait(act, shift_sent[y], 16 * GH * sent_before)
                    act.activation(shift_row[:], p_x[0:3 * GH * TT, 0:P // 2].bitcast(BF16), ACT.Copy)\
                        .then_inc(shift_copied, 1)
                for v, rel, g, rounds in ST.due("o_copy", s, u, before, after):
                    wait(act, round_done, ST.rounds * v + rounds)
                    wait(act, ctx_turned, G * v + g)
                    act.activation(o_t[:], p_o[:], ACT.Copy).then_inc(o_copied, 1)
            units(act, step)

        @block.tensor
        def _(pe):
            pe.wait_ge(ones_made, 5)

            def scores_for_max(v, rel, z, j):
                g, pieces = ST.banks[j]
                y = (z + rel) % 2
                if j == 0:
                    wait(pe, loaded[y], 16 * 2 * len(Q_PART) * (v // 2 + 1))
                if not (isinstance(v, int) and v == 0 and j < 2):
                    wait(pe, bank_read, 2 * N * v + j - 1)
                at = 0
                for h, qb, key, n, masked in pieces:
                    q0 = g * BLK + qb * P
                    out = p_m[:, j % 2, at:at + n]
                    last = pe.matmul(out, q_op[y][0:PROD, h, q0:q0 + P], k_op[y][0:PROD, h, key:key + n],
                                     start=True, stop=not masked)
                    if masked:
                        last = pe.matmul(p_m[:, j % 2, at + n - P:at + n], k.ident_b[:], k.causal[:],
                                         start=False, stop=True)
                    at += n
                last.then_inc(bank_ready, 1)

            def scores(u, z, s):
                kind, g, h, kb = ST.tiles[s]
                if ST.first[g] == s:
                    y = g % 2
                    wait(pe, shift_sent[y], 16 * GH * ((G // 2) * u + g // 2 + 1))
                wait(pe, prob_ready, N * u + s - 1)
                out = p_s[s % 2]

                def product(o, h, kb, q0, n):
                    return pe.matmul(o, k_op[z][:, h, kb * P:(kb + 1) * P], q_op[z][:, h, q0:q0 + n],
                                     start=True, stop=True)
                q0 = g * BLK
                if kind == "full":
                    product(out[:, 0], h, kb, q0, BLK)
                    last = product(out[:, 1], h, kb + 1, q0, BLK)
                elif kind == "diag":
                    product(out[:, 0], h, kb, q0, BLK)
                    product(out[:, 1, 0:3 * P], h, kb + 1, q0 + P, 3 * P)
                    last = product(out[:, 1, 3 * P:], h, kb + 3, q0 + 3 * P, P)
                else:
                    for h in range(GH):
                        a = (h % 2) * 2 * P
                        last = product(out[:, h // 2, a:a + 2 * P], h, kb, q0 + 2 * P, 2 * P)
                last.then_inc(score_ready, 1)

            def values_product(v, y, g, kind, kb, half, first, rounds, masked):
                if kb == 0 and half == 0:
                    wait(pe, o_copied, G * v + g)
                    if g == 0:
                        wait(pe, values_ready, v + 1)

                def product(h, kb, q0, slot, bank, at, n, start, stop):
                    return pe.matmul(p_o[32 * h:32 * h + 2 * HD, q0:q0 + n], v_op[y][:, kb, h, :],
                                     prob[:, slot, bank, at:at + n], start=start, stop=stop,
                                     tile_position=(0, 32 * h), skip_group_check=True)
                slot = [(first + N * y + h) % ST.PBUF for h in range(GH)]
                if kind == "corner":
                    wait(pe, prob_masked, ST.masked * v + masked)
                    for h in range(GH):
                        last = product(h, kb, 2 * P, slot[0], h // 2, (h % 2) * 2 * P, 2 * P, False, True)
                    last.then_inc(round_done, 1)
                    return
                if half == 0:
                    if kind == "diag":
                        wait(pe, prob_masked, ST.masked * v + masked)
                    else:
                        wait(pe, prob_ready, N * v + first + GH)
                for h in range(GH):
                    if half == 0:
                        last = product(h, kb, 0, slot[h], 0, 0, BLK, kb == 0, False)
                    elif kind == "full":
                        last = product(h, kb + 1, 0, slot[h], 1, 0, BLK, False, False)
                    else:
                        last = product(h, kb + 1, P, slot[h], 1, 0, 3 * P, False, False)
                if half and kind == "diag":
                    for h in range(GH):
                        last = product(h, kb + 3, 3 * P, slot[h], 1, 3 * P, P, False, False)
                if half:
                    last.then_inc(round_done, 1)

            turns = [(s, "shift", g) for s, (g,) in ST.plan["shift_turn"]] + \
                [(s, "ctx", g) for s, (g,) in ST.plan["ctx_turn"]]
            assert len({s % N for s, _, _ in turns}) == len(turns)

            def turn_free(kind, g, v):
                s = [a for a, kk, gg in turns if (kk, gg) == (kind, g)][0]
                for other, seen in (("shift", shift_copied), ("ctx", ctx_ready)):
                    counts = [v + ((s - a - 1) // N + 1) for a, kk, _ in turns if kk == other]
                    if isinstance(v, int):
                        counts = [min(max(0, c), UNITS) for c in counts]
                        wait(pe, seen, sum(counts))
                    else:
                        wait(pe, seen, G * v + sum((s - a - 1) // N + 1 for a, kk, _ in turns if kk == other))

            def step(u, z, s, before, after):
                if 0 <= s < N:
                    scores(u, z, s)
                for v, rel, *what in ST.due("pv", s, u, before, after):
                    values_product(v, (z + rel) % 2, *what)
                for v, rel, g in ST.due("ctx_turn", s, u, before, after):
                    turn_free("ctx", g, v)
                    wait(pe, o_copied, G * v + g + 1)
                    for a in range(TT):
                        last = pe.transpose(p_x[:, a * P:(a + 1) * P], o_t[:, a * P:(a + 1) * P], k.ident[:])
                    last.then_inc(ctx_turned, 1)
                for v, rel, g in ST.due("shift_turn", s, u, before, after):
                    turn_free("shift", g, v)
                    wait(pe, split_step, 4 * (G * v + g + 1))
                    pe.transpose(p_x[:, 0:P // 2].bitcast(BF16), shift_cols[:], k.ident_b[:]).then_inc(shift_turned, 1)
                for v, rel, j in ST.banks_due(s, u, after):
                    scores_for_max(v, rel, z, j)
            units(pe, step)


def block_pass(nc, k, w, first):
    name = "d" if first else "e"
    with ExitStack() as ctx:
        sb = lambda n, s, d=F32: ctx.enter_context(nc.sbuf_tensor(f"{name}_{n}", s, d))
        ps = lambda n, s, d=F32: ctx.enter_context(nc.psum_tensor(f"{name}_{n}", s, d))
        sem = lambda n: ctx.enter_context(nc.semaphore(f"{name}_{n}"))
        x_in = sb("x_in", [P, 2, TT, D])
        side = sb("side", [P, 2, TT, D])
        a_t = sb("a_t", [P, CT, BLK])
        state = sb("state", [P, CT, 1 + BLK])
        diff = sb("diff", [P, CT, BLK])
        v_in = sb("v_in", [P, CT, BLK])
        r_in = sb("r_in", [P, CT, BLK])
        gate = sb("gate", [P, TT, D])
        x_mid = sb("x_mid", [P, 2, TT, D])
        x_bias = sb("x_bias", [P, 2, TT, D])
        xn = sb("xn", [P, TT, D])
        x_t = sb("x_t", [P, CT, BLK])
        hidden = sb("hidden", [P, HT, BLK])
        stats = sb("stats", [P, 2, TT, 6])
        mean_var = sb("mean_var", [P, 2, TT, 2])
        var_eps = sb("var_eps", [P, 2, TT])
        rstd = sb("rstd", [P, 2, TT])
        p_turn = ps("turn", [P, CT, BLK])
        p_h = ps("h", [P, 2, BLK])
        p_y = ps("y", [P, TT, D])
        p_w = ps("w", [P, TT, D])
        x_loaded = [sem(f"x_loaded{i}") for i in range(2)]
        biased = sem("biased")
        turn_a = sem("turn_a")
        copied_a = sem("copied_a")
        turn_b = sem("turn_b")
        copied_b = sem("copied_b")
        h_ready = sem("h_ready")
        h_done = sem("h_done")
        r_ready = sem("r_ready")
        gate_done = sem("gate_done")
        w_ready = sem("w_ready")
        w_read = sem("w_read")
        mid_ready = sem("mid_ready")
        bias_done = sem("bias_done")
        y_ready = sem("y_ready")
        x_ready = sem("x_ready")
        stat_step = [sem(f"stat_step{i}") for i in range(2)]
        stats_done = [sem(f"stats_done{i}") for i in range(2)]
        eps_added = [sem(f"eps_added{i}") for i in range(2)]
        rstd_done = [sem(f"rstd_done{i}") for i in range(2)]
        xn_done = [sem(f"xn_done{i}") for i in range(2)]
        carried = sem("carried")
        summed = sem("summed")
        diffed = sem("diffed")
        mixed = sem("mixed")
        stored = [sem(f"stored{i}") for i in range(2)]
        block = ctx.enter_context(nc.Block())
        tiles = "b (n j p) c -> (b n) p j c"
        x_tiles = w.x.rearrange(tiles, n=BPS, p=P)
        out_tiles = w.out.rearrange(tiles, n=BPS, p=P)
        LAST = (BATCH - 1, BPS - 1)

        def sequences(eng, body):
            for j in range(BPS):
                body(0, j)
            with eng.Fori(1, BATCH - 1) as b:
                for j in range(BPS):
                    body(b, j)
            for j in range(BPS):
                body(BATCH - 1, j)

        def following(b, j):
            if isinstance(b, int) and (b, j) == LAST:
                return None
            return (b, j + 1) if j + 1 < BPS else (b + 1, 0)

        def resident(t):
            if isinstance(t, int):
                return k.x_all[:, t]
            return k.x_all[:, bass.ds(t, 1)].rearrange("p u a n -> p (u a) n")

        @block.sync
        def _(sp):
            def load(b, j):
                t = b * BPS + j
                z = j % 2
                wait(sp, w_read, t - 1)
                apart(sp)
                sp.dma_start(x_in[:, z], x_tiles[t]).then_inc(x_loaded[z], 16)
                wait(sp, turn_a, t - 1)
                apart(sp)
                for g in range(HG):
                    sp.dma_start(side[:, z, :, g * GH * HD:(g + 1) * GH * HD],
                                 k.ctx[b * HG + g, j * BLK:(j + 1) * BLK, :].rearrange("(a p) c -> p a c", p=P))\
                        .then_inc(x_loaded[z], 16)

            def store(b, j):
                t = b * BPS + j
                z = j % 2
                wait(sp, x_ready, t + 1)
                apart(sp)
                sp.dma_start(out_tiles[t], side[:, z]).then_inc(stored[z], 16)

            if first:
                sequences(sp, load)
            else:
                sequences(sp, store)
                for z in range(2):
                    sp.wait_ge(stored[z], 16 * NBLK // 2)

        @block.gpsimd
        def _(pool):
            def inverse_std(i, t):
                wait(pool, stats_done[i], TT * (t + 1))
                apart(pool)
                pool.tensor_scalar(var_eps[:, i], mean_var[:, i, :, 1], EPS, None, ALU.add).then_inc(eps_added[i], 1)
                wait(pool, eps_added[i], t + 1)
                pool.tensor_tensor(rstd[:, i], var_eps[:, i], k.minus_half[:], ALU.pow).then_inc(rstd_done[i], 1)

            def body(b, j):
                t = b * BPS + j
                z = j % 2
                if first:
                    wait(pool, x_loaded[z], 16 * (1 + HG) * (b * (BPS // 2) + j // 2 + 1))
                    for a in range(TT):
                        ins = pool.tensor_tensor(x_in[:, z, a], x_in[:, z, a], k.row_bias[:, 0], ALU.add)
                    ins.then_inc(biased, 1)
                else:
                    inverse_std(0, t)
                inverse_std(1, t)
                wait(pool, x_ready, t - 1)
                for a in range(TT):
                    ins = pool.tensor_tensor(x_bias[:, z, a], x_mid[:, z, a], k.row_bias[:, 1], ALU.add)
                ins.then_inc(bias_done, 1)
            sequences(pool, body)

        @block.vector
        def _(dve):
            def norm(i, x, out, t, out_free, out_value):
                for a in range(TT):
                    dve.bn_stats(stats[:, i, a], x[:, a]).then_inc(stat_step[i], 1)
                wait(dve, stat_step[i], TT * (t + 1))
                wait(dve, rstd_done[i], t)
                apart(dve)
                for a in range(TT):
                    dve.bn_aggr(mean_var[:, i, a], stats[:, i, a]).then_inc(stats_done[i], 1)
                wait(dve, stats_done[i], TT * (t + 1))
                wait(dve, rstd_done[i], t + 1)
                wait(dve, out_free, out_value)
                for a in range(TT):
                    ins = dve.tensor_scalar(out[:, a], x[:, a], mean_var[:, i, a, 0:1], rstd[:, i, a:a + 1],
                                            ALU.subtract, ALU.mult)
                ins.then_inc(xn_done[i], 1)

            def decay_sum(b, j):
                t = b * BPS + j
                wait(dve, copied_a, t + 1)
                if j == 0:
                    dve.memset(state[:, :, 0:1], 0.0).then_inc(carried, 1)
                else:
                    dve.tensor_copy(state[:, :, 0:1], state[:, :, BLK:BLK + 1]).then_inc(carried, 1)
                wait(dve, carried, t + 1)
                for c in range(CT):
                    dve.tensor_tensor_scan(state[:, c, 1:BLK + 1], k.channel[:, 4, c:c + 1].broadcast_to([P, BLK]),
                                           a_t[:, c], state[:, c, 0:1], ALU.mult, ALU.add).then_inc(summed, 1)
                wait(dve, summed, CT * (t + 1))
                for c in range(CT):
                    dve.tensor_tensor(diff[:, c], a_t[:, c], state[:, c, 0:BLK], ALU.subtract).then_inc(diffed, 1)
                wait(dve, diffed, CT * (t + 1))
                wait(dve, w_ready, t)
                for c in range(CT):
                    for m, out in ((2, r_in), (1, v_in)):
                        ins = dve.scalar_tensor_tensor(out[:, c], diff[:, c], k.channel[:, m, c:c + 1],
                                                       state[:, c, 0:BLK], ALU.mult, ALU.add)
                ins.then_inc(mixed, 1)

            def front(b, j):
                t = b * BPS + j
                z = j % 2
                wait(dve, w_ready, t + 1)
                wait(dve, bias_done, t - 1)
                if first:
                    wait(dve, biased, t + 1)
                    for a in range(2):
                        ins = dve.tensor_tensor(x_mid[:, z, 2 * a:2 * a + 2], p_w[:, 2 * a:2 * a + 2],
                                                x_in[:, z, 2 * a:2 * a + 2], ALU.add)
                    ins.then_inc(w_read, 1)
                else:
                    wait(dve, gate_done, t + 1)
                    for a in range(2):
                        ins = dve.tensor_tensor(diff[:].rearrange("p c n -> p (c n)")[:, a * BLK:(a + 1) * BLK],
                                                p_w[:, 2 * a:2 * a + 2].rearrange("p a n -> p (a n)"),
                                                gate[:, 2 * a:2 * a + 2].rearrange("p a n -> p (a n)"), ALU.mult)
                    ins.then_inc(w_read, 1)
                    wait(dve, w_read, t + 1)
                    ins = dve.tensor_tensor(x_mid[:, z], diff[:].rearrange("p c n -> p (c n)")
                                            .rearrange("p (a n) -> p a n", a=TT), resident(t), ALU.add)
                ins.then_inc(mid_ready, 1) if not first else None
                if first:
                    wait(dve, w_read, t + 1)
                else:
                    wait(dve, mid_ready, t + 1)
                norm(1, x_mid[:, z], xn, t, turn_b, t)

            def norm_front(b, j):
                if not first:
                    t = b * BPS + j
                    norm(0, resident(t), x_in[:, j % 2], t, turn_a, t - 1)

            def back(b, j):
                t = b * BPS + j
                z = j % 2
                wait(dve, y_ready, t + 1)
                wait(dve, bias_done, t + 1)
                if not first and not (isinstance(t, int) and t < 2):
                    wait(dve, stored[z], 16 * (b * (BPS // 2) + j // 2))
                out = resident(t) if first else side[:, z]
                for a in range(2):
                    ins = dve.tensor_tensor(out[:, 2 * a:2 * a + 2], p_y[:, 2 * a:2 * a + 2],
                                            x_bias[:, z, 2 * a:2 * a + 2], ALU.add)
                ins.then_inc(x_ready, 1)

            norm_front(0, 0)
            if not first:
                decay_sum(0, 0)
            front(0, 0)
            if not first:
                norm_front(0, 1)

            def body(b, j):
                after = following(b, j)
                if after:
                    if not first:
                        decay_sum(*after)
                    front(*after)
                    if not first and following(*after):
                        norm_front(*following(*after))
                back(b, j)
            sequences(dve, body)

        @block.scalar
        def _(act):
            def copy_a(b, j):
                t = b * BPS + j
                wait(act, turn_a, t + 1)
                if first:
                    wait(act, w_ready, t)
                else:
                    wait(act, diffed, CT * t)
                for c in range(CT):
                    ins = act.activation(a_t[:, c], p_turn[:, c], ACT.Copy)
                ins.then_inc(copied_a, 1)

            def copy_b(b, j):
                t = b * BPS + j
                wait(act, turn_b, t + 1)
                wait(act, h_ready, HT * t)
                for c in range(CT):
                    ins = act.activation(x_t[:, c], p_turn[:, c], ACT.Copy)
                ins.then_inc(copied_b, 1)

            def gate_of(b, j):
                if not first:
                    t = b * BPS + j
                    wait(act, r_ready, t + 1)
                    wait(act, w_read, t)
                    for a in range(2):
                        ins = act.activation(gate[:, 2 * a:2 * a + 2], p_w[:, 2 * a:2 * a + 2], ACT.Sigmoid)
                    ins.then_inc(gate_done, 1)

            def gelus(b, j, lo, hi):
                t = b * BPS + j
                for m in range(lo, hi):
                    wait(act, h_ready, HT * t + m + 1)
                    act.activation(hidden[:, m], p_h[:, m % 2], ACT.Gelu, bias=k.hidden_bias[:, m:m + 1])\
                        .then_inc(h_done, 1)

            copy_a(0, 0)
            gate_of(0, 0)
            copy_b(0, 0)

            def body(b, j):
                after = following(b, j)
                gelus(b, j, 0, 2)
                if after:
                    copy_a(*after)
                gelus(b, j, 2, 6)
                if after:
                    gate_of(*after)
                gelus(b, j, 6, HT)
                if after:
                    copy_b(*after)
            sequences(act, body)

        @block.tensor
        def _(pe):
            def turns_a(b, j):
                t = b * BPS + j
                z = j % 2
                if first:
                    wait(pe, x_loaded[z], 16 * (1 + HG) * (b * (BPS // 2) + j // 2 + 1))
                else:
                    wait(pe, xn_done[0], t + 1)
                wait(pe, copied_b, t)
                source = side if first else x_in
                for c in range(CT):
                    for a in range(TT):
                        ins = pe.transpose(p_turn[:, c, a * P:(a + 1) * P], source[:, z, a, c * P:(c + 1) * P],
                                           k.ident[:])
                ins.then_inc(turn_a, 1)

            def turns_b(b, j):
                t = b * BPS + j
                wait(pe, xn_done[1], t + 1)
                wait(pe, copied_a, t + 1)
                for c in range(CT):
                    for a in range(TT):
                        ins = pe.transpose(p_turn[:, c, a * P:(a + 1) * P], xn[:, a, c * P:(c + 1) * P], k.ident[:])
                ins.then_inc(turn_b, 1)

            def rows_product(out, left, right):
                for a in range(TT):
                    for c in range(CT):
                        ins = pe.matmul(out[:, a], left[:, c, a * P:(a + 1) * P], right[:, c],
                                        start=(c == 0), stop=(c == CT - 1))
                return ins

            def gate_product(b, j):
                if not first:
                    t = b * BPS + j
                    wait(pe, mixed, t + 1)
                    wait(pe, w_read, t)
                    rows_product(p_w, r_in, k.w_r).then_inc(r_ready, 1)

            def layer_product(b, j):
                t = b * BPS + j
                if first:
                    wait(pe, copied_a, t + 1)
                    wait(pe, w_read, t)
                    rows_product(p_w, a_t, k.w_o).then_inc(w_ready, 1)
                else:
                    wait(pe, gate_done, t + 1)
                    rows_product(p_w, v_in, k.w_vo).then_inc(w_ready, 1)

            def up(b, j, lo, hi):
                t = b * BPS + j
                if lo == 0:
                    wait(pe, copied_b, t + 1)
                for m in range(lo, hi):
                    wait(pe, h_done, HT * t + m - 1)
                    for c in range(CT):
                        ins = pe.matmul(p_h[:, m % 2], k.up_matrix[:, c, m * P:(m + 1) * P], x_t[:, c],
                                        start=(c == 0), stop=(c == CT - 1))
                    ins.then_inc(h_ready, 1)

            def down(b, j, lo, hi):
                t = b * BPS + j
                if lo == 0:
                    wait(pe, h_done, HT * (t + 1))
                    wait(pe, x_ready, t)
                for a in range(lo, hi):
                    for m in range(HT):
                        ins = pe.matmul(p_y[:, a], hidden[:, m, a * P:(a + 1) * P], k.down_matrix[:, m],
                                        start=(m == 0), stop=(m == HT - 1))
                if hi == TT:
                    ins.then_inc(y_ready, 1)

            turns_a(0, 0)
            gate_product(0, 0)
            layer_product(0, 0)
            turns_b(0, 0)

            def body(b, j):
                after = following(b, j)
                up(b, j, 0, 2)
                if after:
                    turns_a(*after)
                up(b, j, 2, 6)
                if after:
                    gate_product(*after)
                up(b, j, 6, HT)
                if after:
                    layer_product(*after)
                down(b, j, 0, 2)
                if after:
                    turns_b(*after)
                down(b, j, 2, TT)
            sequences(pe, body)


def hybrid_block(nc, w):
    k = Shared()
    k.q_parts = nc.dram_tensor("q_parts", (UNITS, 3, GH * HD, SEQ), BF16, kind="Internal").ap()
    k.k_parts = nc.dram_tensor("k_parts", (UNITS, 3, GH * HD, SEQ), BF16, kind="Internal").ap()
    k.ctx = nc.dram_tensor("ctx", (UNITS, SEQ, GH * HD), F32, kind="Internal").ap()
    with ExitStack() as ctx:
        sb = lambda n, s, d=F32: ctx.enter_context(nc.sbuf_tensor(n, s, d))
        k.ident = sb("ident", [P, P])
        k.ident_b = sb("ident_b", [P, P], BF16)
        k.causal = sb("causal", [P, P], BF16)
        k.minus_half = sb("minus_half", [P, TT])
        k.row_bias = sb("row_bias", [P, 2, D])
        k.hidden_bias = sb("hidden_bias", [P, HT])
        k.channel = sb("channel", [P, 5, CT])
        k.w_o = sb("w_o", [P, CT, D])
        k.w_r = sb("w_r", [P, CT, D])
        k.w_vo = sb("w_vo", [P, CT, D])
        k.up_matrix = sb("up_matrix", [P, CT, HID])
        k.down_matrix = sb("down_matrix", [P, HT, D])
        k.setup_done = ctx.enter_context(nc.semaphore("setup_done"))
        consts_phase(nc, k, w)
        with nc.sbuf_tensor("v_all", [P, UNITS, KB, GH * HD], F32) as v_all:
            k.v_all = v_all
            project_phase(nc, k, w)
            attention_phase(nc, k)
        with nc.sbuf_tensor("x_all", [P, NBLK, TT, D], F32) as x_all:
            k.x_all = x_all
            block_pass(nc, k, w, True)
            block_pass(nc, k, w, False)


_INS = {"L0_attn_a_x": "x", "L0_attn_a_W_q": "W_q", "L0_attn_a_W_k": "W_k", "L0_attn_a_W_v": "W_v",
        "L0_attn_a_W_o": "W_o", "L0_attn_a_b_o": "b_o", "L0_attn_b_time_decay": "time_decay",
        "L0_attn_b_time_mix_k": "time_mix_k", "L0_attn_b_time_mix_v": "time_mix_v",
        "L0_attn_b_time_mix_r": "time_mix_r", "L0_attn_b_Wk": "Wk", "L0_attn_b_Wv": "Wv",
        "L0_attn_b_Wr": "Wr", "L0_attn_b_Wo": "Wo", "L0_ffn_W_exp": "W_exp", "L0_ffn_b_exp": "b_exp",
        "L0_ffn_up_weights": "up_weights", "L0_ffn_up_bias": "up_bias",
        "L0_ffn_down_weights": "down_weights", "L0_ffn_W_con": "W_con", "L0_ffn_b_con": "b_con",
        "L0_ffn_down_bias": "down_bias"}


def kernel(**inputs):
    from types import SimpleNamespace

    import numpy as _np
    import concourse.bacc as _bacc
    from concourse import mybir as _mybir
    from concourse.bass_utils import run_bass_kernel_spmd as _run

    nc = _bacc.Bacc("TRN2", target_bir_lowering=False, num_devices=1)
    arrays, args = {}, {}
    for name, short in _INS.items():
        a = _np.ascontiguousarray(inputs[name])
        arrays[f"in_{name}"] = a
        args[short] = nc.dram_tensor(f"in_{name}", a.shape, _mybir.dt.from_np(a.dtype), kind="ExternalInput").ap()
    out = nc.dram_tensor("out_0", (BATCH, SEQ, D), _mybir.dt.float32, kind="ExternalOutput").ap()
    hybrid_block(nc, SimpleNamespace(out=out, **args))
    r = _run(nc, [arrays], core_ids=[0])
    return r.results[0]["out_0"]
```

```python
from contextlib import ExitStack

import concourse.bass as bass
from concourse import mybir

F32 = mybir.dt.float32
BF16 = mybir.dt.bfloat16
ALU = mybir.AluOpType
ACT = mybir.ActivationFunctionType
AX = mybir.AxisListType

P = 128
BATCH, SEQ, D = 4, 2048, 256
HEADS, HD = 16, 16
HID = 1024
STAGES = 10
CT = D // P
HT = HID // P
BLK = 512
TT = BLK // P
BPS = SEQ // BLK
NBLK = BATCH * BPS
EPS = 1e-5

GH = 4
HG = HEADS // GH
UNITS = BATCH * HG
KB = SEQ // P
GROUPS = SEQ // BLK
SCALE = float(HD) ** -0.5
NEG = -1e30
Q_PART = [0, 0, 1, 1, 0, 2]
K_PART = [0, 1, 0, 1, 2, 0]
PROD = HD * len(Q_PART)
ROWS = PROD + 3


class Steps:

    LEAD = 38
    RING = 3
    PBUF = 8

    def __init__(self):
        self.tiles = []
        self.plan = {}
        self.round_of_tile = []
        self.first = {}
        rounds = 0
        masked = 0
        self.masked_before = []
        for g in range(GROUPS):
            self.first[g] = len(self.tiles)
            for r in range(2 * g + 1):
                kind = "full" if r < 2 * g else "diag"
                for h in range(GH):
                    self.tiles.append((kind, g, h, 2 * r))
                    self.round_of_tile.append(rounds + 1)
                    self.masked_before.append(masked)
                    masked += kind == "diag"
                last = len(self.tiles) - 1
                late = 2 + (kind == "diag")
                for half in range(2):
                    self.add("pv", last + late + half, (g, kind, 2 * r, half, last - GH + 1, rounds, masked))
                rounds += 1
            self.tiles.append(("corner", g, 0, 4 * g + 2))
            self.masked_before.append(masked)
            masked += 1
            self.round_of_tile.append(rounds + 1)
            c = len(self.tiles) - 1
            self.add("pv", c + 3, (g, "corner", 4 * g + 2, 0, c, rounds, masked))
            rounds += 1
            self.add("o_copy", c + 4, (g, rounds))
            self.add("ctx_turn", c + 6, (g,))
            self.add("ctx_store", c + 7, (g,))
        self.n = len(self.tiles)
        self.rounds = rounds
        self.masked = masked
        self.banks = []
        for g in range(GROUPS):
            for h in range(GH):
                for qb in range(TT):
                    for j in range(g):
                        self.banks.append((g, [(h, qb, j * BLK, BLK, False)]))
            for h in range(GH):
                self.banks.append((g, [(h, 3, g * BLK, 4 * P, True)]))
            for h in range(GH):
                self.banks.append((g, [(h, 2, g * BLK, 3 * P, True), (h, 0, g * BLK, P, True)]))
            for h in range(0, GH, 2):
                self.banks.append((g, [(h, 1, g * BLK, 2 * P, True), (h + 1, 1, g * BLK, 2 * P, True)]))
            assert len(self.banks) % 2 == 0
            s = len(self.banks) // 2 - 1 - self.LEAD
            self.add("shift_max", s, (g, len(self.banks)))
            self.add("shift_turn", s + 3, (g,))
            self.add("shift_send", s + 4, (g,))
            assert s + 6 < self.first[g]
        assert len(self.banks) == 2 * self.n and self.n % 4 == 0
        self.add("load", 3 - self.n, ())
        self.add("values", 3 - self.n, ())
        self.ring = []
        self.ring_of_step = []
        for s in range(self.n):
            banks = [(v, "bank", j) for v, _, j in self.banks_due(s, 0)]
            turns = [(v, kind[:-5], g) for kind in ("ctx_turn", "shift_turn")
                     for v, _, g in self.due(kind, s, 0)]
            self.ring_of_step.append(len(self.ring))
            self.ring += [banks[0]] + turns + [banks[1]]
        assert len(self.ring) % self.RING == 0

    def add(self, kind, step, what):
        self.plan.setdefault(kind, []).append((step, what))

    def due(self, kind, step, u, before=True, after=True):
        for rel in (-1, 0, 1):
            if (rel < 0 and not before) or (rel > 0 and not after):
                continue
            for s, what in self.plan[kind]:
                if s == step - rel * self.n:
                    yield (u + rel, rel) + what

    def ring_due(self, step, u):
        s = step % self.n
        end = (self.ring_of_step + [len(self.ring)])[s + 1]
        for at in range(self.ring_of_step[s], end):
            rel, kind, number = self.ring[at]
            v = u + rel + step // self.n
            if not isinstance(v, int) or 0 <= v < UNITS:
                yield v, rel + step // self.n, kind, number, at

    def before(self, at, v):
        rel = self.ring[at][0]
        for back in range(self.RING, 4 * self.RING):
            lap, place = divmod(at - back, len(self.ring))
            other, kind, number = self.ring[place]
            owner = v - rel + other + lap
            if not isinstance(owner, int) or 0 <= owner < UNITS:
                return owner, kind, number
            if isinstance(owner, int) and owner < 0 and kind == "bank":
                return None
        return None

    def banks_due(self, step, u, after=True):
        j = step + self.LEAD
        if j < self.n:
            yield from ((u, 0, 2 * j), (u, 0, 2 * j + 1))
        elif after:
            yield from ((u + 1, 1, 2 * (j - self.n)), (u + 1, 1, 2 * (j - self.n) + 1))


ST = Steps()


def wait(eng, sem, value):
    if isinstance(value, int) and value <= 0:
        return
    eng.wait_ge(sem, value)


def apart(eng):
    eng.nop(nofuse=True)


class Shared:
    pass


LOW = 7
HIGH = STAGES - LOW


def consts_phase(nc, k, w):
    with ExitStack() as ctx:
        sb = lambda n, s, d=F32: ctx.enter_context(nc.sbuf_tensor(n, s, d))
        ps = lambda n, s, d=F32: ctx.enter_context(nc.psum_tensor(n, s, d))
        sem = lambda n: ctx.enter_context(nc.semaphore(n))
        row = sb("butterfly_row", [1, 2, 2 * HID])
        up_w = sb("up_stage", [P, 2, 2 * HID])
        down_w = sb("down_stage", [P, LOW, 2 * HID])
        high_w = sb("high_weights", [P, 2, HIGH, HT // 2, 4])
        low = [sb(f"low{i}", [P, HID]) for i in range(2)]
        low_up = sb("low_up", [P, HID])
        low_down = sb("low_down", [P, HID])
        product = sb("product", [P, 2, HID])
        exp_rows = sb("exp_rows", [P, CT, HID])
        exp_cols = sb("exp_cols", [P, HT, D + 1])
        up_x = [sb(f"up_x{i}", [P, HT, D + 1]) for i in range(2)]
        down_x = [sb(f"down_x{i}", [P, HT, D + 1]) for i in range(2)]
        scaled = sb("scaled", [P, HT, D + 1])
        up_bias = sb("up_bias_cols", [P, HT])
        square = sb("square_weights", [P, 3, CT, D])
        wo_t = sb("wo_turned", [P, CT, D])
        rows = sb("bias_rows", [1, 3, D])
        bank = ps("c_bank", [P, 8, 512])
        con_loaded = sem("c_con_loaded")
        exp_loaded = sem("c_exp_loaded")
        square_loaded = sem("c_square_loaded")
        rows_loaded = sem("c_rows_loaded")
        small_loaded = sem("c_small_loaded")
        row_loaded = [sem(f"c_row_loaded{i}") for i in range(2)]
        down_loaded = [sem(f"c_down_loaded{i}") for i in range(LOW)]
        spread = sem("c_spread")
        ident_step = sem("c_ident_step")
        made = sem("c_made")
        rows_added = sem("c_rows_added")
        low_step = sem("c_low_step")
        low_stage = sem("c_low_stage")
        low_begun = sem("c_low_begun")
        high_scaled = sem("c_high_scaled")
        high_done = sem("c_high_done")
        turned = sem("c_turned")
        exp_copied = sem("c_exp_copied")
        square_copied = sem("c_square_copied")
        composed = sem("c_composed")
        vo_copied = sem("c_vo_copied")
        applied = sem("c_applied")
        up_copied = sem("c_up_copied")
        down_applied = sem("c_down_applied")
        down_copied = sem("c_down_copied")
        bias_ready = sem("c_bias_ready")
        up_turned = sem("c_up_turned")
        matrix_copied = sem("c_matrix_copied")
        block = ctx.enter_context(nc.Block())
        PAIRS = HT // 2
        HIGH_OPS = HIGH * PAIRS * 2

        def pair(stage, n):
            s = 2 ** (stage - LOW)
            a = (n // s) * 2 * s + n % s
            return a, a + s

        @block.sync
        def _(sp):
            sp.dma_start(down_x[0][:, :, 0:D], w.W_con.rearrange("(t p) n -> p t n", p=P)).then_inc(con_loaded, 16)
            for i, m in enumerate((w.up_weights, w.down_weights)):
                for s in range(HIGH):
                    sp.dma_start(high_w[:, i, s], m[LOW + s].rearrange("(n p) r c -> p n (r c)", p=P))\
                        .then_inc(con_loaded, 16)
            for n in range(LOW):
                if n >= 2:
                    sp.wait_ge(spread, n - 1)
                sp.dma_start(row[:, n % 2], w.up_weights[n].rearrange("(o k) r c -> o (k r c)", o=1))\
                    .then_inc(row_loaded[n % 2], 16)
                if n == 1:
                    sp.dma_start(exp_rows[:], w.W_exp.rearrange("(t p) n -> p t n", p=P)).then_inc(exp_loaded, 16)
                    sp.dma_start(exp_cols[:, :, D], w.b_exp.rearrange("(t p) -> p t", p=P),
                                 allow_slow_non_contiguous=True).then_inc(exp_loaded, 16)
                    for i, m in enumerate((w.Wr, w.Wo, w.Wv)):
                        sp.dma_start(square[:, i], m.rearrange("(t p) n -> p t n", p=P)).then_inc(square_loaded, 16)
            for i, m in enumerate((w.b_o, w.b_con, w.down_bias)):
                sp.dma_start(rows[:, i], m.rearrange("(o n) -> o n", o=1)).then_inc(rows_loaded, 16)
            sp.dma_start(k.w_o[:], w.W_o.rearrange("(t p) n -> p t n", p=P)).then_inc(small_loaded, 16)
            for i, m in enumerate((w.time_decay, w.time_mix_v, w.time_mix_r)):
                sp.dma_start(k.channel[:, i, :], m.rearrange("(t p) -> p t", p=P),
                             allow_slow_non_contiguous=True).then_inc(small_loaded, 16)
            sp.dma_start(up_bias[:], w.up_bias.rearrange("(t p) -> p t", p=P),
                         allow_slow_non_contiguous=True).then_inc(small_loaded, 16)
            sp.wait_ge(small_loaded, 5 * 16)

        @block.gpsimd
        def _(pool):
            pool.memset(k.ident[:], 0.0).then_inc(ident_step, 1)
            pool.wait_ge(ident_step, 1)
            pool.affine_select(out=k.ident[:], in_=k.ident[:], compare_op=ALU.not_equal, fill=1.0, base=0,
                               pattern=[[-1, P]], channel_multiplier=1).then_inc(ident_step, 1)
            pool.memset(k.causal[:], 0.0).then_inc(ident_step, 1)
            for n in range(LOW):
                if n >= 2:
                    pool.wait_ge(low_stage, n - 1)
                pool.wait_ge(row_loaded[n % 2], 16 * (n // 2 + 1))
                pool.partition_broadcast(up_w[:, n % 2], row[:, n % 2]).then_inc(spread, 1)
            pool.wait_ge(ident_step, 3)
            pool.affine_select(out=k.causal[:], in_=k.causal[:], compare_op=ALU.is_ge, fill=NEG, base=0,
                               pattern=[[-1, P]], channel_multiplier=1).then_inc(made, 1)
            pool.tensor_copy(k.ident_b[:], k.ident[:]).then_inc(made, 1)
            pool.memset(k.minus_half[:], -0.5).then_inc(made, 1)
            pool.wait_ge(rows_loaded, 3 * 16)
            pool.tensor_tensor(rows[:, 1], rows[:, 1], rows[:, 2], ALU.add).then_inc(rows_added, 1)
            pool.wait_ge(rows_added, 1)
            pool.partition_broadcast(k.row_bias[:, 0, :], rows[:, 0]).then_inc(made, 1)
            pool.partition_broadcast(k.row_bias[:, 1, :], rows[:, 1]).then_inc(made, 1)
            pool.wait_ge(made, 5)

        @block.vector
        def _(dve):
            count = [0]

            def high_stages(which, x, stages, base):
                for m, stage in enumerate(stages):
                    src, dst = x[m % 2], x[(m + 1) % 2]
                    for n in range(PAIRS):
                        a, b = pair(stage, n)
                        for r, out in enumerate((a, b)):
                            rc = 2 * r + 1 if which == 0 else 2 + r
                            wide = D + 1 if which == 0 else D
                            dve.wait_ge(high_scaled, base + (m * PAIRS + n) * 2 + r + 1)
                            dve.scalar_tensor_tensor(
                                dst[:, out, 0:wide], src[:, b, 0:wide],
                                high_w[:, which, stage - LOW, n, rc:rc + 1], scaled[:, 2 * n + r, 0:wide],
                                ALU.mult, ALU.add).then_inc(high_done, 1)
                    dve.wait_ge(high_done, base + (m + 1) * PAIRS * 2)

            def low_stages(which, out):
                for t in range(HT):
                    ins = dve.tensor_copy(low[0][:, t * P:(t + 1) * P], k.ident[:])
                ins.then_inc(low_begun, 1)
                dve.wait_ge(low_begun, which + 1)
                for m in range(LOW):
                    stage = m if which == 0 else LOW - 1 - m
                    s = 2 ** stage
                    src = low[m % 2]
                    dst = low[(m + 1) % 2] if m < LOW - 1 else out
                    if which == 0:
                        dve.wait_ge(spread, m + 1)
                        weights = up_w[:, m % 2]
                    else:
                        dve.wait_ge(down_loaded[stage], 16)
                        weights = down_w[:, stage]
                    weights = weights.rearrange("p (b s r c) -> p r c b s", s=s, r=2, c=2)
                    v = src[:].rearrange("p (b c s) -> p c b s", c=2, s=s)
                    o = dst[:].rearrange("p (b r s) -> p r b s", r=2, s=s)
                    shape = [P, 2, HID // 2 // s, s]
                    for c in range(2):
                        part = weights[:, :, c] if which == 0 else weights[:, c]
                        half = v[:, c].unsqueeze(1).broadcast_to(shape)
                        dve.tensor_tensor(product[:, c].rearrange("p (r b s) -> p r b s", r=2, s=s), part, half,
                                          ALU.mult).then_inc(low_step, 1)
                        count[0] += 1
                    dve.wait_ge(low_step, count[0])
                    dve.tensor_tensor(o, product[:, 0].rearrange("p (r b s) -> p r b s", r=2, s=s),
                                      product[:, 1].rearrange("p (r b s) -> p r b s", r=2, s=s),
                                      ALU.add).then_inc(low_stage, 1)
                    dve.wait_ge(low_stage, which * LOW + m + 1)

            dve.wait_ge(ident_step, 2)
            low_stages(0, low_up)
            high_stages(1, down_x, range(STAGES - 1, LOW - 1, -1), 0)
            low_stages(1, low_down)
            dve.wait_ge(small_loaded, 5 * 16)
            high_stages(0, up_x, range(LOW, STAGES), HIGH_OPS)
            dve.tensor_tensor(k.hidden_bias[:], up_x[HIGH % 2][:, :, D], up_bias[:], ALU.add).then_inc(bias_ready, 1)
            dve.wait_ge(bias_ready, 1)

        @block.scalar
        def _(act):
            for n in range(LOW - 1, -1, -1):
                act.dma_start(down_w[:, n], w.down_weights[n].rearrange("k r c -> (k r c)").partition_broadcast(P))\
                    .then_inc(down_loaded[n], 16)

            act.wait_ge(con_loaded, 7 * 16)
            for m, stage in enumerate(range(STAGES - 1, LOW - 1, -1)):
                if m:
                    act.wait_ge(high_done, m * PAIRS * 2)
                for n in range(PAIRS):
                    a, _ = pair(stage, n)
                    for r in range(2):
                        act.activation(scaled[:, 2 * n + r, 0:D], down_x[m % 2][:, a, 0:D], ACT.Copy,
                                       scale=high_w[:, 1, stage - LOW, n, r:r + 1]).then_inc(high_scaled, 1)
            for t in range(2):
                act.wait_ge(turned, t + 1)
                act.activation(exp_cols[:, 4 * t:4 * t + 4, 0:D],
                               bank[:, 2 * t:2 * t + 2, :].rearrange("p b (t n) -> p (b t) n", n=D),
                               ACT.Copy).then_inc(exp_copied, 1)
            for i, dst in enumerate((k.w_r, wo_t)):
                act.wait_ge(turned, 3)
                act.activation(dst[:], bank[:, 4 + i].rearrange("p (a n) -> p a n", a=CT), ACT.Copy)\
                    .then_inc(square_copied, 1)
            act.wait_ge(composed, 1)
            act.activation(k.w_vo[:], bank[:, 6].rearrange("p (a n) -> p a n", a=CT), ACT.Copy).then_inc(vo_copied, 1)
            act.wait_ge(small_loaded, 5 * 16)
            act.activation(k.channel[:, 3, :], k.channel[:, 0, :], ACT.Exp).then_inc(k.setup_done, 1)
            act.wait_ge(k.setup_done, 1)
            act.activation(k.channel[:, 4, :], k.channel[:, 3, :], ACT.Exp, scale=-1.0).then_inc(k.setup_done, 1)
            for t in range(HT):
                act.wait_ge(applied, t + 1)
                act.activation(up_x[0][:, t], bank[:, t, 0:D + 1], ACT.Copy).then_inc(up_copied, 1)
            for m, stage in enumerate(range(LOW, STAGES)):
                act.wait_ge(up_copied, HT)
                if m:
                    act.wait_ge(high_done, HIGH_OPS + m * PAIRS * 2)
                else:
                    act.wait_ge(high_done, HIGH_OPS)
                for n in range(PAIRS):
                    a, _ = pair(stage, n)
                    for r in range(2):
                        act.activation(scaled[:, 2 * n + r], up_x[m % 2][:, a], ACT.Copy,
                                       scale=high_w[:, 0, stage - LOW, n, 2 * r:2 * r + 1]).then_inc(high_scaled, 1)
            for t in range(4):
                act.wait_ge(down_applied, t + 1)
                act.activation(k.down_matrix[:, 2 * t:2 * t + 2], bank[:, t].rearrange("p (t n) -> p t n", n=D),
                               ACT.Copy).then_inc(down_copied, 1)
            for c in range(CT):
                act.wait_ge(up_turned, c + 1)
                act.activation(k.up_matrix[:, c], bank[:, 4 + 2 * c:6 + 2 * c].rearrange("p b n -> p (b n)"),
                               ACT.Copy).then_inc(matrix_copied, 1)
            act.wait_ge(matrix_copied, CT)
            act.wait_ge(down_copied, 4)

        @block.tensor
        def _(pe):
            pe.wait_ge(ident_step, 2)
            pe.wait_ge(exp_loaded, 2 * 16)
            for t in range(HT):
                for c in range(CT):
                    ins = pe.transpose(bank[:, t // 2, (t % 2) * D + c * P:(t % 2) * D + (c + 1) * P],
                                       exp_rows[:, c, t * P:(t + 1) * P], k.ident[:])
                if t % 4 == 3:
                    ins.then_inc(turned, 1)
            pe.wait_ge(square_loaded, 3 * 16)
            for i in range(2):
                for a in range(CT):
                    for b in range(CT):
                        ins = pe.transpose(bank[:, 4 + i, b * D + a * P:b * D + (a + 1) * P],
                                           square[:, i, a, b * P:(b + 1) * P], k.ident[:])
            ins.then_inc(turned, 1)
            pe.wait_ge(square_copied, 2)
            for h in range(CT):
                for m in range(CT):
                    ins = pe.matmul(bank[:, 6, h * D:(h + 1) * D], square[:, 2, m, h * P:(h + 1) * P],
                                    wo_t[:, m, :], start=(m == 0), stop=(m == CT - 1))
            ins.then_inc(composed, 1)
            pe.wait_ge(low_stage, LOW)
            pe.wait_ge(exp_copied, 2)
            pe.wait_ge(vo_copied, 1)
            for t in range(HT):
                pe.matmul(bank[:, t, 0:D + 1], low_up[:, t * P:(t + 1) * P], exp_cols[:, t], start=True, stop=True)\
                    .then_inc(applied, 1)
            pe.wait_ge(low_stage, 2 * LOW)
            pe.wait_ge(high_done, HIGH_OPS)
            pe.wait_ge(up_copied, HT)
            for t in range(HT):
                ins = pe.matmul(bank[:, t // 2, (t % 2) * D:(t % 2 + 1) * D], low_down[:, t * P:(t + 1) * P],
                                down_x[HIGH % 2][:, t, 0:D], start=True, stop=True)
                if t % 2:
                    ins.then_inc(down_applied, 1)
            pe.wait_ge(high_done, 2 * HIGH_OPS)
            for c in range(CT):
                for t in range(HT):
                    ins = pe.transpose(bank[:, 4 + 2 * c + t // 4, (t % 4) * P:(t % 4 + 1) * P],
                                       up_x[HIGH % 2][:, t, c * P:(c + 1) * P], k.ident[:])
                ins.then_inc(up_turned, 1)


def project_phase(nc, k, w):
    with ExitStack() as ctx:
        sb = lambda n, s, d=F32: ctx.enter_context(nc.sbuf_tensor(n, s, d))
        sem = lambda n: ctx.enter_context(nc.semaphore(n))
        w_qk = sb("w_qk", [P, CT, 2 * D])
        w_v = sb("w_v", [P, CT, D])
        w_loaded = sem("a_w_loaded")
        x_in = sb("a_x", [P, 2, TT, D])
        stats = sb("a_stats", [P, 2, TT, 6])
        mean_var = sb("a_mean_var", [P, 2, TT, 2])
        var_eps = sb("a_var_eps", [P, 2, TT])
        rstd = sb("a_rstd", [P, 2, TT])
        xn = sb("a_xn", [P, 2, TT, D])
        xt = sb("a_xt", [P, 2, CT, BLK])
        part = sb("a_parts", [P, 2, 3, 2 * CT, BLK], BF16)
        rest = sb("a_rest", [P, 2, 2 * CT, BLK])
        p_turn = ctx.enter_context(nc.psum_tensor("a_turn", [P, CT, BLK], F32))
        p_qk = ctx.enter_context(nc.psum_tensor("a_qk", [P, 2 * CT, BLK], F32))
        p_v = ctx.enter_context(nc.psum_tensor("a_v", [P, TT, D], F32))
        x_loaded = [sem(f"a_x_loaded{i}") for i in range(2)]
        stat_step = sem("a_stat_step")
        stats_done = sem("a_stats_done")
        eps_added = sem("a_eps_added")
        rstd_done = sem("a_rstd_done")
        xn_done = sem("a_xn_done")
        turned = sem("a_turned")
        xt_done = sem("a_xt_done")
        qk_done = sem("a_qk_done")
        v_done = sem("a_v_done")
        part1 = sem("a_part1")
        rest_done = sem("a_rest_done")
        part2 = sem("a_part2")
        part3 = sem("a_part3")
        v_copied = sem("a_v_copied")
        stored = [sem(f"a_stored{i}") for i in range(2)]
        block = ctx.enter_context(nc.Block())
        x_tiles = w.x.rearrange("b (n j p) c -> (b n) p j c", n=BPS, p=P)

        def sequences(eng, body):
            for j in range(BPS):
                body(0, j)
            with eng.Fori(1, BATCH - 1) as b:
                for j in range(BPS):
                    body(b, j)
            for j in range(BPS):
                body(BATCH - 1, j)

        def is_last(b, j):
            return isinstance(b, int) and (b, j) == (BATCH - 1, BPS - 1)

        @block.sync
        def _(sp):
            for i, m in enumerate((w.W_q, w.W_k)):
                sp.dma_start(w_qk[:, :, i * D:(i + 1) * D], m.rearrange("(t p) n -> p t n", p=P))\
                    .then_inc(w_loaded, 16)
            sp.dma_start(w_v[:], w.W_v.rearrange("(t p) n -> p t n", p=P)).then_inc(w_loaded, 16)

            def store(b, j):
                t = b * BPS + j
                z = j % 2
                wait(sp, part1, 4 * t + 4)
                apart(sp)
                wait(sp, part2, 4 * t + 4)
                apart(sp)
                wait(sp, part3, 4 * t + 4)
                apart(sp)
                for m in range(2 * CT):
                    dst = k.q_parts if m < CT else k.k_parts
                    sp.dma_start(dst[b * CT + m % CT, :, :, j * BLK:(j + 1) * BLK].rearrange("i r s -> r i s"),
                                 part[:, z, :, m, :]).then_inc(stored[z], 16)

            def load(b, j):
                t = b * BPS + j
                wait(sp, xn_done, TT * (t - 1))
                apart(sp)
                sp.dma_start(x_in[:, j % 2], x_tiles[t]).then_inc(x_loaded[j % 2], 16)

            load(0, 0)

            def body(b, j):
                if not is_last(b, j):
                    load(b, j + 1) if j + 1 < BPS else load(b + 1, 0)
                if not (isinstance(b, int) and (b, j) == (0, 0)):
                    if j:
                        store(b, j - 1)
                    else:
                        store(b - 1, BPS - 1)
            sequences(sp, body)
            store(BATCH - 1, BPS - 1)
            for z in range(2):
                sp.wait_ge(stored[z], 16 * 2 * CT * NBLK // 2)

        @block.gpsimd
        def _(pool):
            def body(b, j):
                t = b * BPS + j
                z = j % 2
                wait(pool, stats_done, TT * (t + 1))
                apart(pool)
                pool.tensor_scalar(var_eps[:, z], mean_var[:, z, :, 1], EPS, None, ALU.add).then_inc(eps_added, 1)
                wait(pool, eps_added, t + 1)
                pool.tensor_tensor(rstd[:, z], var_eps[:, z], k.minus_half[:], ALU.pow).then_inc(rstd_done, 1)
                if not (isinstance(b, int) and (b, j) == (0, 0)):
                    split(b, j - 1) if j else split(b - 1, BPS - 1)

            def split(b, j):
                t = b * BPS + j
                z = j % 2
                for m in range(2 * CT):
                    wait(pool, part2, 4 * t + m + 1)
                    pool.tensor_tensor(part[:, z, 2, m], rest[:, z, m], part[:, z, 1, m], ALU.subtract)\
                        .then_inc(part3, 1)
            sequences(pool, body)
            split(BATCH - 1, BPS - 1)

        @block.vector
        def _(dve):
            def norm(b, j):
                t = b * BPS + j
                z = j % 2
                wait(dve, x_loaded[z], 16 * (b * (BPS // 2) + j // 2 + 1))
                for a in range(TT):
                    dve.bn_stats(stats[:, z, a], x_in[:, z, a]).then_inc(stat_step, 1)
                wait(dve, stat_step, TT * (t + 1))
                wait(dve, rstd_done, t - 1)
                apart(dve)
                for a in range(TT):
                    dve.bn_aggr(mean_var[:, z, a], stats[:, z, a]).then_inc(stats_done, 1)
                wait(dve, stats_done, TT * (t + 1))
                wait(dve, rstd_done, t + 1)
                wait(dve, turned, t - 1)
                for a in range(TT):
                    dve.tensor_scalar(xn[:, z, a], x_in[:, z, a], mean_var[:, z, a, 0:1], rstd[:, z, a:a + 1],
                                      ALU.subtract, ALU.mult).then_inc(xn_done, 1)

            def split(b, j):
                t = b * BPS + j
                z = j % 2
                for m in range(2 * CT):
                    wait(dve, part1, 4 * t + m + 1)
                    wait(dve, part3, 4 * (t - 2) + m + 1) if not (isinstance(t, int) and t < 2) else None
                    dve.tensor_tensor(rest[:, z, m], p_qk[:, m], part[:, z, 0, m], ALU.subtract)\
                        .then_inc(rest_done, 1)
                for m in range(2 * CT):
                    wait(dve, rest_done, 4 * t + m + 1)
                    if m == 0 and not (isinstance(t, int) and t < 2):
                        wait(dve, stored[z], 16 * 2 * CT * (b * (BPS // 2) + j // 2))
                    dve.tensor_copy(part[:, z, 1, m], rest[:, z, m]).then_inc(part2, 1)
            norm(0, 0)

            def body(b, j):
                if not is_last(b, j):
                    norm(b, j + 1) if j + 1 < BPS else norm(b + 1, 0)
                split(b, j)
            sequences(dve, body)

        @block.scalar
        def _(act):
            def turn(b, j):
                t = b * BPS + j
                z = j % 2
                wait(act, turned, t + 1)
                wait(act, v_done, t - 1)
                for c in range(CT):
                    act.activation(xt[:, z, c], p_turn[:, c], ACT.Copy).then_inc(xt_done, 1)

            def body(b, j):
                t = b * BPS + j
                z = j % 2
                if not is_last(b, j):
                    turn(b, j + 1) if j + 1 < BPS else turn(b + 1, 0)
                for m in range(2 * CT):
                    wait(act, qk_done, 4 * t + m + 1)
                    if m == 0 and not (isinstance(t, int) and t < 2):
                        wait(act, stored[z], 16 * 2 * CT * (b * (BPS // 2) + j // 2))
                    act.activation(part[:, z, 0, m], p_qk[:, m], ACT.Copy).then_inc(part1, 1)
                wait(act, v_done, t + 1)
                for g in range(HG):
                    act.activation(
                        k.v_all[:, b * HG + g, TT * j:TT * j + TT, :] if isinstance(b, int) else
                        k.v_all[:, bass.ds(b * HG + g, 1), TT * j:TT * j + TT, :].rearrange("p u t d -> p (u t) d"),
                        p_v[:, :, g * GH * HD:(g + 1) * GH * HD], ACT.Copy).then_inc(v_copied, 1)
            turn(0, 0)
            sequences(act, body)

        @block.tensor
        def _(pe):
            def turn(b, j):
                t = b * BPS + j
                z = j % 2
                wait(pe, xn_done, TT * (t + 1))
                wait(pe, xt_done, CT * t)
                for c in range(CT):
                    for a in range(TT):
                        ins = pe.transpose(p_turn[:, c, a * P:(a + 1) * P], xn[:, z, a, c * P:(c + 1) * P],
                                           k.ident[:])
                ins.then_inc(turned, 1)

            def body(b, j):
                t = b * BPS + j
                z = j % 2
                if not is_last(b, j):
                    turn(b, j + 1) if j + 1 < BPS else turn(b + 1, 0)
                wait(pe, xt_done, CT * (t + 1))
                for m in range(2 * CT):
                    wait(pe, rest_done, 4 * (t - 1) + m + 1) if not (isinstance(t, int) and t < 1) else None
                    for c in range(CT):
                        ins = pe.matmul(p_qk[:, m], w_qk[:, c, m * P:(m + 1) * P], xt[:, z, c],
                                        start=(c == 0), stop=(c == CT - 1))
                    ins.then_inc(qk_done, 1)
                wait(pe, v_copied, HG * t)
                for a in range(TT):
                    for c in range(CT):
                        ins = pe.matmul(p_v[:, a], xt[:, z, c, a * P:(a + 1) * P], w_v[:, c],
                                        start=(c == 0), stop=(c == CT - 1))
                ins.then_inc(v_done, 1)
            turn(0, 0)
            pe.wait_ge(w_loaded, 3 * 16)
            sequences(pe, body)


def attention_phase(nc, k):
    with ExitStack() as ctx:
        sb = lambda n, s, d=F32: ctx.enter_context(nc.sbuf_tensor(n, s, d))
        ps = lambda n, s, d=F32: ctx.enter_context(nc.psum_tensor(n, s, d))
        sem = lambda n: ctx.enter_context(nc.semaphore(n))
        q_op = [sb(f"q_op{z}", [ROWS, GH, SEQ], BF16) for z in range(2)]
        k_op = [sb(f"k_op{z}", [ROWS, GH, SEQ], BF16) for z in range(2)]
        v_op = [sb(f"v_op{z}", [P, KB, GH, 2 * HD]) for z in range(2)]
        prob = sb("prob", [P, ST.PBUF, 2, BLK])
        part_max = sb("part_max", [P, GH, TT, GROUPS])
        neg_max = sb("neg_max", [P, GH, TT])
        neg_rest = sb("neg_rest", [P, GH, TT])
        shift_cols = sb("shift_cols", [P, P], BF16)
        shift = shift_cols[:, 0:3 * GH * TT].rearrange("p (h a n) -> p h a n", h=GH, a=3)
        shift_row = sb("shift_row", [3 * GH * TT, P], BF16)
        o_t = sb("o_t", [P, BLK])
        inv_sum = sb("inv_sum", [P, TT, GH])
        ctx_out = sb("ctx_out", [P, TT, GH, HD])
        p_s = [ps(f"p_score{i}", [P, 2, BLK]) for i in range(2)]
        p_r = ps("p_ring", [P, ST.RING, BLK])
        p_o = ps("p_out", [P, BLK])
        loaded = [sem(f"b_loaded{z}") for z in range(2)]
        ones_made = sem("b_ones_made")
        values_ready = sem("b_values_ready")
        score_ready = sem("b_score_ready")
        prob_ready = sem("b_prob_ready")
        prob_masked = sem("b_prob_masked")
        round_done = sem("b_round_done")
        bank_ready = sem("b_bank_ready")
        bank_read = sem("b_bank_read")
        max_ready = sem("b_max_ready")
        split_step = sem("b_split_step")
        shift_ready = sem("b_shift_ready")
        shift_turned = sem("b_shift_turned")
        shift_copied = sem("b_shift_copied")
        shift_sent = [sem(f"b_shift_sent{i}") for i in range(2)]
        o_copied = sem("b_o_copied")
        ctx_turned = sem("b_ctx_turned")
        inv_ready = sem("b_inv_ready")
        ctx_ready = sem("b_ctx_ready")
        ctx_stored = sem("b_ctx_stored")
        block = ctx.enter_context(nc.Block())
        N, G = ST.n, GROUPS

        def units(eng, step):
            for s in range(-ST.LEAD, 0):
                step(0, 0, s, False, False)
            for z in range(2):
                for s in range(N):
                    step(z, z, s, z > 0, True)
            with eng.Fori(1, UNITS // 2 - 1) as i:
                for z in range(2):
                    for s in range(N):
                        step(2 * i + z, z, s, True, True)
            for z in range(2):
                for s in range(N):
                    step(UNITS - 2 + z, z, s, True, z == 0)
            for s in range(N, N + 14):
                step(UNITS - 1, 1, s, False, False)

        @block.sync
        def _(sp):
            def load(u, z):
                wait(sp, score_ready, N * (u - 1))
                apart(sp)
                wait(sp, bank_ready, 2 * N * (u - 1))
                apart(sp)
                for i in range(len(Q_PART)):
                    for dst, src, p in ((q_op, k.q_parts, Q_PART[i]), (k_op, k.k_parts, K_PART[i])):
                        sp.dma_start(dst[z][i * HD:(i + 1) * HD, :, :],
                                     src[u // 2, p, z * GH * HD:(z + 1) * GH * HD]
                                     .rearrange("(h r) s -> r h s", r=HD)).then_inc(loaded[z], 16)

            load(0, 0)

            def step(u, z, s, before, after):
                for v, rel in ST.due("load", s, u, False, after):
                    load(v, (z + rel) % 2)
                for v, rel, g in ST.due("shift_send", s, u, before, after):
                    y = (z + rel) % 2
                    wait(sp, shift_copied, G * v + g + 1)
                    apart(sp)
                    for h in range(GH):
                        sp.dma_start(q_op[y][PROD:ROWS, h, g * BLK:(g + 1) * BLK],
                                     shift_row[h * 3 * TT:(h + 1) * 3 * TT, :]).then_inc(shift_sent[g % 2], 16)
                for v, rel, g in ST.due("ctx_store", s, u, before, after):
                    wait(sp, ctx_ready, G * v + g + 1)
                    apart(sp)
                    sp.dma_start(k.ctx[v, g * BLK:(g + 1) * BLK, :].rearrange("(a p) c -> p a c", p=P),
                                 ctx_out[:].rearrange("p a h d -> p a (h d)")).then_inc(ctx_stored, 16)
            units(sp, step)
            sp.wait_ge(ctx_stored, 16 * G * UNITS)

        @block.gpsimd
        def _(pool):
            pool.memset(shift_cols[:], 0.0).then_inc(ones_made, 1)
            made = 1
            for z in range(2):
                for part in (k_op[z][PROD:ROWS], v_op[z][:, :, :, HD:2 * HD]):
                    pool.wait_ge(ones_made, made)
                    pool.memset(part, 1.0).then_inc(ones_made, 1)
                    made += 1

            def values(v, z):
                wait(pool, round_done, ST.rounds * (v - 1))
                apart(pool)
                src = k.v_all[:, v] if isinstance(v, int) else \
                    k.v_all[:, bass.ds(v, 1)].rearrange("p u t d -> p (u t) d")
                pool.tensor_copy(v_op[z][:, :, :, 0:HD], src.rearrange("p t (h d) -> p t h d", h=GH))\
                    .then_inc(values_ready, 1)
            pool.wait_ge(ones_made, 5)
            values(0, 0)

            def mask(i, at, n, stride):
                part = prob[:, i % ST.PBUF, :, :].rearrange("p b n -> p (b n)")
                if n > 1:
                    part = part[:, at:at + n * stride].rearrange("p (n w) -> p n w", n=n)[:, :, 0:P]
                    pattern = [[0, n], [1, P]]
                else:
                    part = part[:, at:at + P]
                    pattern = [[1, P]]
                return pool.affine_select(out=part, in_=part, compare_op=ALU.is_ge, fill=0.0, base=0,
                                          pattern=pattern, channel_multiplier=-1)

            def step(u, z, s, before, after):
                for v, rel in ST.due("values", s, u, False, after):
                    values(v, (z + rel) % 2)
                if 0 <= s < N and ST.tiles[s][0] != "full":
                    kind = ST.tiles[s][0]
                    i = s + N * z
                    wait(pool, prob_ready, N * u + s + 1)
                    apart(pool)
                    if kind == "diag":
                        mask(i, 0, 2, BLK)
                        mask(i, BLK + 3 * P, 1, 0).then_inc(prob_masked, 1)
                    else:
                        mask(i, 0, GH, 2 * P).then_inc(prob_masked, 1)
                for v, rel, g, _ in ST.due("shift_max", s, u, before, after):
                    c = (G * v + g) * 4
                    wait(pool, max_ready, G * v + g + 1)
                    wait(pool, shift_turned, G * v + g)
                    apart(pool)
                    pool.tensor_copy(shift[:, :, 0, :], neg_max[:]).then_inc(split_step, 1)
                    wait(pool, split_step, c + 1)
                    pool.tensor_tensor(neg_rest[:], neg_max[:], shift[:, :, 0, :], ALU.subtract).then_inc(split_step, 1)
                    wait(pool, split_step, c + 2)
                    apart(pool)
                    pool.tensor_copy(shift[:, :, 1, :], neg_rest[:]).then_inc(split_step, 1)
                    wait(pool, split_step, c + 3)
                    pool.tensor_tensor(shift[:, :, 2, :], neg_rest[:], shift[:, :, 1, :], ALU.subtract)\
                        .then_inc(split_step, 1)
            units(pool, step)

        @block.vector
        def _(dve):
            def bank_max(v, j, bank):
                g, pieces = ST.banks[j]
                wait(dve, bank_ready, 2 * N * v + j + 1)
                if len(pieces) == 1:
                    h, qb, key, n, _ = pieces[0]
                    dve.tensor_reduce(part_max[:, h, qb, key // BLK:key // BLK + 1], bank[:, 0:n],
                                      AX.X, ALU.max).then_inc(bank_read, 1)
                elif pieces[0][3] == pieces[1][3]:
                    h = pieces[0][0]
                    dve.tensor_reduce(part_max[:, h:h + 2, 1, g:g + 1], bank.rearrange("p (h n) -> p h n", h=2),
                                      AX.X, ALU.max).then_inc(bank_read, 1)
                else:
                    at = 0
                    for h, qb, key, n, _ in pieces:
                        ins = dve.tensor_reduce(part_max[:, h, qb, g:g + 1], bank[:, at:at + n], AX.X, ALU.max)
                        at += n
                    ins.then_inc(bank_read, 1)

            def copy_shift(v, g, bank):
                wait(dve, shift_turned, G * v + g + 1)
                if not (isinstance(v, int) and (v, g) == (0, 0)):
                    y = (g - 1) % 2
                    wait(dve, shift_sent[y], 16 * GH * ((G // 2) * v + (g + 1 if y == 0 else g) // 2))
                dve.tensor_copy(shift_row[:], bank[0:3 * GH * TT, 0:P // 2].bitcast(BF16)).then_inc(shift_copied, 1)

            def normalise(v, g, bank):
                turned = bank.rearrange("p (a h e) -> p a h e", a=TT, h=GH)
                wait(dve, ctx_turned, G * v + g + 1)
                wait(dve, ctx_ready, G * v + g)
                dve.reciprocal(inv_sum[:], turned[:, :, :, HD]).then_inc(inv_ready, 1)
                wait(dve, inv_ready, G * v + g + 1)
                wait(dve, ctx_stored, 16 * (G * v + g))
                dve.tensor_tensor(ctx_out[:], turned[:, :, :, 0:HD],
                                  inv_sum[:].unsqueeze(3).broadcast_to([P, TT, GH, HD]), ALU.mult)\
                    .then_inc(ctx_ready, 1)

            def step(u, z, s, before, after):
                for v, _, kind, number, at in ST.ring_due(s, u):
                    bank = p_r[:, at % ST.RING]
                    {"bank": bank_max, "shift": copy_shift, "ctx": normalise}[kind](v, number, bank)
                for v, rel, g, nb in ST.due("shift_max", s, u, before, after):
                    wait(dve, bank_read, 2 * N * v + nb)
                    wait(dve, split_step, 4 * (G * v + g))
                    dve.tensor_reduce(neg_max[:], part_max[:, :, :, 0:g + 1], AX.X, ALU.max, negate=True)\
                        .then_inc(max_ready, 1)
                    wait(dve, max_ready, G * v + g + 1)
            units(dve, step)

        @block.scalar
        def _(act):
            def step(u, z, s, before, after):
                if 0 <= s < N:
                    i = s + N * z
                    wait(act, score_ready, N * u + s + 1)
                    if not (isinstance(u, int) and u == 0 and s < ST.PBUF):
                        if s >= ST.PBUF:
                            wait(act, round_done, ST.rounds * u + ST.round_of_tile[s - ST.PBUF])
                        else:
                            wait(act, round_done, ST.rounds * (u - 1) + ST.round_of_tile[s - ST.PBUF + N])
                    act.activation(prob[:, i % ST.PBUF, :, :], p_s[s % 2][:], ACT.Exp, scale=SCALE)\
                        .then_inc(prob_ready, 1)
                for v, rel, g, rounds in ST.due("o_copy", s, u, before, after):
                    wait(act, round_done, ST.rounds * v + rounds)
                    wait(act, ctx_turned, G * v + g)
                    act.activation(o_t[:], p_o[:], ACT.Copy).then_inc(o_copied, 1)
            units(act, step)

        @block.tensor
        def _(pe):
            pe.wait_ge(ones_made, 5)

            def scores_for_max(v, y, j, bank):
                g, pieces = ST.banks[j]
                if j == 0:
                    wait(pe, loaded[y], 16 * 2 * len(Q_PART) * (v // 2 + 1))
                at = 0
                for h, qb, key, n, masked in pieces:
                    q0 = g * BLK + qb * P
                    out = bank[:, at:at + n]
                    last = pe.matmul(out, q_op[y][0:PROD, h, q0:q0 + P], k_op[y][0:PROD, h, key:key + n],
                                     start=True, stop=not masked)
                    if masked:
                        last = pe.matmul(bank[:, at + n - P:at + n], k.ident_b[:], k.causal[:],
                                         start=False, stop=True)
                    at += n
                last.then_inc(bank_ready, 1)

            def scores(u, z, s):
                kind, g, h, kb = ST.tiles[s]
                if ST.first[g] == s:
                    y = g % 2
                    wait(pe, shift_sent[y], 16 * GH * ((G // 2) * u + g // 2 + 1))
                wait(pe, prob_ready, N * u + s - 1)
                out = p_s[s % 2]

                def product(o, h, kb, q0, n):
                    return pe.matmul(o, k_op[z][:, h, kb * P:(kb + 1) * P], q_op[z][:, h, q0:q0 + n],
                                     start=True, stop=True)
                q0 = g * BLK
                if kind == "full":
                    product(out[:, 0], h, kb, q0, BLK)
                    last = product(out[:, 1], h, kb + 1, q0, BLK)
                elif kind == "diag":
                    product(out[:, 0], h, kb, q0, BLK)
                    product(out[:, 1, 0:3 * P], h, kb + 1, q0 + P, 3 * P)
                    last = product(out[:, 1, 3 * P:], h, kb + 3, q0 + 3 * P, P)
                else:
                    for h in range(GH):
                        a = (h % 2) * 2 * P
                        last = product(out[:, h // 2, a:a + 2 * P], h, kb, q0 + 2 * P, 2 * P)
                last.then_inc(score_ready, 1)

            def values_product(v, y, g, kind, kb, half, first, rounds, masked):
                if kb == 0 and half == 0:
                    wait(pe, o_copied, G * v + g)
                    if g == 0:
                        wait(pe, values_ready, v + 1)

                def product(h, kb, q0, slot, bank, at, n, start, stop):
                    return pe.matmul(p_o[32 * h:32 * h + 2 * HD, q0:q0 + n], v_op[y][:, kb, h, :],
                                     prob[:, slot, bank, at:at + n], start=start, stop=stop,
                                     tile_position=(0, 32 * h), skip_group_check=True)
                slot = [(first + N * y + h) % ST.PBUF for h in range(GH)]
                if kind == "corner":
                    wait(pe, prob_masked, ST.masked * v + masked)
                    for h in range(GH):
                        last = product(h, kb, 2 * P, slot[0], h // 2, (h % 2) * 2 * P, 2 * P, False, True)
                    last.then_inc(round_done, 1)
                    return
                if half == 0:
                    if kind == "diag":
                        wait(pe, prob_masked, ST.masked * v + masked)
                    else:
                        wait(pe, prob_ready, N * v + first + GH)
                for h in range(GH):
                    if half == 0:
                        last = product(h, kb, 0, slot[h], 0, 0, BLK, kb == 0, False)
                    elif kind == "full":
                        last = product(h, kb + 1, 0, slot[h], 1, 0, BLK, False, False)
                    else:
                        last = product(h, kb + 1, P, slot[h], 1, 0, 3 * P, False, False)
                if half and kind == "diag":
                    for h in range(GH):
                        last = product(h, kb + 3, 3 * P, slot[h], 1, 3 * P, P, False, False)
                if half:
                    last.then_inc(round_done, 1)

            def turn_ctx(v, y, g, bank):
                wait(pe, o_copied, G * v + g + 1)
                for a in range(TT):
                    last = pe.transpose(bank[:, a * P:(a + 1) * P], o_t[:, a * P:(a + 1) * P], k.ident[:])
                last.then_inc(ctx_turned, 1)

            def turn_shift(v, y, g, bank):
                wait(pe, split_step, 4 * (G * v + g + 1))
                pe.transpose(bank[:, 0:P // 2].bitcast(BF16), shift_cols[:], k.ident_b[:]).then_inc(shift_turned, 1)

            def into_ring(v, rel, z, kind, number, at):
                earlier = ST.before(at, v)
                if earlier:
                    owner, was, n = earlier
                    if was == "bank":
                        wait(pe, bank_read, 2 * N * owner + n + 1)
                    else:
                        wait(pe, {"shift": shift_copied, "ctx": ctx_ready}[was], G * owner + n + 1)
                bank = p_r[:, at % ST.RING]
                {"bank": scores_for_max, "shift": turn_shift, "ctx": turn_ctx}[kind](v, (z + rel) % 2, number, bank)

            def step(u, z, s, before, after):
                if 0 <= s < N:
                    scores(u, z, s)
                entries = list(ST.ring_due(s, u))
                for v, rel, *entry in entries[:1]:
                    into_ring(v, rel, z, *entry)
                for v, rel, *what in ST.due("pv", s, u, before, after):
                    values_product(v, (z + rel) % 2, *what)
                for v, rel, *entry in entries[1:]:
                    into_ring(v, rel, z, *entry)
            units(pe, step)


def block_pass(nc, k, w, first):
    name = "d" if first else "e"
    with ExitStack() as ctx:
        sb = lambda n, s, d=F32: ctx.enter_context(nc.sbuf_tensor(f"{name}_{n}", s, d))
        ps = lambda n, s, d=F32: ctx.enter_context(nc.psum_tensor(f"{name}_{n}", s, d))
        sem = lambda n: ctx.enter_context(nc.semaphore(f"{name}_{n}"))
        x_in = sb("x_in", [P, 2, TT, D])
        side = sb("side", [P, 2, TT, D])
        a_t = sb("a_t", [P, CT, BLK])
        state = sb("state", [P, CT, 1 + BLK])
        diff = sb("diff", [P, CT, BLK])
        v_in = sb("v_in", [P, CT, BLK])
        r_in = sb("r_in", [P, CT, BLK])
        gate = sb("gate", [P, TT, D])
        x_mid = sb("x_mid", [P, 2, TT, D])
        x_bias = sb("x_bias", [P, 2, TT, D])
        xn = sb("xn", [P, TT, D])
        x_t = sb("x_t", [P, CT, BLK])
        hidden = sb("hidden", [P, HT, BLK])
        stats = sb("stats", [P, 2, TT, 6])
        mean_var = sb("mean_var", [P, 2, TT, 2])
        var_eps = sb("var_eps", [P, 2, TT])
        rstd = sb("rstd", [P, 2, TT])
        p_turn = ps("turn", [P, CT, BLK])
        p_h = ps("h", [P, 2, BLK])
        p_y = ps("y", [P, TT, D])
        p_w = ps("w", [P, TT, D])
        x_loaded = [sem(f"x_loaded{i}") for i in range(2)]
        biased = sem("biased")
        turn_a = sem("turn_a")
        copied_a = sem("copied_a")
        turn_b = sem("turn_b")
        copied_b = sem("copied_b")
        h_ready = sem("h_ready")
        h_done = sem("h_done")
        r_ready = sem("r_ready")
        gate_done = sem("gate_done")
        w_ready = sem("w_ready")
        w_read = sem("w_read")
        mid_ready = sem("mid_ready")
        bias_done = sem("bias_done")
        y_ready = sem("y_ready")
        x_ready = sem("x_ready")
        stat_step = [sem(f"stat_step{i}") for i in range(2)]
        stats_done = [sem(f"stats_done{i}") for i in range(2)]
        eps_added = [sem(f"eps_added{i}") for i in range(2)]
        rstd_done = [sem(f"rstd_done{i}") for i in range(2)]
        xn_done = [sem(f"xn_done{i}") for i in range(2)]
        carried = sem("carried")
        summed = sem("summed")
        diffed = sem("diffed")
        mixed = sem("mixed")
        stored = [sem(f"stored{i}") for i in range(2)]
        block = ctx.enter_context(nc.Block())
        tiles = "b (n j p) c -> (b n) p j c"
        x_tiles = w.x.rearrange(tiles, n=BPS, p=P)
        out_tiles = w.out.rearrange(tiles, n=BPS, p=P)
        LAST = (BATCH - 1, BPS - 1)

        def sequences(eng, body):
            for j in range(BPS):
                body(0, j)
            with eng.Fori(1, BATCH - 1) as b:
                for j in range(BPS):
                    body(b, j)
            for j in range(BPS):
                body(BATCH - 1, j)

        def following(b, j):
            if isinstance(b, int) and (b, j) == LAST:
                return None
            return (b, j + 1) if j + 1 < BPS else (b + 1, 0)

        def resident(t):
            if isinstance(t, int):
                return k.x_all[:, t]
            return k.x_all[:, bass.ds(t, 1)].rearrange("p u a n -> p (u a) n")

        @block.sync
        def _(sp):
            def load(b, j):
                t = b * BPS + j
                z = j % 2
                wait(sp, w_read, t - 1)
                apart(sp)
                sp.dma_start(x_in[:, z], x_tiles[t]).then_inc(x_loaded[z], 16)
                wait(sp, turn_a, t - 1)
                apart(sp)
                for g in range(HG):
                    sp.dma_start(side[:, z, :, g * GH * HD:(g + 1) * GH * HD],
                                 k.ctx[b * HG + g, j * BLK:(j + 1) * BLK, :].rearrange("(a p) c -> p a c", p=P))\
                        .then_inc(x_loaded[z], 16)

            def store(b, j):
                t = b * BPS + j
                z = j % 2
                wait(sp, x_ready, t + 1)
                apart(sp)
                sp.dma_start(out_tiles[t], side[:, z]).then_inc(stored[z], 16)

            if first:
                sequences(sp, load)
            else:
                sequences(sp, store)
                for z in range(2):
                    sp.wait_ge(stored[z], 16 * NBLK // 2)

        @block.gpsimd
        def _(pool):
            def inverse_std(i, t):
                wait(pool, stats_done[i], TT * (t + 1))
                apart(pool)
                pool.tensor_scalar(var_eps[:, i], mean_var[:, i, :, 1], EPS, None, ALU.add).then_inc(eps_added[i], 1)
                wait(pool, eps_added[i], t + 1)
                pool.tensor_tensor(rstd[:, i], var_eps[:, i], k.minus_half[:], ALU.pow).then_inc(rstd_done[i], 1)

            def body(b, j):
                t = b * BPS + j
                z = j % 2
                if first:
                    wait(pool, x_loaded[z], 16 * (1 + HG) * (b * (BPS // 2) + j // 2 + 1))
                    for a in range(TT):
                        ins = pool.tensor_tensor(x_in[:, z, a], x_in[:, z, a], k.row_bias[:, 0], ALU.add)
                    ins.then_inc(biased, 1)
                else:
                    inverse_std(0, t)
                inverse_std(1, t)
                wait(pool, x_ready, t - 1)
                for a in range(TT):
                    ins = pool.tensor_tensor(x_bias[:, z, a], x_mid[:, z, a], k.row_bias[:, 1], ALU.add)
                ins.then_inc(bias_done, 1)
            sequences(pool, body)

        @block.vector
        def _(dve):
            def norm(i, x, out, t, out_free, out_value):
                for a in range(TT):
                    dve.bn_stats(stats[:, i, a], x[:, a]).then_inc(stat_step[i], 1)
                wait(dve, stat_step[i], TT * (t + 1))
                wait(dve, rstd_done[i], t)
                apart(dve)
                for a in range(TT):
                    dve.bn_aggr(mean_var[:, i, a], stats[:, i, a]).then_inc(stats_done[i], 1)
                wait(dve, stats_done[i], TT * (t + 1))
                wait(dve, rstd_done[i], t + 1)
                wait(dve, out_free, out_value)
                for a in range(TT):
                    ins = dve.tensor_scalar(out[:, a], x[:, a], mean_var[:, i, a, 0:1], rstd[:, i, a:a + 1],
                                            ALU.subtract, ALU.mult)
                ins.then_inc(xn_done[i], 1)

            def decay_sum(b, j):
                t = b * BPS + j
                wait(dve, copied_a, t + 1)
                if j == 0:
                    dve.memset(state[:, :, 0:1], 0.0).then_inc(carried, 1)
                else:
                    dve.tensor_copy(state[:, :, 0:1], state[:, :, BLK:BLK + 1]).then_inc(carried, 1)
                wait(dve, carried, t + 1)
                for c in range(CT):
                    dve.tensor_tensor_scan(state[:, c, 1:BLK + 1], k.channel[:, 4, c:c + 1].broadcast_to([P, BLK]),
                                           a_t[:, c], state[:, c, 0:1], ALU.mult, ALU.add).then_inc(summed, 1)
                wait(dve, summed, CT * (t + 1))
                for c in range(CT):
                    dve.tensor_tensor(diff[:, c], a_t[:, c], state[:, c, 0:BLK], ALU.subtract).then_inc(diffed, 1)
                wait(dve, diffed, CT * (t + 1))
                wait(dve, w_ready, t)
                for c in range(CT):
                    for m, out in ((2, r_in), (1, v_in)):
                        ins = dve.scalar_tensor_tensor(out[:, c], diff[:, c], k.channel[:, m, c:c + 1],
                                                       state[:, c, 0:BLK], ALU.mult, ALU.add)
                ins.then_inc(mixed, 1)

            def front(b, j):
                t = b * BPS + j
                z = j % 2
                wait(dve, w_ready, t + 1)
                wait(dve, bias_done, t - 1)
                if first:
                    wait(dve, biased, t + 1)
                    for a in range(2):
                        ins = dve.tensor_tensor(x_mid[:, z, 2 * a:2 * a + 2], p_w[:, 2 * a:2 * a + 2],
                                                x_in[:, z, 2 * a:2 * a + 2], ALU.add)
                    ins.then_inc(w_read, 1)
                else:
                    wait(dve, gate_done, t + 1)
                    for a in range(2):
                        ins = dve.tensor_tensor(diff[:].rearrange("p c n -> p (c n)")[:, a * BLK:(a + 1) * BLK],
                                                p_w[:, 2 * a:2 * a + 2].rearrange("p a n -> p (a n)"),
                                                gate[:, 2 * a:2 * a + 2].rearrange("p a n -> p (a n)"), ALU.mult)
                    ins.then_inc(w_read, 1)
                    wait(dve, w_read, t + 1)
                    ins = dve.tensor_tensor(x_mid[:, z], diff[:].rearrange("p c n -> p (c n)")
                                            .rearrange("p (a n) -> p a n", a=TT), resident(t), ALU.add)
                ins.then_inc(mid_ready, 1) if not first else None
                if first:
                    wait(dve, w_read, t + 1)
                else:
                    wait(dve, mid_ready, t + 1)
                norm(1, x_mid[:, z], xn, t, turn_b, t)

            def norm_front(b, j):
                if not first:
                    t = b * BPS + j
                    norm(0, resident(t), x_in[:, j % 2], t, turn_a, t - 1)

            def back(b, j):
                t = b * BPS + j
                z = j % 2
                wait(dve, y_ready, t + 1)
                wait(dve, bias_done, t + 1)
                if not first and not (isinstance(t, int) and t < 2):
                    wait(dve, stored[z], 16 * (b * (BPS // 2) + j // 2))
                out = resident(t) if first else side[:, z]
                for a in range(2):
                    ins = dve.tensor_tensor(out[:, 2 * a:2 * a + 2], p_y[:, 2 * a:2 * a + 2],
                                            x_bias[:, z, 2 * a:2 * a + 2], ALU.add)
                ins.then_inc(x_ready, 1)

            norm_front(0, 0)
            if not first:
                decay_sum(0, 0)
            front(0, 0)
            if not first:
                norm_front(0, 1)

            def body(b, j):
                after = following(b, j)
                if after:
                    if not first:
                        decay_sum(*after)
                    front(*after)
                    if not first and following(*after):
                        norm_front(*following(*after))
                back(b, j)
            sequences(dve, body)

        @block.scalar
        def _(act):
            def copy_a(b, j):
                t = b * BPS + j
                wait(act, turn_a, t + 1)
                if first:
                    wait(act, w_ready, t)
                else:
                    wait(act, diffed, CT * t)
                for c in range(CT):
                    ins = act.activation(a_t[:, c], p_turn[:, c], ACT.Copy)
                ins.then_inc(copied_a, 1)

            def copy_b(b, j):
                t = b * BPS + j
                wait(act, turn_b, t + 1)
                wait(act, h_ready, HT * t)
                for c in range(CT):
                    ins = act.activation(x_t[:, c], p_turn[:, c], ACT.Copy)
                ins.then_inc(copied_b, 1)

            def gate_of(b, j):
                if not first:
                    t = b * BPS + j
                    wait(act, r_ready, t + 1)
                    wait(act, w_read, t)
                    for a in range(2):
                        ins = act.activation(gate[:, 2 * a:2 * a + 2], p_w[:, 2 * a:2 * a + 2], ACT.Sigmoid)
                    ins.then_inc(gate_done, 1)

            def gelus(b, j, lo, hi):
                t = b * BPS + j
                for m in range(lo, hi):
                    wait(act, h_ready, HT * t + m + 1)
                    act.activation(hidden[:, m], p_h[:, m % 2], ACT.Gelu, bias=k.hidden_bias[:, m:m + 1])\
                        .then_inc(h_done, 1)

            copy_a(0, 0)
            gate_of(0, 0)
            copy_b(0, 0)

            def body(b, j):
                after = following(b, j)
                gelus(b, j, 0, 2)
                if after:
                    copy_a(*after)
                gelus(b, j, 2, 6)
                if after:
                    gate_of(*after)
                gelus(b, j, 6, HT)
                if after:
                    copy_b(*after)
            sequences(act, body)

        @block.tensor
        def _(pe):
            def turns_a(b, j):
                t = b * BPS + j
                z = j % 2
                if first:
                    wait(pe, x_loaded[z], 16 * (1 + HG) * (b * (BPS // 2) + j // 2 + 1))
                else:
                    wait(pe, xn_done[0], t + 1)
                wait(pe, copied_b, t)
                source = side if first else x_in
                for c in range(CT):
                    for a in range(TT):
                        ins = pe.transpose(p_turn[:, c, a * P:(a + 1) * P], source[:, z, a, c * P:(c + 1) * P],
                                           k.ident[:])
                ins.then_inc(turn_a, 1)

            def turns_b(b, j):
                t = b * BPS + j
                wait(pe, xn_done[1], t + 1)
                wait(pe, copied_a, t + 1)
                for c in range(CT):
                    for a in range(TT):
                        ins = pe.transpose(p_turn[:, c, a * P:(a + 1) * P], xn[:, a, c * P:(c + 1) * P], k.ident[:])
                ins.then_inc(turn_b, 1)

            def rows_product(out, left, right):
                for a in range(TT):
                    for c in range(CT):
                        ins = pe.matmul(out[:, a], left[:, c, a * P:(a + 1) * P], right[:, c],
                                        start=(c == 0), stop=(c == CT - 1))
                return ins

            def gate_product(b, j):
                if not first:
                    t = b * BPS + j
                    wait(pe, mixed, t + 1)
                    wait(pe, w_read, t)
                    rows_product(p_w, r_in, k.w_r).then_inc(r_ready, 1)

            def layer_product(b, j):
                t = b * BPS + j
                if first:
                    wait(pe, copied_a, t + 1)
                    wait(pe, w_read, t)
                    rows_product(p_w, a_t, k.w_o).then_inc(w_ready, 1)
                else:
                    wait(pe, gate_done, t + 1)
                    rows_product(p_w, v_in, k.w_vo).then_inc(w_ready, 1)

            def up(b, j, lo, hi):
                t = b * BPS + j
                if lo == 0:
                    wait(pe, copied_b, t + 1)
                for m in range(lo, hi):
                    wait(pe, h_done, HT * t + m - 1)
                    for c in range(CT):
                        ins = pe.matmul(p_h[:, m % 2], k.up_matrix[:, c, m * P:(m + 1) * P], x_t[:, c],
                                        start=(c == 0), stop=(c == CT - 1))
                    ins.then_inc(h_ready, 1)

            def down(b, j, lo, hi):
                t = b * BPS + j
                if lo == 0:
                    wait(pe, h_done, HT * (t + 1))
                    wait(pe, x_ready, t)
                for a in range(lo, hi):
                    for m in range(HT):
                        ins = pe.matmul(p_y[:, a], hidden[:, m, a * P:(a + 1) * P], k.down_matrix[:, m],
                                        start=(m == 0), stop=(m == HT - 1))
                if hi == TT:
                    ins.then_inc(y_ready, 1)

            turns_a(0, 0)
            gate_product(0, 0)
            layer_product(0, 0)
            turns_b(0, 0)

            def body(b, j):
                after = following(b, j)
                up(b, j, 0, 2)
                if after:
                    turns_a(*after)
                up(b, j, 2, 6)
                if after:
                    gate_product(*after)
                up(b, j, 6, HT)
                if after:
                    layer_product(*after)
                down(b, j, 0, 2)
                if after:
                    turns_b(*after)
                down(b, j, 2, TT)
            sequences(pe, body)


def hybrid_block(nc, w):
    k = Shared()
    k.q_parts = nc.dram_tensor("q_parts", (UNITS // 2, 3, P, SEQ), BF16, kind="Internal").ap()
    k.k_parts = nc.dram_tensor("k_parts", (UNITS // 2, 3, P, SEQ), BF16, kind="Internal").ap()
    k.ctx = nc.dram_tensor("ctx", (UNITS, SEQ, GH * HD), F32, kind="Internal").ap()
    with ExitStack() as ctx:
        sb = lambda n, s, d=F32: ctx.enter_context(nc.sbuf_tensor(n, s, d))
        k.ident = sb("ident", [P, P])
        k.ident_b = sb("ident_b", [P, P], BF16)
        k.causal = sb("causal", [P, P], BF16)
        k.minus_half = sb("minus_half", [P, TT])
        k.row_bias = sb("row_bias", [P, 2, D])
        k.hidden_bias = sb("hidden_bias", [P, HT])
        k.channel = sb("channel", [P, 5, CT])
        k.w_o = sb("w_o", [P, CT, D])
        k.w_r = sb("w_r", [P, CT, D])
        k.w_vo = sb("w_vo", [P, CT, D])
        k.up_matrix = sb("up_matrix", [P, CT, HID])
        k.down_matrix = sb("down_matrix", [P, HT, D])
        k.setup_done = ctx.enter_context(nc.semaphore("setup_done"))
        consts_phase(nc, k, w)
        with nc.sbuf_tensor("v_all", [P, UNITS, KB, GH * HD], F32) as v_all:
            k.v_all = v_all
            project_phase(nc, k, w)
            attention_phase(nc, k)
        with nc.sbuf_tensor("x_all", [P, NBLK, TT, D], F32) as x_all:
            k.x_all = x_all
            block_pass(nc, k, w, True)
            block_pass(nc, k, w, False)


_INS = {"L0_attn_a_x": "x", "L0_attn_a_W_q": "W_q", "L0_attn_a_W_k": "W_k", "L0_attn_a_W_v": "W_v",
        "L0_attn_a_W_o": "W_o", "L0_attn_a_b_o": "b_o", "L0_attn_b_time_decay": "time_decay",
        "L0_attn_b_time_mix_k": "time_mix_k", "L0_attn_b_time_mix_v": "time_mix_v",
        "L0_attn_b_time_mix_r": "time_mix_r", "L0_attn_b_Wk": "Wk", "L0_attn_b_Wv": "Wv",
        "L0_attn_b_Wr": "Wr", "L0_attn_b_Wo": "Wo", "L0_ffn_W_exp": "W_exp", "L0_ffn_b_exp": "b_exp",
        "L0_ffn_up_weights": "up_weights", "L0_ffn_up_bias": "up_bias",
        "L0_ffn_down_weights": "down_weights", "L0_ffn_W_con": "W_con", "L0_ffn_b_con": "b_con",
        "L0_ffn_down_bias": "down_bias"}


def kernel(**inputs):
    from types import SimpleNamespace

    import numpy as _np
    import concourse.bacc as _bacc
    from concourse import mybir as _mybir
    from concourse.bass_utils import run_bass_kernel_spmd as _run

    nc = _bacc.Bacc("TRN2", target_bir_lowering=False, num_devices=1)
    arrays, args = {}, {}
    for name, short in _INS.items():
        a = _np.ascontiguousarray(inputs[name])
        arrays[f"in_{name}"] = a
        args[short] = nc.dram_tensor(f"in_{name}", a.shape, _mybir.dt.from_np(a.dtype), kind="ExternalInput").ap()
    out = nc.dram_tensor("out_0", (BATCH, SEQ, D), _mybir.dt.float32, kind="ExternalOutput").ap()
    hybrid_block(nc, SimpleNamespace(out=out, **args))
    r = _run(nc, [arrays], core_ids=[0])
    return r.results[0]["out_0"]
```

```python
from contextlib import ExitStack

import concourse.bass as bass
from concourse import mybir

F32 = mybir.dt.float32
BF16 = mybir.dt.bfloat16
F32R = mybir.dt.float32r
ALU = mybir.AluOpType
ACT = mybir.ActivationFunctionType
AX = mybir.AxisListType

P = 128
BATCH, SEQ, D = 4, 2048, 256
HEADS, HD = 16, 16
HID = 1024
STAGES = 10
CT = D // P
HT = HID // P
BLK = 512
TT = BLK // P
BPS = SEQ // BLK
NBLK = BATCH * BPS
EPS = 1e-5

GH = 4
HG = HEADS // GH
UNITS = BATCH * HG
KB = SEQ // P
GROUPS = SEQ // BLK
SCALE = float(HD) ** -0.5
NEG = -1e30
LOWEST = -3e38
Q_PART = [0, 0, 1, 1, 0, 2]
K_PART = [0, 1, 0, 1, 2, 0]
PROD = HD * len(Q_PART)
ROWS = PROD + 3
HALVES = ((0, 0), (0, 1), (1, 0))


class Steps:

    LEAD = 38
    RING = 3
    PBUF = 8

    def __init__(self):
        self.tiles = []
        self.plan = {}
        self.round_of_tile = []
        self.first = {}
        rounds = 0
        masked = 0
        self.masked_before = []
        for g in range(GROUPS):
            self.first[g] = len(self.tiles)
            for r in range(2 * g + 1):
                kind = "full" if r < 2 * g else "diag"
                for h in range(GH):
                    self.tiles.append((kind, g, h, 2 * r))
                    self.round_of_tile.append(rounds + 1)
                    self.masked_before.append(masked)
                    masked += kind == "diag"
                last = len(self.tiles) - 1
                late = 2 + (kind == "diag")
                for half in range(2):
                    self.add("pv", last + late + half, (g, kind, 2 * r, half, last - GH + 1, rounds, masked))
                rounds += 1
            self.tiles.append(("corner", g, 0, 4 * g + 2))
            self.masked_before.append(masked)
            masked += 1
            self.round_of_tile.append(rounds + 1)
            c = len(self.tiles) - 1
            self.add("pv", c + 3, (g, "corner", 4 * g + 2, 0, c, rounds, masked))
            rounds += 1
            self.add("o_copy", c + 4, (g, rounds))
            self.add("ctx_turn", c + 6, (g,))
            self.add("ctx_store", c + 7, (g,))
        self.n = len(self.tiles)
        self.rounds = rounds
        self.masked = masked
        self.banks = []
        for g in range(GROUPS):
            for h in range(GH):
                for qb in range(TT):
                    for j in range(g):
                        self.banks.append((g, [(h, qb, j * BLK, BLK, False)]))
            for h in range(GH):
                self.banks.append((g, [(h, 3, g * BLK, 4 * P, True)]))
            for h in range(GH):
                self.banks.append((g, [(h, 2, g * BLK, 3 * P, True), (h, 0, g * BLK, P, True)]))
            for h in range(0, GH, 2):
                self.banks.append((g, [(h, 1, g * BLK, 2 * P, True), (h + 1, 1, g * BLK, 2 * P, True)]))
            assert len(self.banks) % 2 == 0
            s = len(self.banks) // 2 - 1 - self.LEAD
            self.add("shift_max", s, (g, len(self.banks)))
            self.add("shift_turn", s + 3, (g,))
            self.add("shift_send", s + 4, (g,))
            assert s + 6 < self.first[g]
        assert len(self.banks) == 2 * self.n and self.n % 4 == 0
        self.add("load", 3 - self.n, ())
        self.add("values", 3 - self.n, ())
        self.ring = []
        self.ring_of_step = []
        for s in range(self.n):
            banks = [(v, "bank", j) for v, _, j in self.banks_due(s, 0)]
            turns = [(v, kind[:-5], g) for kind in ("ctx_turn", "shift_turn")
                     for v, _, g in self.due(kind, s, 0)]
            self.ring_of_step.append(len(self.ring))
            self.ring += [banks[0]] + turns + [banks[1]]
        assert len(self.ring) % self.RING == 0

    def add(self, kind, step, what):
        self.plan.setdefault(kind, []).append((step, what))

    def due(self, kind, step, u, before=True, after=True):
        for rel in (-1, 0, 1):
            if (rel < 0 and not before) or (rel > 0 and not after):
                continue
            for s, what in self.plan[kind]:
                if s == step - rel * self.n:
                    yield (u + rel, rel) + what

    def ring_due(self, step, u):
        s = step % self.n
        end = (self.ring_of_step + [len(self.ring)])[s + 1]
        for at in range(self.ring_of_step[s], end):
            rel, kind, number = self.ring[at]
            v = u + rel + step // self.n
            if not isinstance(v, int) or 0 <= v < UNITS:
                yield v, rel + step // self.n, kind, number, at

    def before(self, at, v):
        rel = self.ring[at][0]
        for back in range(self.RING, 4 * self.RING):
            lap, place = divmod(at - back, len(self.ring))
            other, kind, number = self.ring[place]
            owner = v - rel + other + lap
            if not isinstance(owner, int) or 0 <= owner < UNITS:
                return owner, kind, number
            if isinstance(owner, int) and owner < 0 and kind == "bank":
                return None
        return None

    def banks_due(self, step, u, after=True):
        j = step + self.LEAD
        if j < self.n:
            yield from ((u, 0, 2 * j), (u, 0, 2 * j + 1))
        elif after:
            yield from ((u + 1, 1, 2 * (j - self.n)), (u + 1, 1, 2 * (j - self.n) + 1))


ST = Steps()


def wait(eng, sem, value):
    if isinstance(value, int) and value <= 0:
        return
    eng.wait_ge(sem, value)


def apart(eng):
    eng.nop(nofuse=True)


class Shared:
    pass


LOW = 7
HIGH = STAGES - LOW


def consts_phase(nc, k, w):
    with ExitStack() as ctx:
        sb = lambda n, s, d=F32: ctx.enter_context(nc.sbuf_tensor(n, s, d))
        ps = lambda n, s, d=F32: ctx.enter_context(nc.psum_tensor(n, s, d))
        sem = lambda n: ctx.enter_context(nc.semaphore(n))
        row = sb("butterfly_row", [1, 2, 2 * HID])
        up_w = sb("up_stage", [P, 2, 2 * HID])
        down_w = sb("down_stage", [P, LOW, 2 * HID])
        high_w = sb("high_weights", [P, 2, HIGH, HT // 2, 4])
        low = [sb(f"low{i}", [P, HID]) for i in range(2)]
        low_up = sb("low_up", [P, HID])
        low_down = sb("low_down", [P, HID])
        product = sb("product", [P, 2, HID])
        exp_rows = sb("exp_rows", [P, CT, HID])
        exp_cols = sb("exp_cols", [P, HT, D + 1])
        up_x = [sb(f"up_x{i}", [P, HT, D + 1]) for i in range(2)]
        down_x = [sb(f"down_x{i}", [P, HT, D + 1]) for i in range(2)]
        scaled = sb("scaled", [P, HT, D + 1])
        up_bias = sb("up_bias_cols", [P, HT])
        square = sb("square_weights", [P, 3, CT, D])
        wo_t = sb("wo_turned", [P, CT, D])
        rows = sb("bias_rows", [1, 3, D])
        up_matrix = sb("up_matrix", [P, CT, HID])
        down_matrix = sb("down_matrix", [P, HT, D])
        bank = ps("c_bank", [P, 8, 512])
        con_loaded = sem("c_con_loaded")
        exp_loaded = sem("c_exp_loaded")
        square_loaded = sem("c_square_loaded")
        rows_loaded = sem("c_rows_loaded")
        small_loaded = sem("c_small_loaded")
        row_loaded = [sem(f"c_row_loaded{i}") for i in range(2)]
        down_loaded = [sem(f"c_down_loaded{i}") for i in range(LOW)]
        spread = sem("c_spread")
        ident_step = sem("c_ident_step")
        made = sem("c_made")
        rows_added = sem("c_rows_added")
        low_step = sem("c_low_step")
        low_stage = sem("c_low_stage")
        low_begun = sem("c_low_begun")
        high_scaled = sem("c_high_scaled")
        high_done = sem("c_high_done")
        turned = sem("c_turned")
        exp_copied = sem("c_exp_copied")
        square_copied = sem("c_square_copied")
        composed = sem("c_composed")
        vo_copied = sem("c_vo_copied")
        applied = sem("c_applied")
        up_copied = sem("c_up_copied")
        down_applied = sem("c_down_applied")
        down_copied = sem("c_down_copied")
        bias_ready = sem("c_bias_ready")
        up_turned = sem("c_up_turned")
        matrix_copied = sem("c_matrix_copied")
        matrix_stored = sem("c_matrix_stored")
        block = ctx.enter_context(nc.Block())
        PAIRS = HT // 2
        HIGH_OPS = HIGH * PAIRS * 2

        def pair(stage, n):
            s = 2 ** (stage - LOW)
            a = (n // s) * 2 * s + n % s
            return a, a + s

        @block.sync
        def _(sp):
            for n in range(LOW):
                if n >= 2:
                    sp.wait_ge(spread, n - 1)
                sp.dma_start(row[:, n % 2], w.up_weights[n].rearrange("(o k) r c -> o (k r c)", o=1))\
                    .then_inc(row_loaded[n % 2], 16)
            for i, m in enumerate((w.b_o, w.b_con, w.down_bias)):
                sp.dma_start(rows[:, i], m.rearrange("(o n) -> o n", o=1)).then_inc(rows_loaded, 16)
            sp.dma_start(k.w_o[:], w.W_o.rearrange("(t p) n -> p t n", p=P)).then_inc(small_loaded, 16)
            for i, m in enumerate((w.time_decay, w.time_mix_v, w.time_mix_r)):
                sp.dma_start(k.channel[:, i, :], m.rearrange("(t p) -> p t", p=P),
                             allow_slow_non_contiguous=True).then_inc(small_loaded, 16)
            sp.dma_start(up_bias[:], w.up_bias.rearrange("(t p) -> p t", p=P),
                         allow_slow_non_contiguous=True).then_inc(small_loaded, 16)
            sp.wait_ge(small_loaded, 5 * 16)
            for t in range(4):
                sp.wait_ge(down_copied, t + 1)
                sp.dma_start(k.down_dram[:, 2 * t:2 * t + 2], down_matrix[:, 2 * t:2 * t + 2]).then_inc(matrix_stored, 16)
            for c in range(CT):
                sp.wait_ge(matrix_copied, c + 1)
                sp.dma_start(k.up_dram[:, c], up_matrix[:, c]).then_inc(matrix_stored, 16)
            sp.wait_ge(matrix_stored, 16 * (4 + CT))

        @block.gpsimd
        def _(pool):
            pool.memset(k.ident[:], 0.0).then_inc(ident_step, 1)
            pool.wait_ge(ident_step, 1)
            pool.affine_select(out=k.ident[:], in_=k.ident[:], compare_op=ALU.not_equal, fill=1.0, base=0,
                               pattern=[[-1, P]], channel_multiplier=1).then_inc(ident_step, 1)
            for n in range(LOW):
                if n >= 2:
                    pool.wait_ge(low_stage, n - 1)
                pool.wait_ge(row_loaded[n % 2], 16 * (n // 2 + 1))
                pool.partition_broadcast(up_w[:, n % 2], row[:, n % 2]).then_inc(spread, 1)
            pool.wait_ge(ident_step, 2)
            pool.tensor_copy(k.ident_b[:], k.ident[:]).then_inc(made, 1)
            pool.memset(k.minus_half[:], -0.5).then_inc(made, 1)
            pool.wait_ge(rows_loaded, 3 * 16)
            pool.tensor_tensor(rows[:, 1], rows[:, 1], rows[:, 2], ALU.add).then_inc(rows_added, 1)
            pool.wait_ge(rows_added, 1)
            pool.partition_broadcast(k.row_bias[:, 0, :], rows[:, 0]).then_inc(made, 1)
            pool.partition_broadcast(k.row_bias[:, 1, :], rows[:, 1]).then_inc(made, 1)
            pool.wait_ge(made, 4)

        @block.vector
        def _(dve):
            count = [0]

            def high_stages(which, x, stages, base):
                for m, stage in enumerate(stages):
                    src, dst = x[m % 2], x[(m + 1) % 2]
                    for n in range(PAIRS):
                        a, b = pair(stage, n)
                        for r, out in enumerate((a, b)):
                            rc = 2 * r + 1 if which == 0 else 2 + r
                            wide = D + 1 if which == 0 else D
                            dve.wait_ge(high_scaled, base + (m * PAIRS + n) * 2 + r + 1)
                            dve.scalar_tensor_tensor(
                                dst[:, out, 0:wide], src[:, b, 0:wide],
                                high_w[:, which, stage - LOW, n, rc:rc + 1], scaled[:, 2 * n + r, 0:wide],
                                ALU.mult, ALU.add).then_inc(high_done, 1)
                    dve.wait_ge(high_done, base + (m + 1) * PAIRS * 2)

            def low_stages(which, out):
                for t in range(HT):
                    ins = dve.tensor_copy(low[0][:, t * P:(t + 1) * P], k.ident[:])
                ins.then_inc(low_begun, 1)
                dve.wait_ge(low_begun, which + 1)
                for m in range(LOW):
                    stage = m if which == 0 else LOW - 1 - m
                    s = 2 ** stage
                    src = low[m % 2]
                    dst = low[(m + 1) % 2] if m < LOW - 1 else out
                    if which == 0:
                        dve.wait_ge(spread, m + 1)
                        weights = up_w[:, m % 2]
                    else:
                        dve.wait_ge(down_loaded[stage], 16)
                        weights = down_w[:, stage]
                    weights = weights.rearrange("p (b s r c) -> p r c b s", s=s, r=2, c=2)
                    v = src[:].rearrange("p (b c s) -> p c b s", c=2, s=s)
                    o = dst[:].rearrange("p (b r s) -> p r b s", r=2, s=s)
                    shape = [P, 2, HID // 2 // s, s]
                    for c in range(2):
                        part = weights[:, :, c] if which == 0 else weights[:, c]
                        half = v[:, c].unsqueeze(1).broadcast_to(shape)
                        dve.tensor_tensor(product[:, c].rearrange("p (r b s) -> p r b s", r=2, s=s), part, half,
                                          ALU.mult).then_inc(low_step, 1)
                        count[0] += 1
                    dve.wait_ge(low_step, count[0])
                    dve.tensor_tensor(o, product[:, 0].rearrange("p (r b s) -> p r b s", r=2, s=s),
                                      product[:, 1].rearrange("p (r b s) -> p r b s", r=2, s=s),
                                      ALU.add).then_inc(low_stage, 1)
                    dve.wait_ge(low_stage, which * LOW + m + 1)

            dve.wait_ge(ident_step, 2)
            low_stages(0, low_up)
            high_stages(1, down_x, range(STAGES - 1, LOW - 1, -1), 0)
            low_stages(1, low_down)
            dve.wait_ge(small_loaded, 5 * 16)
            high_stages(0, up_x, range(LOW, STAGES), HIGH_OPS)
            dve.tensor_tensor(k.hidden_bias[:], up_x[HIGH % 2][:, :, D], up_bias[:], ALU.add).then_inc(bias_ready, 1)
            dve.wait_ge(bias_ready, 1)

        @block.scalar
        def _(act):
            act.wait_ge(spread, 2)
            act.dma_start(exp_rows[:], w.W_exp.rearrange("(t p) n -> p t n", p=P)).then_inc(exp_loaded, 16)
            act.dma_start(exp_cols[:, :, D], w.b_exp.rearrange("(t p) -> p t", p=P),
                          allow_slow_non_contiguous=True).then_inc(exp_loaded, 16)
            act.wait_ge(spread, 3)
            act.dma_start(down_x[0][:, :, 0:D], w.W_con.rearrange("(t p) n -> p t n", p=P)).then_inc(con_loaded, 16)
            act.wait_ge(spread, 4)
            for i, m in enumerate((w.up_weights, w.down_weights)):
                for s in range(HIGH):
                    act.dma_start(high_w[:, i, s], m[LOW + s].rearrange("(n p) r c -> p n (r c)", p=P))\
                        .then_inc(con_loaded, 16)
            act.wait_ge(spread, 5)
            for i, m in enumerate((w.Wr, w.Wo, w.Wv)):
                act.dma_start(square[:, i], m.rearrange("(t p) n -> p t n", p=P)).then_inc(square_loaded, 16)
            for n in range(LOW - 1, -1, -1):
                act.dma_start(down_w[:, n], w.down_weights[n].rearrange("k r c -> (k r c)").partition_broadcast(P))\
                    .then_inc(down_loaded[n], 16)

            act.wait_ge(con_loaded, 7 * 16)
            for m, stage in enumerate(range(STAGES - 1, LOW - 1, -1)):
                if m:
                    act.wait_ge(high_done, m * PAIRS * 2)
                for n in range(PAIRS):
                    a, _ = pair(stage, n)
                    for r in range(2):
                        act.activation(scaled[:, 2 * n + r, 0:D], down_x[m % 2][:, a, 0:D], ACT.Copy,
                                       scale=high_w[:, 1, stage - LOW, n, r:r + 1]).then_inc(high_scaled, 1)
            for t in range(2):
                act.wait_ge(turned, t + 1)
                act.activation(exp_cols[:, 4 * t:4 * t + 4, 0:D],
                               bank[:, 2 * t:2 * t + 2, :].rearrange("p b (t n) -> p (b t) n", n=D),
                               ACT.Copy).then_inc(exp_copied, 1)
            for i, dst in enumerate((k.w_r, wo_t)):
                act.wait_ge(turned, 3)
                act.activation(dst[:], bank[:, 4 + i].rearrange("p (a n) -> p a n", a=CT), ACT.Copy)\
                    .then_inc(square_copied, 1)
            act.wait_ge(composed, 1)
            act.activation(k.w_vo[:], bank[:, 6].rearrange("p (a n) -> p a n", a=CT), ACT.Copy).then_inc(vo_copied, 1)
            act.wait_ge(small_loaded, 5 * 16)
            act.activation(k.channel[:, 3, :], k.channel[:, 0, :], ACT.Exp).then_inc(k.setup_done, 1)
            act.wait_ge(k.setup_done, 1)
            act.activation(k.channel[:, 4, :], k.channel[:, 3, :], ACT.Exp, scale=-1.0).then_inc(k.setup_done, 1)
            for t in range(HT):
                act.wait_ge(applied, t + 1)
                act.activation(up_x[0][:, t], bank[:, t, 0:D + 1], ACT.Copy).then_inc(up_copied, 1)
            for m, stage in enumerate(range(LOW, STAGES)):
                act.wait_ge(up_copied, HT)
                if m:
                    act.wait_ge(high_done, HIGH_OPS + m * PAIRS * 2)
                else:
                    act.wait_ge(high_done, HIGH_OPS)
                for n in range(PAIRS):
                    a, _ = pair(stage, n)
                    for r in range(2):
                        act.activation(scaled[:, 2 * n + r], up_x[m % 2][:, a], ACT.Copy,
                                       scale=high_w[:, 0, stage - LOW, n, 2 * r:2 * r + 1]).then_inc(high_scaled, 1)
            for t in range(4):
                act.wait_ge(down_applied, t + 1)
                act.activation(down_matrix[:, 2 * t:2 * t + 2], bank[:, t].rearrange("p (t n) -> p t n", n=D),
                               ACT.Copy).then_inc(down_copied, 1)
            for c in range(CT):
                act.wait_ge(up_turned, c + 1)
                act.activation(up_matrix[:, c], bank[:, 4 + 2 * c:6 + 2 * c].rearrange("p b n -> p (b n)"),
                               ACT.Copy).then_inc(matrix_copied, 1)
            act.wait_ge(matrix_copied, CT)
            act.wait_ge(down_copied, 4)

        @block.tensor
        def _(pe):
            pe.wait_ge(ident_step, 2)
            pe.wait_ge(exp_loaded, 2 * 16)
            for t in range(HT):
                for c in range(CT):
                    ins = pe.transpose(bank[:, t // 2, (t % 2) * D + c * P:(t % 2) * D + (c + 1) * P],
                                       exp_rows[:, c, t * P:(t + 1) * P], k.ident[:])
                if t % 4 == 3:
                    ins.then_inc(turned, 1)
            pe.wait_ge(square_loaded, 3 * 16)
            for i in range(2):
                for a in range(CT):
                    for b in range(CT):
                        ins = pe.transpose(bank[:, 4 + i, b * D + a * P:b * D + (a + 1) * P],
                                           square[:, i, a, b * P:(b + 1) * P], k.ident[:])
            ins.then_inc(turned, 1)
            pe.wait_ge(square_copied, 2)
            for h in range(CT):
                for m in range(CT):
                    ins = pe.matmul(bank[:, 6, h * D:(h + 1) * D], square[:, 2, m, h * P:(h + 1) * P],
                                    wo_t[:, m, :], start=(m == 0), stop=(m == CT - 1))
            ins.then_inc(composed, 1)
            pe.wait_ge(low_stage, LOW)
            pe.wait_ge(exp_copied, 2)
            pe.wait_ge(vo_copied, 1)
            for t in range(HT):
                pe.matmul(bank[:, t, 0:D + 1], low_up[:, t * P:(t + 1) * P], exp_cols[:, t], start=True, stop=True)\
                    .then_inc(applied, 1)
            pe.wait_ge(low_stage, 2 * LOW)
            pe.wait_ge(high_done, HIGH_OPS)
            pe.wait_ge(up_copied, HT)
            for t in range(HT):
                ins = pe.matmul(bank[:, t // 2, (t % 2) * D:(t % 2 + 1) * D], low_down[:, t * P:(t + 1) * P],
                                down_x[HIGH % 2][:, t, 0:D], start=True, stop=True)
                if t % 2:
                    ins.then_inc(down_applied, 1)
            pe.wait_ge(high_done, 2 * HIGH_OPS)
            for c in range(CT):
                for t in range(HT):
                    ins = pe.transpose(bank[:, 4 + 2 * c + t // 4, (t % 4) * P:(t % 4 + 1) * P],
                                       up_x[HIGH % 2][:, t, c * P:(c + 1) * P], k.ident[:])
                ins.then_inc(up_turned, 1)


def project_phase(nc, k, w):
    with ExitStack() as ctx:
        sb = lambda n, s, d=F32: ctx.enter_context(nc.sbuf_tensor(n, s, d))
        sem = lambda n: ctx.enter_context(nc.semaphore(n))
        w_raw = sb("w_raw", [P, CT, 3 * D])
        w_half = [sb(f"w_half{i}", [P, CT, 3 * D], F32R) for i in range(2)]
        w_loaded = sem("a_w_loaded")
        x_in = sb("a_x", [P, 2, TT, D])
        stats = sb("a_stats", [P, 2, TT, 6])
        mean_var = sb("a_mean_var", [P, 2, TT, 2])
        var_eps = sb("a_var_eps", [P, 2, TT])
        rstd = sb("a_rstd", [P, 2, TT])
        xn = sb("a_xn", [P, 2, TT, D])
        xt = [sb(f"a_xt{i}", [P, 2, CT, BLK], F32R) for i in range(2)]
        part = sb("a_parts", [P, 2, 3, 2 * CT, BLK], BF16)
        rest = sb("a_rest", [P, 2, 2 * CT, BLK])
        p_turn = ctx.enter_context(nc.psum_tensor("a_turn", [P, CT, BLK], F32))
        p_qk = ctx.enter_context(nc.psum_tensor("a_qk", [P, 2 * CT, BLK], F32))
        p_v = ctx.enter_context(nc.psum_tensor("a_v", [P, TT, D], F32))
        x_loaded = [sem(f"a_x_loaded{i}") for i in range(2)]
        stat_step = sem("a_stat_step")
        stats_done = sem("a_stats_done")
        eps_added = sem("a_eps_added")
        rstd_done = sem("a_rstd_done")
        xn_done = sem("a_xn_done")
        turned = sem("a_turned")
        xt_done = sem("a_xt_done")
        xt_low = sem("a_xt_low")
        w_high = sem("a_w_high")
        w_low = sem("a_w_low")
        qk_done = sem("a_qk_done")
        v_done = sem("a_v_done")
        part1 = sem("a_part1")
        rest_done = sem("a_rest_done")
        part2 = sem("a_part2")
        part3 = sem("a_part3")
        v_copied = sem("a_v_copied")
        stored = [sem(f"a_stored{i}") for i in range(2)]
        block = ctx.enter_context(nc.Block())
        x_tiles = w.x.rearrange("b (n j p) c -> (b n) p j c", n=BPS, p=P)

        def sequences(eng, body):
            for j in range(BPS):
                body(0, j)
            with eng.Fori(1, BATCH - 1) as b:
                for j in range(BPS):
                    body(b, j)
            for j in range(BPS):
                body(BATCH - 1, j)

        def is_last(b, j):
            return isinstance(b, int) and (b, j) == (BATCH - 1, BPS - 1)

        @block.sync
        def _(sp):
            for i, m in enumerate((w.W_q, w.W_k, w.W_v)):
                sp.dma_start(w_raw[:, :, i * D:(i + 1) * D], m.rearrange("(t p) n -> p t n", p=P))\
                    .then_inc(w_loaded, 16)

            def store(b, j):
                t = b * BPS + j
                z = j % 2
                wait(sp, part1, 4 * t + 4)
                apart(sp)
                wait(sp, part2, 4 * t + 4)
                apart(sp)
                wait(sp, part3, 4 * t + 4)
                apart(sp)
                for m in range(2 * CT):
                    dst = k.q_parts if m < CT else k.k_parts
                    sp.dma_start(dst[b * CT + m % CT, :, :, j * BLK:(j + 1) * BLK].rearrange("i r s -> r i s"),
                                 part[:, z, :, m, :]).then_inc(stored[z], 16)

            def load(b, j):
                t = b * BPS + j
                wait(sp, xn_done, TT * (t - 1))
                apart(sp)
                sp.dma_start(x_in[:, j % 2], x_tiles[t]).then_inc(x_loaded[j % 2], 16)

            load(0, 0)
            load(0, 1)

            def body(b, j):
                if not (isinstance(b, int) and b == BATCH - 1 and j >= BPS - 2):
                    load(b, j + 2) if j + 2 < BPS else load(b + 1, j + 2 - BPS)
                if not (isinstance(b, int) and (b, j) == (0, 0)):
                    if j:
                        store(b, j - 1)
                    else:
                        store(b - 1, BPS - 1)
            sequences(sp, body)
            store(BATCH - 1, BPS - 1)
            for z in range(2):
                sp.wait_ge(stored[z], 16 * 2 * CT * NBLK // 2)

        @block.gpsimd
        def _(pool):
            def inverse_std(b, j):
                t = b * BPS + j
                z = j % 2
                wait(pool, stats_done, TT * (t + 1))
                apart(pool)
                pool.tensor_scalar(var_eps[:, z], mean_var[:, z, :, 1], EPS, None, ALU.add).then_inc(eps_added, 1)
                wait(pool, eps_added, t + 1)
                pool.tensor_tensor(rstd[:, z], var_eps[:, z], k.minus_half[:], ALU.pow).then_inc(rstd_done, 1)

            def split(b, j):
                t = b * BPS + j
                z = j % 2
                for m in range(2 * CT):
                    wait(pool, part2, 4 * t + m + 1)
                    pool.tensor_tensor(part[:, z, 2, m], rest[:, z, m], part[:, z, 1, m], ALU.subtract)\
                        .then_inc(part3, 1)
            inverse_std(0, 0)
            inverse_std(0, 1)

            def body(b, j):
                if not (isinstance(b, int) and b == BATCH - 1 and j >= BPS - 2):
                    inverse_std(b, j + 2) if j + 2 < BPS else inverse_std(b + 1, j + 2 - BPS)
                split(b, j)
            sequences(pool, body)

        @block.vector
        def _(dve):
            def statistics(b, j):
                t = b * BPS + j
                z = j % 2
                wait(dve, x_loaded[z], 16 * (b * (BPS // 2) + j // 2 + 1))
                for a in range(TT):
                    dve.bn_stats(stats[:, z, a], x_in[:, z, a]).then_inc(stat_step, 1)
                wait(dve, stat_step, TT * (t + 1))
                wait(dve, rstd_done, t - 1)
                apart(dve)
                for a in range(TT):
                    dve.bn_aggr(mean_var[:, z, a], stats[:, z, a]).then_inc(stats_done, 1)

            def norm(b, j):
                t = b * BPS + j
                z = j % 2
                wait(dve, stats_done, TT * (t + 1))
                wait(dve, rstd_done, t + 1)
                wait(dve, turned, t - 1)
                for a in range(TT):
                    dve.tensor_scalar(xn[:, z, a], x_in[:, z, a], mean_var[:, z, a, 0:1], rstd[:, z, a:a + 1],
                                      ALU.subtract, ALU.mult).then_inc(xn_done, 1)

            def first_rest(b, j):
                t = b * BPS + j
                z = j % 2
                for m in range(2 * CT):
                    wait(dve, part1, 4 * t + m + 1)
                    wait(dve, part3, 4 * (t - 2) + m + 1) if not (isinstance(t, int) and t < 2) else None
                    dve.tensor_tensor(rest[:, z, m], p_qk[:, m], part[:, z, 0, m], ALU.subtract)\
                        .then_inc(rest_done, 1)

            def second_part(b, j):
                t = b * BPS + j
                z = j % 2
                for m in range(2 * CT):
                    wait(dve, rest_done, 4 * t + m + 1)
                    if m == 0 and not (isinstance(t, int) and t < 2):
                        wait(dve, stored[z], 16 * 2 * CT * (b * (BPS // 2) + j // 2))
                    dve.tensor_copy(part[:, z, 1, m], rest[:, z, m]).then_inc(part2, 1)
            def low_half_of_turned(b, j):
                t = b * BPS + j
                for c in range(CT):
                    wait(dve, xt_done, CT * t + c + 1)
                    dve.tensor_tensor(xt[1][:, j % 2, c], p_turn[:, c], xt[0][:, j % 2, c], ALU.subtract)\
                        .then_inc(xt_low, 1)

            for j in range(2):
                statistics(0, j)
                norm(0, j)
            for c in range(CT):
                dve.wait_ge(w_high, c + 1)
                dve.tensor_tensor(w_half[1][:, c], w_raw[:, c], w_half[0][:, c], ALU.subtract).then_inc(w_low, 1)
            low_half_of_turned(0, 0)

            def body(b, j):
                if not is_last(b, j):
                    low_half_of_turned(b, j + 1) if j + 1 < BPS else low_half_of_turned(b + 1, 0)
                ahead = (b, j + 2) if j + 2 < BPS else (b + 1, j + 2 - BPS)
                if isinstance(b, int) and b == BATCH - 1 and j >= BPS - 2:
                    ahead = None
                if ahead:
                    statistics(*ahead)
                first_rest(b, j)
                if ahead:
                    norm(*ahead)
                second_part(b, j)
            sequences(dve, body)

        @block.scalar
        def _(act):
            def turn(b, j):
                t = b * BPS + j
                z = j % 2
                wait(act, turned, t + 1)
                wait(act, v_done, t - 1)
                for c in range(CT):
                    act.activation(xt[0][:, z, c], p_turn[:, c], ACT.Copy).then_inc(xt_done, 1)

            def body(b, j):
                t = b * BPS + j
                z = j % 2
                if not is_last(b, j):
                    turn(b, j + 1) if j + 1 < BPS else turn(b + 1, 0)
                for m in range(2 * CT):
                    wait(act, qk_done, 4 * t + m + 1)
                    if m == 0 and not (isinstance(t, int) and t < 2):
                        wait(act, stored[z], 16 * 2 * CT * (b * (BPS // 2) + j // 2))
                    act.activation(part[:, z, 0, m], p_qk[:, m], ACT.Copy).then_inc(part1, 1)
                wait(act, v_done, t + 1)
                for g in range(HG):
                    act.activation(
                        k.v_all[:, b * HG + g, TT * j:TT * j + TT, :] if isinstance(b, int) else
                        k.v_all[:, bass.ds(b * HG + g, 1), TT * j:TT * j + TT, :].rearrange("p u t d -> p (u t) d"),
                        p_v[:, :, g * GH * HD:(g + 1) * GH * HD], ACT.Copy).then_inc(v_copied, 1)
            act.wait_ge(w_loaded, 3 * 16)
            for c in range(CT):
                act.activation(w_half[0][:, c], w_raw[:, c], ACT.Copy).then_inc(w_high, 1)
            turn(0, 0)
            sequences(act, body)

        @block.tensor
        def _(pe):
            def turn(b, j):
                t = b * BPS + j
                z = j % 2
                wait(pe, xn_done, TT * (t + 1))
                wait(pe, xt_low, CT * t)
                for c in range(CT):
                    for a in range(TT):
                        ins = pe.transpose(p_turn[:, c, a * P:(a + 1) * P], xn[:, z, a, c * P:(c + 1) * P],
                                           k.ident[:])
                ins.then_inc(turned, 1)

            def body(b, j):
                t = b * BPS + j
                z = j % 2
                if not is_last(b, j):
                    turn(b, j + 1) if j + 1 < BPS else turn(b + 1, 0)
                wait(pe, xt_low, CT * (t + 1))
                for m in range(2 * CT):
                    wait(pe, rest_done, 4 * (t - 1) + m + 1) if not (isinstance(t, int) and t < 1) else None
                    for c in range(CT):
                        for l, r in HALVES:
                            ins = pe.matmul(p_qk[:, m], w_half[l][:, c, m * P:(m + 1) * P], xt[r][:, z, c],
                                            start=(c == 0 and l + r == 0), stop=(c == CT - 1 and l == 1))
                    ins.then_inc(qk_done, 1)
                wait(pe, v_copied, HG * t)
                for a in range(TT):
                    for c in range(CT):
                        for l, r in HALVES:
                            ins = pe.matmul(p_v[:, a], xt[l][:, z, c, a * P:(a + 1) * P], w_half[r][:, c, 2 * D:],
                                            start=(c == 0 and l + r == 0), stop=(c == CT - 1 and l == 1))
                ins.then_inc(v_done, 1)
            turn(0, 0)
            pe.wait_ge(w_low, CT)
            sequences(pe, body)


def attention_phase(nc, k):
    with ExitStack() as ctx:
        sb = lambda n, s, d=F32: ctx.enter_context(nc.sbuf_tensor(n, s, d))
        ps = lambda n, s, d=F32: ctx.enter_context(nc.psum_tensor(n, s, d))
        sem = lambda n: ctx.enter_context(nc.semaphore(n))
        q_op = [sb(f"q_op{z}", [ROWS, GH, SEQ], BF16) for z in range(2)]
        k_op = [sb(f"k_op{z}", [ROWS, GH, SEQ], BF16) for z in range(2)]
        v_op = [sb(f"v_op{z}", [P, KB, GH, 2 * HD]) for z in range(2)]
        prob = sb("prob", [P, ST.PBUF, 2, BLK])
        causal = sb("causal", [P, 4 * P])
        part_max = sb("part_max", [P, GH, TT, GROUPS])
        neg_max = sb("neg_max", [P, GH, TT])
        neg_rest = sb("neg_rest", [P, GH, TT])
        shift_cols = sb("shift_cols", [P, P], BF16)
        shift = shift_cols[:, 0:3 * GH * TT].rearrange("p (h a n) -> p h a n", h=GH, a=3)
        shift_row = sb("shift_row", [3 * GH * TT, P], BF16)
        o_t = sb("o_t", [P, BLK])
        inv_sum = sb("inv_sum", [P, TT, GH])
        ctx_out = sb("ctx_out", [P, TT, GH, HD])
        p_s = [ps(f"p_score{i}", [P, 2, BLK]) for i in range(2)]
        p_r = ps("p_ring", [P, ST.RING, BLK])
        p_o = ps("p_out", [P, BLK])
        loaded = [sem(f"b_loaded{z}") for z in range(2)]
        ones_made = sem("b_ones_made")
        values_ready = sem("b_values_ready")
        score_ready = sem("b_score_ready")
        prob_ready = sem("b_prob_ready")
        prob_masked = sem("b_prob_masked")
        round_done = sem("b_round_done")
        bank_ready = sem("b_bank_ready")
        bank_read = sem("b_bank_read")
        max_ready = sem("b_max_ready")
        split_step = sem("b_split_step")
        shift_turned = sem("b_shift_turned")
        shift_copied = sem("b_shift_copied")
        shift_sent = [sem(f"b_shift_sent{i}") for i in range(2)]
        o_copied = sem("b_o_copied")
        ctx_turned = sem("b_ctx_turned")
        inv_ready = sem("b_inv_ready")
        ctx_ready = sem("b_ctx_ready")
        ctx_stored = sem("b_ctx_stored")
        block = ctx.enter_context(nc.Block())
        N, G = ST.n, GROUPS

        def units(eng, step):
            for s in range(-ST.LEAD, 0):
                step(0, 0, s, False, False)
            for z in range(2):
                for s in range(N):
                    step(z, z, s, z > 0, True)
            with eng.Fori(1, UNITS // 2 - 1) as i:
                for z in range(2):
                    for s in range(N):
                        step(2 * i + z, z, s, True, True)
            for z in range(2):
                for s in range(N):
                    step(UNITS - 2 + z, z, s, True, z == 0)
            for s in range(N, N + 14):
                step(UNITS - 1, 1, s, False, False)

        @block.sync
        def _(sp):
            def load(u, z):
                wait(sp, score_ready, N * (u - 1))
                apart(sp)
                wait(sp, bank_ready, 2 * N * (u - 1))
                apart(sp)
                for i in range(len(Q_PART)):
                    for dst, src, p in ((q_op, k.q_parts, Q_PART[i]), (k_op, k.k_parts, K_PART[i])):
                        sp.dma_start(dst[z][i * HD:(i + 1) * HD, :, :],
                                     src[u // 2, p, z * GH * HD:(z + 1) * GH * HD]
                                     .rearrange("(h r) s -> r h s", r=HD)).then_inc(loaded[z], 16)

            load(0, 0)

            def step(u, z, s, before, after):
                for v, rel in ST.due("load", s, u, False, after):
                    load(v, (z + rel) % 2)
                for v, rel, g in ST.due("shift_send", s, u, before, after):
                    y = (z + rel) % 2
                    wait(sp, shift_copied, G * v + g + 1)
                    apart(sp)
                    for h in range(GH):
                        sp.dma_start(q_op[y][PROD:ROWS, h, g * BLK:(g + 1) * BLK],
                                     shift_row[h * 3 * TT:(h + 1) * 3 * TT, :]).then_inc(shift_sent[g % 2], 16)
                for v, rel, g in ST.due("ctx_store", s, u, before, after):
                    wait(sp, ctx_ready, G * v + g + 1)
                    apart(sp)
                    sp.dma_start(k.ctx[v, g * BLK:(g + 1) * BLK, :].rearrange("(a p) c -> p a c", p=P),
                                 ctx_out[:].rearrange("p a h d -> p a (h d)")).then_inc(ctx_stored, 16)
            units(sp, step)
            sp.wait_ge(ctx_stored, 16 * G * UNITS)

        @block.gpsimd
        def _(pool):
            pool.memset(shift_cols[:], 0.0).then_inc(ones_made, 1)
            made = 1
            for z in range(2):
                for part in (k_op[z][PROD:ROWS], v_op[z][:, :, :, HD:2 * HD]):
                    pool.wait_ge(ones_made, made)
                    pool.memset(part, 1.0).then_inc(ones_made, 1)
                    made += 1
            pool.memset(causal[:], 0.0).then_inc(ones_made, 1)
            pool.wait_ge(ones_made, 6)
            pool.affine_select(out=causal[:, 3 * P:], in_=causal[:, 3 * P:], compare_op=ALU.is_ge, fill=NEG, base=0,
                               pattern=[[-1, P]], channel_multiplier=1).then_inc(ones_made, 1)

            def values(v, z):
                wait(pool, round_done, ST.rounds * (v - 1))
                apart(pool)
                src = k.v_all[:, v] if isinstance(v, int) else \
                    k.v_all[:, bass.ds(v, 1)].rearrange("p u t d -> p (u t) d")
                pool.tensor_copy(v_op[z][:, :, :, 0:HD], src.rearrange("p t (h d) -> p t h d", h=GH))\
                    .then_inc(values_ready, 1)
            pool.wait_ge(ones_made, 7)
            values(0, 0)

            def mask(i, at, n, stride):
                part = prob[:, i % ST.PBUF, :, :].rearrange("p b n -> p (b n)")
                if n > 1:
                    part = part[:, at:at + n * stride].rearrange("p (n w) -> p n w", n=n)[:, :, 0:P]
                    pattern = [[0, n], [1, P]]
                else:
                    part = part[:, at:at + P]
                    pattern = [[1, P]]
                return pool.affine_select(out=part, in_=part, compare_op=ALU.is_ge, fill=0.0, base=0,
                                          pattern=pattern, channel_multiplier=-1)

            def step(u, z, s, before, after):
                for v, rel in ST.due("values", s, u, False, after):
                    values(v, (z + rel) % 2)
                if 0 <= s < N and ST.tiles[s][0] != "full":
                    kind = ST.tiles[s][0]
                    i = s + N * z
                    wait(pool, prob_ready, N * u + s + 1)
                    apart(pool)
                    if kind == "diag":
                        mask(i, 0, 2, BLK)
                        mask(i, BLK + 3 * P, 1, 0).then_inc(prob_masked, 1)
                    else:
                        mask(i, 0, GH, 2 * P).then_inc(prob_masked, 1)
                for v, rel, g, _ in ST.due("shift_max", s, u, before, after):
                    c = (G * v + g) * 4
                    wait(pool, max_ready, G * v + g + 1)
                    wait(pool, shift_turned, G * v + g)
                    apart(pool)
                    pool.tensor_copy(shift[:, :, 0, :], neg_max[:]).then_inc(split_step, 1)
                    wait(pool, split_step, c + 1)
                    pool.tensor_tensor(neg_rest[:], neg_max[:], shift[:, :, 0, :], ALU.subtract).then_inc(split_step, 1)
                    wait(pool, split_step, c + 2)
                    apart(pool)
                    pool.tensor_copy(shift[:, :, 1, :], neg_rest[:]).then_inc(split_step, 1)
                    wait(pool, split_step, c + 3)
                    pool.tensor_tensor(shift[:, :, 2, :], neg_rest[:], shift[:, :, 1, :], ALU.subtract)\
                        .then_inc(split_step, 1)
            units(pool, step)

        @block.vector
        def _(dve):
            def bank_max(v, j, bank):
                g, pieces = ST.banks[j]
                wait(dve, bank_ready, 2 * N * v + j + 1)
                if not pieces[0][4]:
                    h, qb, key, n, _ = pieces[0]
                    dve.tensor_reduce(part_max[:, h, qb, key // BLK:key // BLK + 1], bank, AX.X, ALU.max)\
                        .then_inc(bank_read, 1)
                    return
                apart(dve)
                at = 0
                for h, qb, key, n, _ in pieces:
                    piece = bank[:, at:at + n]
                    ins = dve.tensor_tensor_reduce(piece, piece, causal[:, 4 * P - n:], 1.0, LOWEST, ALU.add,
                                                   ALU.max, part_max[:, h, qb, g:g + 1])
                    at += n
                ins.then_inc(bank_read, 1)

            def copy_shift(v, g, bank):
                wait(dve, shift_turned, G * v + g + 1)
                if not (isinstance(v, int) and (v, g) == (0, 0)):
                    y = (g - 1) % 2
                    wait(dve, shift_sent[y], 16 * GH * ((G // 2) * v + (g + 1 if y == 0 else g) // 2))
                dve.tensor_copy(shift_row[:], bank[0:3 * GH * TT, 0:P // 2].bitcast(BF16)).then_inc(shift_copied, 1)

            def normalise(v, g, bank):
                turned = bank.rearrange("p (a h e) -> p a h e", a=TT, h=GH)
                wait(dve, ctx_turned, G * v + g + 1)
                wait(dve, ctx_ready, G * v + g)
                dve.reciprocal(inv_sum[:], turned[:, :, :, HD]).then_inc(inv_ready, 1)
                wait(dve, inv_ready, G * v + g + 1)
                wait(dve, ctx_stored, 16 * (G * v + g))
                dve.tensor_tensor(ctx_out[:], turned[:, :, :, 0:HD],
                                  inv_sum[:].unsqueeze(3).broadcast_to([P, TT, GH, HD]), ALU.mult)\
                    .then_inc(ctx_ready, 1)

            def step(u, z, s, before, after):
                for v, _, kind, number, at in ST.ring_due(s, u):
                    bank = p_r[:, at % ST.RING]
                    {"bank": bank_max, "shift": copy_shift, "ctx": normalise}[kind](v, number, bank)
                for v, rel, g, nb in ST.due("shift_max", s, u, before, after):
                    wait(dve, bank_read, 2 * N * v + nb)
                    wait(dve, split_step, 4 * (G * v + g))
                    dve.tensor_reduce(neg_max[:], part_max[:, :, :, 0:g + 1], AX.X, ALU.max, negate=True)\
                        .then_inc(max_ready, 1)
                    wait(dve, max_ready, G * v + g + 1)
            dve.wait_ge(ones_made, 7)
            units(dve, step)

        @block.scalar
        def _(act):
            def step(u, z, s, before, after):
                if 0 <= s < N:
                    i = s + N * z
                    wait(act, score_ready, N * u + s + 1)
                    if not (isinstance(u, int) and u == 0 and s < ST.PBUF):
                        if s >= ST.PBUF:
                            wait(act, round_done, ST.rounds * u + ST.round_of_tile[s - ST.PBUF])
                        else:
                            wait(act, round_done, ST.rounds * (u - 1) + ST.round_of_tile[s - ST.PBUF + N])
                    act.activation(prob[:, i % ST.PBUF, :, :], p_s[s % 2][:], ACT.Exp, scale=SCALE)\
                        .then_inc(prob_ready, 1)
                for v, rel, g, rounds in ST.due("o_copy", s, u, before, after):
                    wait(act, round_done, ST.rounds * v + rounds)
                    wait(act, ctx_turned, G * v + g)
                    act.activation(o_t[:], p_o[:], ACT.Copy).then_inc(o_copied, 1)
            units(act, step)

        @block.tensor
        def _(pe):
            pe.wait_ge(ones_made, 5)

            def scores_for_max(v, y, j, bank):
                g, pieces = ST.banks[j]
                if j == 0:
                    wait(pe, loaded[y], 16 * 2 * len(Q_PART) * (v // 2 + 1))
                at = 0
                for h, qb, key, n, _ in pieces:
                    q0 = g * BLK + qb * P
                    out = bank[:, at:at + n]
                    last = pe.matmul(out, q_op[y][0:PROD, h, q0:q0 + P], k_op[y][0:PROD, h, key:key + n],
                                     start=True, stop=True)
                    at += n
                last.then_inc(bank_ready, 1)

            def scores(u, z, s):
                kind, g, h, kb = ST.tiles[s]
                if ST.first[g] == s:
                    y = g % 2
                    wait(pe, shift_sent[y], 16 * GH * ((G // 2) * u + g // 2 + 1))
                wait(pe, prob_ready, N * u + s - 1)
                out = p_s[s % 2]

                def product(o, h, kb, q0, n):
                    return pe.matmul(o, k_op[z][:, h, kb * P:(kb + 1) * P], q_op[z][:, h, q0:q0 + n],
                                     start=True, stop=True)
                q0 = g * BLK
                if kind == "full":
                    product(out[:, 0], h, kb, q0, BLK)
                    last = product(out[:, 1], h, kb + 1, q0, BLK)
                elif kind == "diag":
                    product(out[:, 0], h, kb, q0, BLK)
                    product(out[:, 1, 0:3 * P], h, kb + 1, q0 + P, 3 * P)
                    last = product(out[:, 1, 3 * P:], h, kb + 3, q0 + 3 * P, P)
                else:
                    for h in range(GH):
                        a = (h % 2) * 2 * P
                        last = product(out[:, h // 2, a:a + 2 * P], h, kb, q0 + 2 * P, 2 * P)
                last.then_inc(score_ready, 1)

            def values_product(v, y, g, kind, kb, half, first, rounds, masked):
                if kb == 0 and half == 0:
                    wait(pe, o_copied, G * v + g)
                    if g == 0:
                        wait(pe, values_ready, v + 1)

                def product(h, kb, q0, slot, bank, at, n, start, stop):
                    return pe.matmul(p_o[32 * h:32 * h + 2 * HD, q0:q0 + n], v_op[y][:, kb, h, :],
                                     prob[:, slot, bank, at:at + n], start=start, stop=stop,
                                     tile_position=(0, 32 * h), skip_group_check=True)
                slot = [(first + N * y + h) % ST.PBUF for h in range(GH)]
                if kind == "corner":
                    wait(pe, prob_masked, ST.masked * v + masked)
                    for h in range(GH):
                        last = product(h, kb, 2 * P, slot[0], h // 2, (h % 2) * 2 * P, 2 * P, False, True)
                    last.then_inc(round_done, 1)
                    return
                if half == 0:
                    if kind == "diag":
                        wait(pe, prob_masked, ST.masked * v + masked)
                    else:
                        wait(pe, prob_ready, N * v + first + GH)
                for h in range(GH):
                    if half == 0:
                        last = product(h, kb, 0, slot[h], 0, 0, BLK, kb == 0, False)
                    elif kind == "full":
                        last = product(h, kb + 1, 0, slot[h], 1, 0, BLK, False, False)
                    else:
                        last = product(h, kb + 1, P, slot[h], 1, 0, 3 * P, False, False)
                if half and kind == "diag":
                    for h in range(GH):
                        last = product(h, kb + 3, 3 * P, slot[h], 1, 3 * P, P, False, False)
                if half:
                    last.then_inc(round_done, 1)

            def turn_ctx(v, y, g, bank):
                wait(pe, o_copied, G * v + g + 1)
                for a in range(TT):
                    last = pe.transpose(bank[:, a * P:(a + 1) * P], o_t[:, a * P:(a + 1) * P], k.ident[:])
                last.then_inc(ctx_turned, 1)

            def turn_shift(v, y, g, bank):
                wait(pe, split_step, 4 * (G * v + g + 1))
                pe.transpose(bank[:, 0:P // 2].bitcast(BF16), shift_cols[:], k.ident_b[:]).then_inc(shift_turned, 1)

            def into_ring(v, rel, z, kind, number, at):
                earlier = ST.before(at, v)
                if earlier:
                    owner, was, n = earlier
                    if was == "bank":
                        wait(pe, bank_read, 2 * N * owner + n + 1)
                    else:
                        wait(pe, {"shift": shift_copied, "ctx": ctx_ready}[was], G * owner + n + 1)
                bank = p_r[:, at % ST.RING]
                {"bank": scores_for_max, "shift": turn_shift, "ctx": turn_ctx}[kind](v, (z + rel) % 2, number, bank)

            def step(u, z, s, before, after):
                if 0 <= s < N:
                    scores(u, z, s)
                entries = list(ST.ring_due(s, u))
                for v, rel, *entry in entries[:1]:
                    into_ring(v, rel, z, *entry)
                for v, rel, *what in ST.due("pv", s, u, before, after):
                    values_product(v, (z + rel) % 2, *what)
                for v, rel, *entry in entries[1:]:
                    into_ring(v, rel, z, *entry)
            units(pe, step)


def block_pass(nc, k, w, first):
    name = "d" if first else "e"
    norms = (1,) if first else (0, 1)
    RAW = 4
    with ExitStack() as ctx:
        sb = lambda n, s, d=F32: ctx.enter_context(nc.sbuf_tensor(f"{name}_{n}", s, d))
        ps = lambda n, s, d=F32: ctx.enter_context(nc.psum_tensor(f"{name}_{n}", s, d))
        sem = lambda n: ctx.enter_context(nc.semaphore(f"{name}_{n}"))
        x_in = sb("x_in", [P, 2 if first else 1, TT, D])
        side = sb("side", [P, 2, TT, D])
        a_t = sb("a_t", [P, CT, BLK], F32R if first else F32)
        if first:
            a_low = sb("a_low", [P, CT, BLK], F32R)
            wo_half = [sb(f"wo_half{i}", [P, CT, D], F32R) for i in range(2)]
        else:
            state = sb("state", [P, CT, 1 + BLK])
            diff = sb("diff", [P, CT, BLK])
            gate = diff[:].rearrange("p c n -> p (c n)").rearrange("p (a n) -> p a n", a=TT)
            v_in = sb("v_in", [P, CT, BLK])
            r_in = sb("r_in", [P, CT, BLK])
        x_mid = sb("x_mid", [P, 2, TT, D])
        x_bias = sb("x_bias", [P, 2, TT, D])
        xn = sb("xn", [P, TT, D])
        x_t = [sb(f"x_t{i}", [P, CT, BLK], F32R) for i in range(2)]
        hidden = [sb(f"hidden{i}", [P, HT, BLK], F32R) for i in range(2)]
        gelu = sb("gelu", [P, RAW, BLK])
        stats = sb("stats", [P, 2, TT, 6])
        mean_var = sb("mean_var", [P, 2, TT, 2])
        var_eps = sb("var_eps", [P, 2, TT])
        rstd = sb("rstd", [P, 2, TT])
        p_turn = ps("turn", [P, CT, BLK])
        p_h = ps("h", [P, 2, BLK])
        p_y = ps("y", [P, TT, D])
        p_w = ps("w", [P, TT, D])
        p_wide = p_w[:].rearrange("p a n -> p (a n)").rearrange("p (c n) -> p c n", c=CT)
        p_layer = p_w if first else p_turn[:].rearrange("p c n -> p (c n)").rearrange("p (a n) -> p a n", a=TT)
        turn_a = sem("turn_a")
        copied_a = sem("copied_a")
        turn_b = sem("turn_b")
        copied_b = sem("copied_b")
        h_ready = sem("h_ready")
        low_b = sem("low_b")
        gelu_done = sem("gelu_done")
        h_high = sem("h_high")
        h_low = sem("h_low")
        w_ready = sem("w_ready")
        w_read = sem("w_read")
        bias_done = sem("bias_done")
        y_ready = sem("y_ready")
        x_ready = sem("x_ready")
        stat_step = {i: sem(f"stat_step{i}") for i in norms}
        stats_done = {i: sem(f"stats_done{i}") for i in norms}
        eps_added = {i: sem(f"eps_added{i}") for i in norms}
        rstd_done = {i: sem(f"rstd_done{i}") for i in norms}
        xn_done = {i: sem(f"xn_done{i}") for i in norms}
        if first:
            biased = sem("biased")
            weights_loaded = [sem(f"weights_loaded{i}") for i in range(4)]
            weights_high = sem("weights_high")
            wo_high = sem("wo_high")
            wo_low = sem("wo_low")
            low_a = sem("low_a")
            weights_low = sem("weights_low")
            x_loaded = [sem(f"x_loaded{i}") for i in range(2)]
        else:
            r_ready = sem("r_ready")
            gate_done = sem("gate_done")
            mid_ready = sem("mid_ready")
            carried = sem("carried")
            summed = sem("summed")
            diffed = sem("diffed")
            mixed = sem("mixed")
            stored = [sem(f"stored{i}") for i in range(2)]
        block = ctx.enter_context(nc.Block())
        tiles = "b (n j p) c -> (b n) p j c"
        x_tiles = w.x.rearrange(tiles, n=BPS, p=P)
        out_tiles = w.out.rearrange(tiles, n=BPS, p=P)
        LAST = (BATCH - 1, BPS - 1)

        def sequences(eng, body):
            for j in range(BPS):
                body(0, j)
            with eng.Fori(1, BATCH - 1) as b:
                for j in range(BPS):
                    body(b, j)
            for j in range(BPS):
                body(BATCH - 1, j)

        def following(b, j):
            if isinstance(b, int) and (b, j) == LAST:
                return None
            return (b, j + 1) if j + 1 < BPS else (b + 1, 0)

        def resident(t):
            if isinstance(t, int):
                return k.x_all[:, t]
            return k.x_all[:, bass.ds(t, 1)].rearrange("p u a n -> p (u a) n")

        pieces = []
        for i in range(4):
            h = i % 2
            raw = k.x_all[:, NBLK // 2 + i].rearrange("p a n -> p (a n)")
            if i < 2:
                pieces.append((k.up_dram[:, h], raw, *[x[:, h] for x in k.up_half]))
            else:
                four = slice(h * HT // 2, (h + 1) * HT // 2)
                pieces.append((k.down_dram[:, four], raw.rearrange("p (t n) -> p t n", n=D),
                               *[x[:, four] for x in k.down_half]))

        @block.sync
        def _(sp):
            def load(b, j):
                t = b * BPS + j
                z = j % 2
                if (t if isinstance(t, int) else 0) == 1:
                    for i, (dram, raw, _, _) in enumerate(pieces):
                        sp.dma_start(raw, dram).then_inc(weights_loaded[i], 16)
                wait(sp, w_read, t - 1)
                apart(sp)
                sp.dma_start(x_in[:, z], x_tiles[t]).then_inc(x_loaded[z], 16)
                wait(sp, turn_a, t - 1)
                apart(sp)
                for g in range(HG):
                    sp.dma_start(side[:, z, :, g * GH * HD:(g + 1) * GH * HD],
                                 k.ctx[b * HG + g, j * BLK:(j + 1) * BLK, :].rearrange("(a p) c -> p a c", p=P))\
                        .then_inc(x_loaded[z], 16)

            def store(b, j):
                t = b * BPS + j
                z = j % 2
                wait(sp, x_ready, t + 1)
                apart(sp)
                sp.dma_start(out_tiles[t], side[:, z]).then_inc(stored[z], 16)

            if first:
                sequences(sp, load)
            else:
                sequences(sp, store)
                for z in range(2):
                    sp.wait_ge(stored[z], 16 * NBLK // 2)

        @block.gpsimd
        def _(pool):
            def inverse_std(i, t):
                wait(pool, stats_done[i], TT * (t + 1))
                apart(pool)
                pool.tensor_scalar(var_eps[:, i], mean_var[:, i, :, 1], EPS, None, ALU.add).then_inc(eps_added[i], 1)
                wait(pool, eps_added[i], t + 1)
                pool.tensor_tensor(rstd[:, i], var_eps[:, i], k.minus_half[:], ALU.pow).then_inc(rstd_done[i], 1)

            def body(b, j):
                t = b * BPS + j
                z = j % 2
                after = following(b, j)
                if first:
                    wait(pool, x_loaded[z], 16 * (1 + HG) * (b * (BPS // 2) + j // 2 + 1))
                    for a in range(TT):
                        ins = pool.tensor_tensor(x_in[:, z, a], x_in[:, z, a], k.row_bias[:, 0], ALU.add)
                    ins.then_inc(biased, 1)
                elif after:
                    inverse_std(0, t + 1)
                inverse_std(1, t)
                wait(pool, x_ready, t - 1)
                for a in range(TT):
                    ins = pool.tensor_tensor(x_bias[:, z, a], x_mid[:, z, a], k.row_bias[:, 1], ALU.add)
                ins.then_inc(bias_done, 1)
            if not first:
                inverse_std(0, 0)
            sequences(pool, body)

        @block.vector
        def _(dve):
            def statistics(i, x, t):
                for a in range(TT):
                    dve.bn_stats(stats[:, i, a], x[:, a]).then_inc(stat_step[i], 1)
                wait(dve, stat_step[i], TT * (t + 1))
                wait(dve, rstd_done[i], t)
                apart(dve)
                for a in range(TT):
                    dve.bn_aggr(mean_var[:, i, a], stats[:, i, a]).then_inc(stats_done[i], 1)

            def norm(i, x, out, t, out_free, out_value):
                wait(dve, stats_done[i], TT * (t + 1))
                wait(dve, rstd_done[i], t + 1)
                wait(dve, out_free, out_value)
                for a in range(TT):
                    ins = dve.tensor_scalar(out[:, a], x[:, a], mean_var[:, i, a, 0:1], rstd[:, i, a:a + 1],
                                            ALU.subtract, ALU.mult)
                ins.then_inc(xn_done[i], 1)

            def decay_sum(b, j, step):
                t = b * BPS + j
                if step == 0:
                    wait(dve, copied_a, t + 1)
                    if j == 0:
                        dve.memset(state[:, :, 0:1], 0.0).then_inc(carried, 1)
                    else:
                        dve.tensor_copy(state[:, :, 0:1], state[:, :, BLK:BLK + 1]).then_inc(carried, 1)
                    wait(dve, carried, t + 1)
                    for c in range(CT):
                        dve.tensor_tensor_scan(state[:, c, 1:BLK + 1],
                                               k.channel[:, 4, c:c + 1].broadcast_to([P, BLK]), a_t[:, c],
                                               state[:, c, 0:1], ALU.mult, ALU.add).then_inc(summed, 1)
                elif step == 1:
                    wait(dve, summed, CT * (t + 1))
                    for c in range(CT):
                        dve.tensor_tensor(diff[:, c], a_t[:, c], state[:, c, 0:BLK], ALU.subtract)\
                            .then_inc(diffed, 1)
                else:
                    m, out = ((2, r_in), (1, v_in))[step - 2]
                    wait(dve, diffed, CT * (t + 1))
                    wait(dve, w_ready, t)
                    for c in range(CT):
                        ins = dve.scalar_tensor_tensor(out[:, c], diff[:, c], k.channel[:, m, c:c + 1],
                                                       state[:, c, 0:BLK], ALU.mult, ALU.add)
                    ins.then_inc(mixed, 1)

            def low_half_of_matrices():
                for i, (_, raw, high, low) in enumerate(pieces):
                    wait(dve, weights_high, i + 1)
                    dve.tensor_tensor(low, raw, high, ALU.subtract).then_inc(weights_low, 1)

            def low_half_of_context(b, j):
                t = b * BPS + j
                wait(dve, copied_a, t + 1)
                wait(dve, w_ready, t)
                for c in range(CT):
                    ins = dve.tensor_tensor(a_low[:, c], p_wide[:, c], a_t[:, c], ALU.subtract)
                ins.then_inc(low_a, 1)

            def low_half_of_turned(b, j):
                t = b * BPS + j
                for c in range(CT):
                    wait(dve, copied_b, CT * t + c + 1)
                    dve.tensor_tensor(x_t[1][:, c], p_turn[:, c], x_t[0][:, c], ALU.subtract).then_inc(low_b, 1)

            def low_half_of_hidden(b, j, m):
                t = b * BPS + j
                wait(dve, h_high, HT * t + m + 1)
                dve.tensor_tensor(hidden[1][:, m], gelu[:, m % RAW], hidden[0][:, m], ALU.subtract)\
                    .then_inc(h_low, 1)

            def front(b, j):
                t = b * BPS + j
                z = j % 2
                wait(dve, w_ready, t + 1)
                wait(dve, bias_done, t - 1)
                if first:
                    wait(dve, biased, t + 1)
                    for a in range(2):
                        ins = dve.tensor_tensor(x_mid[:, z, 2 * a:2 * a + 2], p_w[:, 2 * a:2 * a + 2],
                                                x_in[:, z, 2 * a:2 * a + 2], ALU.add)
                    ins.then_inc(w_read, 1)
                else:
                    wait(dve, gate_done, t + 1)
                    for a in range(2):
                        ins = dve.tensor_tensor(gate[:, 2 * a:2 * a + 2], p_layer[:, 2 * a:2 * a + 2],
                                                gate[:, 2 * a:2 * a + 2], ALU.mult)
                    ins.then_inc(w_read, 1)
                    wait(dve, w_read, t + 1)
                    ins = dve.tensor_tensor(x_mid[:, z], gate, resident(t), ALU.add)
                ins.then_inc(mid_ready, 1) if not first else None
                if first:
                    wait(dve, w_read, t + 1)
                else:
                    wait(dve, mid_ready, t + 1)
                statistics(1, x_mid[:, z], t)
                norm(1, x_mid[:, z], xn, t, turn_b, t)

            def statistics_front(b, j):
                if not first:
                    t = b * BPS + j
                    statistics(0, resident(t), t)

            def norm_front(b, j):
                if not first:
                    t = b * BPS + j
                    norm(0, resident(t), x_in[:, 0], t, turn_a, t)

            def back(b, j):
                t = b * BPS + j
                z = j % 2
                wait(dve, y_ready, t + 1)
                wait(dve, bias_done, t + 1)
                if not first and not (isinstance(t, int) and t < 2):
                    wait(dve, stored[z], 16 * (b * (BPS // 2) + j // 2))
                out = resident(t) if first else side[:, z]
                for a in range(2):
                    ins = dve.tensor_tensor(out[:, 2 * a:2 * a + 2], p_y[:, 2 * a:2 * a + 2],
                                            x_bias[:, z, 2 * a:2 * a + 2], ALU.add)
                ins.then_inc(x_ready, 1)

            for j in range(2):
                statistics_front(0, j)
                norm_front(0, j)
            if not first:
                for step in range(4):
                    decay_sum(0, 0, step)
            else:
                dve.wait_ge(wo_high, 1)
                dve.tensor_tensor(wo_half[1][:], k.w_o[:], wo_half[0][:], ALU.subtract).then_inc(wo_low, 1)
                low_half_of_context(0, 0)
            front(0, 0)
            if first:
                low_half_of_matrices()
            low_half_of_turned(0, 0)

            def body(b, j):
                after = following(b, j)
                later = after and following(*after)
                for m in range(HT):
                    if after and not first and m < 4:
                        decay_sum(*after, m)
                    low_half_of_hidden(b, j, m)
                    if after and first and m == 2:
                        low_half_of_context(*after)
                    if later and m == 4:
                        statistics_front(*later)
                if later:
                    norm_front(*later)
                if after:
                    front(*after)
                    low_half_of_turned(*after)
                back(b, j)
            sequences(dve, body)

        @block.scalar
        def _(act):
            def copy_a(b, j):
                t = b * BPS + j
                wait(act, turn_a, t + 1)
                if first:
                    wait(act, w_ready, t)
                else:
                    wait(act, diffed, CT * t)
                for c in range(CT):
                    ins = act.activation(a_t[:, c], p_wide[:, c], ACT.Copy)
                ins.then_inc(copied_a, 1)

            def copy_b(b, j):
                t = b * BPS + j
                wait(act, turn_b, t + 1)
                wait(act, h_ready, HT * t)
                for c in range(CT):
                    act.activation(x_t[0][:, c], p_turn[:, c], ACT.Copy).then_inc(copied_b, 1)

            def gate_of(b, j):
                if not first:
                    t = b * BPS + j
                    wait(act, r_ready, t + 1)
                    wait(act, mixed, 2 * t + 2)
                    wait(act, w_read, t)
                    for a in range(2):
                        ins = act.activation(gate[:, 2 * a:2 * a + 2], p_w[:, 2 * a:2 * a + 2], ACT.Sigmoid)
                    ins.then_inc(gate_done, 1)

            def gelus(b, j, lo, hi):
                t = b * BPS + j
                for m in range(lo, hi + (hi == HT)):
                    if m < HT:
                        wait(act, h_ready, HT * t + m + 1)
                        wait(act, h_low, HT * t + m + 1 - RAW)
                        act.activation(gelu[:, m % RAW], p_h[:, m % 2], ACT.Gelu,
                                       bias=k.hidden_bias[:, m:m + 1]).then_inc(gelu_done, 1)
                    if m > 0:
                        wait(act, gelu_done, HT * t + m)
                        act.activation(hidden[0][:, m - 1], gelu[:, (m - 1) % RAW], ACT.Copy).then_inc(h_high, 1)

            def high_half_of_matrices():
                for i, (_, raw, high, _) in enumerate(pieces):
                    wait(act, weights_loaded[i], 16)
                    act.activation(high, raw, ACT.Copy).then_inc(weights_high, 1)

            if first:
                act.activation(wo_half[0][:], k.w_o[:], ACT.Copy).then_inc(wo_high, 1)
            copy_a(0, 0)
            gate_of(0, 0)
            if first:
                high_half_of_matrices()
            copy_b(0, 0)

            def body(b, j):
                after = following(b, j)
                if after:
                    copy_a(*after)
                gelus(b, j, 0, HT)
                if after:
                    gate_of(*after)
                    copy_b(*after)
            sequences(act, body)

        @block.tensor
        def _(pe):
            def turns_a(b, j):
                t = b * BPS + j
                z = j % 2
                if first:
                    wait(pe, x_loaded[z], 16 * (1 + HG) * (b * (BPS // 2) + j // 2 + 1))
                else:
                    wait(pe, xn_done[0], t + 1)
                wait(pe, w_read, t)
                source = side if first else x_in
                for c in range(CT):
                    for a in range(TT):
                        ins = pe.transpose(p_wide[:, c, a * P:(a + 1) * P], source[:, z if first else 0, a, c * P:(c + 1) * P],
                                           k.ident[:])
                ins.then_inc(turn_a, 1)

            def turns_b(b, j):
                t = b * BPS + j
                wait(pe, xn_done[1], t + 1)
                wait(pe, low_b, CT * t)
                for c in range(CT):
                    for a in range(TT):
                        ins = pe.transpose(p_turn[:, c, a * P:(a + 1) * P], xn[:, a, c * P:(c + 1) * P], k.ident[:])
                ins.then_inc(turn_b, 1)

            def rows_product(out, left, right):
                for a in range(TT):
                    for c in range(CT):
                        ins = pe.matmul(out[:, a], left[:, c, a * P:(a + 1) * P], right[:, c],
                                        start=(c == 0), stop=(c == CT - 1))
                return ins

            def gate_product(b, j):
                if not first:
                    t = b * BPS + j
                    wait(pe, copied_a, t + 1)
                    wait(pe, mixed, 2 * t + 1)
                    rows_product(p_w, r_in, k.w_r).then_inc(r_ready, 1)

            def layer_product(b, j):
                t = b * BPS + j
                if first:
                    wait(pe, low_a, t + 1)
                    if isinstance(t, int) and t == 0:
                        wait(pe, wo_low, 1)
                    for a in range(TT):
                        for c in range(CT):
                            for l, r in HALVES:
                                ins = pe.matmul(p_w[:, a], (a_t, a_low)[l][:, c, a * P:(a + 1) * P],
                                                wo_half[r][:, c], start=(c == 0 and l + r == 0),
                                                stop=(c == CT - 1 and l == 1))
                    ins.then_inc(w_ready, 1)
                else:
                    wait(pe, low_b, CT * t)
                    wait(pe, mixed, 2 * t + 2)
                    rows_product(p_layer, v_in, k.w_vo).then_inc(w_ready, 1)

            def up(b, j):
                t = b * BPS + j
                wait(pe, low_b, CT * (t + 1))
                if first and isinstance(t, int) and t == 0:
                    wait(pe, weights_low, 4)
                for m in range(HT):
                    wait(pe, gelu_done, HT * t + m - 1)
                    for c in range(CT):
                        for l, r in HALVES:
                            ins = pe.matmul(p_h[:, m % 2], k.up_half[l][:, c, m * P:(m + 1) * P], x_t[r][:, c],
                                            start=(c == 0 and l + r == 0), stop=(c == CT - 1 and l == 1))
                    ins.then_inc(h_ready, 1)

            def down(b, j, lo, hi):
                t = b * BPS + j
                if lo == 0:
                    wait(pe, h_low, HT * (t + 1))
                    wait(pe, x_ready, t)
                for a in range(lo, hi):
                    for m in range(HT):
                        for l, r in HALVES:
                            ins = pe.matmul(p_y[:, a], hidden[l][:, m, a * P:(a + 1) * P], k.down_half[r][:, m],
                                            start=(m == 0 and l + r == 0), stop=(m == HT - 1 and l == 1))
                if hi == TT:
                    ins.then_inc(y_ready, 1)

            turns_a(0, 0)
            gate_product(0, 0)
            layer_product(0, 0)
            turns_b(0, 0)

            def body(b, j):
                after = following(b, j)
                if after:
                    turns_a(*after)
                up(b, j)
                if after:
                    gate_product(*after)
                    layer_product(*after)
                    down(b, j, 0, TT - 1)
                    turns_b(*after)
                    down(b, j, TT - 1, TT)
                else:
                    down(b, j, 0, TT)
            sequences(pe, body)


def hybrid_block(nc, w):
    k = Shared()
    k.q_parts = nc.dram_tensor("q_parts", (UNITS // 2, 3, P, SEQ), BF16, kind="Internal").ap()
    k.k_parts = nc.dram_tensor("k_parts", (UNITS // 2, 3, P, SEQ), BF16, kind="Internal").ap()
    k.ctx = nc.dram_tensor("ctx", (UNITS, SEQ, GH * HD), F32, kind="Internal").ap()
    k.up_dram = nc.dram_tensor("up_matrix_dram", (P, CT, HID), F32, kind="Internal").ap()
    k.down_dram = nc.dram_tensor("down_matrix_dram", (P, HT, D), F32, kind="Internal").ap()
    with ExitStack() as ctx:
        sb = lambda n, s, d=F32: ctx.enter_context(nc.sbuf_tensor(n, s, d))
        k.ident = sb("ident", [P, P])
        k.ident_b = sb("ident_b", [P, P], BF16)
        k.minus_half = sb("minus_half", [P, TT])
        k.row_bias = sb("row_bias", [P, 2, D])
        k.hidden_bias = sb("hidden_bias", [P, HT])
        k.channel = sb("channel", [P, 5, CT])
        k.w_o = sb("w_o", [P, CT, D])
        k.w_r = sb("w_r", [P, CT, D])
        k.w_vo = sb("w_vo", [P, CT, D])
        k.setup_done = ctx.enter_context(nc.semaphore("setup_done"))
        consts_phase(nc, k, w)
        with nc.sbuf_tensor("v_all", [P, UNITS, KB, GH * HD], F32) as v_all:
            k.v_all = v_all
            project_phase(nc, k, w)
            attention_phase(nc, k)
        with ExitStack() as late:
            k.x_all = late.enter_context(nc.sbuf_tensor("x_all", [P, NBLK, TT, D], F32))
            k.up_half = [late.enter_context(nc.sbuf_tensor(f"up_half{i}", [P, CT, HID], F32R)) for i in range(2)]
            k.down_half = [late.enter_context(nc.sbuf_tensor(f"down_half{i}", [P, HT, D], F32R)) for i in range(2)]
            block_pass(nc, k, w, True)
            block_pass(nc, k, w, False)


_INS = {"L0_attn_a_x": "x", "L0_attn_a_W_q": "W_q", "L0_attn_a_W_k": "W_k", "L0_attn_a_W_v": "W_v",
        "L0_attn_a_W_o": "W_o", "L0_attn_a_b_o": "b_o", "L0_attn_b_time_decay": "time_decay",
        "L0_attn_b_time_mix_k": "time_mix_k", "L0_attn_b_time_mix_v": "time_mix_v",
        "L0_attn_b_time_mix_r": "time_mix_r", "L0_attn_b_Wk": "Wk", "L0_attn_b_Wv": "Wv",
        "L0_attn_b_Wr": "Wr", "L0_attn_b_Wo": "Wo", "L0_ffn_W_exp": "W_exp", "L0_ffn_b_exp": "b_exp",
        "L0_ffn_up_weights": "up_weights", "L0_ffn_up_bias": "up_bias",
        "L0_ffn_down_weights": "down_weights", "L0_ffn_W_con": "W_con", "L0_ffn_b_con": "b_con",
        "L0_ffn_down_bias": "down_bias"}


def kernel(**inputs):
    from types import SimpleNamespace

    import numpy as _np
    import concourse.bacc as _bacc
    from concourse import mybir as _mybir
    from concourse.bass_utils import run_bass_kernel_spmd as _run

    nc = _bacc.Bacc("TRN2", target_bir_lowering=False, num_devices=1)
    arrays, args = {}, {}
    for name, short in _INS.items():
        a = _np.ascontiguousarray(inputs[name])
        arrays[f"in_{name}"] = a
        args[short] = nc.dram_tensor(f"in_{name}", a.shape, _mybir.dt.from_np(a.dtype), kind="ExternalInput").ap()
    out = nc.dram_tensor("out_0", (BATCH, SEQ, D), _mybir.dt.float32, kind="ExternalOutput").ap()
    hybrid_block(nc, SimpleNamespace(out=out, **args))
    r = _run(nc, [arrays], core_ids=[0])
    return r.results[0]["out_0"]
```
